# Optimizing a Trainium2 kernel written in Bass

```python
import numpy as np
import jax
import jax.numpy as jnp

def _softmax(x, axis=-1):
    return jax.nn.softmax(x, axis=axis)

def _gelu(x):
    return jax.nn.gelu(x, approximate=True)

def _silu(x):
    return jax.nn.silu(x)

def _sigmoid(x):
    return jax.nn.sigmoid(x)

def _layernorm(x, axis=-1, eps=1e-05):
    m = jnp.mean(x, axis=axis, keepdims=True)
    v = jnp.var(x, axis=axis, keepdims=True)
    return (x - m) / jnp.sqrt(v + eps)

def _scatter_add(tgt, idx, src, axis=0):
    return tgt.at[idx].add(src)

def _segment_sum(src, seg, n):
    return jax.ops.segment_sum(src, seg, n)
kernel_name = 'mk_lm_tower_d2_tok_ids256_r4_881ea7'

def setup_inputs(seed: int=0):
    np.random.seed(seed)
    _w = jnp.asarray

    def _rec_inputs():
        import jax
        import jax.numpy as jnp
        _rk = jax.random.key(seed)
        x = jax.random.randint(jax.random.fold_in(_rk, 1), (16, 128), 0, 64, jnp.int32)
        return x
    x = _rec_inputs()

    def _L0_tok_setup():
        import jax, jax.numpy as jnp
        import numpy as np
        D_MODEL = 128
        N_LAYERS = 4
        VOCAB = 64
        SEQ = 512
        BATCH = 8
        EPS = 1e-05

        def _ln(x, g, b):
            mu = jnp.mean(x, axis=-1, keepdims=True)
            var = jnp.mean(jnp.square(x - mu), axis=-1, keepdims=True)
            return (x - mu) * jax.lax.rsqrt(var + EPS) * g + b

        def _fast_memory(x, mask, W_upd, b_upd, W_f, b_f, decay_param):
            decay = jax.nn.sigmoid(decay_param[0])
            u = jnp.einsum('bsd,de->bse', x, W_upd) + b_upd
            u_t = jnp.swapaxes(u, 0, 1)
            m_t = jnp.swapaxes(mask, 0, 1)[..., None]

            def step(mem, inp):
                u_i, msk = inp
                new = decay * mem + u_i
                mem = msk * new + (1.0 - msk) * mem
                return (mem, mem)
            mem0 = jnp.zeros((x.shape[0], x.shape[2]), x.dtype)
            _, mems = jax.lax.scan(step, mem0, (u_t, m_t))
            mems = jnp.swapaxes(mems, 0, 1)
            return jnp.einsum('bsd,de->bse', mems, W_f) + b_f
        key = jax.random.key(seed)
        ks = jax.random.split(key, 16)
        d, dff = (D_MODEL, 4 * D_MODEL)
        s = 0.02
        inp = {'tokens': jax.random.randint(ks[0], (BATCH, SEQ), 0, VOCAB, dtype=jnp.int64), 'emb': jax.random.normal(ks[1], (VOCAB, d), jnp.float32) * s, 'W_upd': jax.random.normal(ks[2], (d, d), jnp.float32) * s, 'b_upd': jnp.zeros((d,), jnp.float32), 'W_f': jax.random.normal(ks[3], (d, d), jnp.float32) * s, 'b_f': jnp.zeros((d,), jnp.float32), 'decay_param': jnp.zeros((1,), jnp.float32), 'norm_g': jnp.ones((d,), jnp.float32), 'norm_b': jnp.zeros((d,), jnp.float32), 'cms_ln_g': jnp.ones((N_LAYERS, d), jnp.float32), 'cms_ln_b': jnp.zeros((N_LAYERS, d), jnp.float32), 'cms_W1': jax.random.normal(ks[4], (N_LAYERS, d, dff), jnp.float32) * s, 'cms_b1': jnp.zeros((N_LAYERS, dff), jnp.float32), 'cms_W2': jax.random.normal(ks[5], (N_LAYERS, dff, d), jnp.float32) * s, 'cms_b2': jnp.zeros((N_LAYERS, d), jnp.float32), 'head_W': jax.random.normal(ks[6], (d, VOCAB), jnp.float32) * s, 'head_b': jnp.zeros((VOCAB,), jnp.float32)}
        return inp
    _L0_tok_all = _L0_tok_setup()
    _L0_tok_in = {k: v for k, v in _L0_tok_all.items() if k in ('emb', 'W_upd', 'b_upd', 'W_f', 'b_f', 'decay_param', 'norm_g', 'norm_b', 'cms_ln_g', 'cms_ln_b', 'cms_W1', 'cms_b1', 'cms_W2', 'cms_b2', 'head_W', 'head_b')}
    del _L0_tok_all

    def _L0_attn_setup():
        import jax, jax.numpy as jnp
        import numpy as np
        S, B, D, H, DH = (128, 32, 64, 8, 32)
        LN_EPS = 1e-05

        def elu_p1(x):
            return jax.nn.elu(x) + 1.0

        def sum_norm(x):
            return x / jnp.sum(x, axis=-1, keepdims=True)

        def layer_norm(x, g, b):
            mu = jnp.mean(x, axis=-1, keepdims=True)
            var = jnp.mean(jnp.square(x - mu), axis=-1, keepdims=True)
            return (x - mu) * jax.lax.rsqrt(var + LN_EPS) * g + b

        def _fast_rnn_forward(x, slow_W, out_W, ln_g, ln_b):
            slen, bsz, _ = x.shape
            o = layer_norm(x, ln_g, ln_b)
            qkv = jnp.einsum('sbd,ed->sbe', o, slow_W)
            qkv = qkv.reshape(slen, bsz, H, 5 * DH + 2)
            q, k, v, rk, rv, beta, rbeta = jnp.split(qkv, [DH, 2 * DH, 3 * DH, 4 * DH, 5 * DH, 5 * DH + 1], axis=-1)
            beta = jax.nn.sigmoid(beta)
            rbeta = jax.nn.sigmoid(rbeta)
            q = sum_norm(elu_p1(q))
            k = sum_norm(elu_p1(k))
            rk = jax.nn.softmax(rk, axis=-1)

            def ff_step(W, inp):
                qt, kt, vt, bt = inp
                v_old = jnp.einsum('bhij,bhj->bhi', W, kt)
                W = W + (bt * (vt - v_old))[..., :, None] * kt[..., None, :]
                z = jnp.einsum('bhij,bhj->bhi', W, qt)
                return (W, z)
            W0 = jnp.zeros((bsz, H, DH, DH), x.dtype)
            _, z = jax.lax.scan(ff_step, W0, (q, k, v, beta))

            def rec_step(carry, inp):
                R, h = carry
                zt, kt, vt, bt = inp
                q_rec = jax.nn.softmax(h, axis=-1)
                v_old = jnp.einsum('bhij,bhj->bhi', R, kt)
                R = R + (bt * (vt - v_old))[..., :, None] * kt[..., None, :]
                h = zt + jnp.einsum('bhij,bhj->bhi', R, q_rec)
                return ((R, h), h)
            R0 = jnp.zeros((bsz, H, DH, DH), x.dtype)
            h0 = jnp.zeros((bsz, H, DH), x.dtype)
            _, hs = jax.lax.scan(rec_step, (R0, h0), (z, rk, rv, rbeta))
            out = hs.reshape(slen, bsz, H * DH)
            out = jnp.einsum('sbe,de->sbd', out, out_W)
            return x + out
        key = jax.random.key(seed)
        k1, k2, k3 = jax.random.split(key, 3)
        x = jax.random.normal(k1, (S, B, D), jnp.float32)
        slow_W = jax.random.normal(k2, (H * (5 * DH + 2), D), jnp.float32) * 0.02
        out_W = jax.random.normal(k3, (D, H * DH), jnp.float32) * 0.02
        ln_g = jnp.ones((D,), jnp.float32)
        ln_b = jnp.zeros((D,), jnp.float32)
        return {'x': x, 'slow_W': slow_W, 'out_W': out_W, 'ln_g': ln_g, 'ln_b': ln_b}
    _L0_attn_all = _L0_attn_setup()
    _L0_attn_in = {k: v for k, v in _L0_attn_all.items() if k in ('slow_W', 'out_W', 'ln_g', 'ln_b')}
    del _L0_attn_all

    def _L0_ffn_setup():
        import math
        import jax, jax.numpy as jnp
        import numpy as np
        CAPACITY_FACTOR = 1.25
        TOP_K = 2
        LN_EPS = 1e-05

        def _layer_norm(x, gamma, beta):
            mu = jnp.mean(x, axis=-1, keepdims=True)
            var = jnp.var(x, axis=-1, keepdims=True)
            return (x - mu) * jax.lax.rsqrt(var + LN_EPS) * gamma + beta
        key = jax.random.key(seed)
        ks = jax.random.split(key, 4)
        B, S, D, F, E = (8, 1024, 64, 128, 8)
        x = jax.random.normal(ks[0], (B, S, D), dtype=jnp.float32)
        Wr = jax.random.normal(ks[1], (D, E), dtype=jnp.float32) / np.sqrt(D)
        br = jnp.zeros((E,), jnp.float32)
        W1 = jax.random.normal(ks[2], (E, D, F), dtype=jnp.float32) / np.sqrt(D)
        b1 = jnp.zeros((E, F), jnp.float32)
        W2 = jax.random.normal(ks[3], (E, F, D), dtype=jnp.float32) / np.sqrt(F)
        b2 = jnp.zeros((E, D), jnp.float32)
        gamma = jnp.ones((D,), jnp.float32)
        beta = jnp.zeros((D,), jnp.float32)
        return {'x': x, 'Wr': Wr, 'br': br, 'W1': W1, 'b1': b1, 'W2': W2, 'b2': b2, 'gamma': gamma, 'beta': beta}
    _L0_ffn_all = _L0_ffn_setup()
    _L0_ffn_in = {k: v for k, v in _L0_ffn_all.items() if k in ('Wr', 'br', 'W1', 'b1', 'W2', 'b2', 'gamma', 'beta')}
    del _L0_ffn_all

    def _L1_attn_setup():
        import jax, jax.numpy as jnp
        import numpy as np
        B, N, C, H = (64, 75, 64, 8)
        STD = 0.02

        def _rel_indices(n):
            d = (jnp.arange(n)[None, :] - jnp.arange(n)[:, None]).astype(jnp.float32)
            return jnp.stack([d, jnp.zeros_like(d), d * d], axis=-1)
        key = jax.random.key(seed)
        ks = jax.random.split(key, 6)
        return {'x': jax.random.normal(ks[0], (B, N, C), jnp.float32), 'Wqk': jax.random.normal(ks[1], (2 * C, C), jnp.float32) * STD, 'Wv': jax.random.normal(ks[2], (C, C), jnp.float32) * STD, 'Wpos': jax.random.normal(ks[3], (H, 3), jnp.float32) * STD, 'bpos': jnp.zeros((H,), jnp.float32), 'Wproj': jax.random.normal(ks[4], (C, C), jnp.float32) * STD, 'bproj': jnp.zeros((C,), jnp.float32), 'gating': jnp.ones((H,), jnp.float32)}
    _L1_attn_all = _L1_attn_setup()
    _L1_attn_in = {k: v for k, v in _L1_attn_all.items() if k in ('Wqk', 'Wv', 'Wpos', 'bpos', 'Wproj', 'bproj', 'gating')}
    del _L1_attn_all

    def _L1_ffn_setup():
        import jax, jax.numpy as jnp
        import numpy as np
        E = 8
        K = 2
        D = 64
        H = 128
        DOUT = 64
        EPS = 1e-05
        key = jax.random.key(seed)
        ks = jax.random.split(key, 9)
        s = 0.02
        return {'x': jax.random.normal(ks[0], (4, 2048, D), jnp.float32), 'gamma': 1.0 + 0.05 * jax.random.normal(ks[1], (D,), jnp.float32), 'beta': 0.05 * jax.random.normal(ks[2], (D,), jnp.float32), 'Wr': 0.01 * jax.random.normal(ks[3], (D, E), jnp.float32), 'br': jnp.zeros((E,), jnp.float32), 'W1': s * jax.random.normal(ks[4], (E, D, H), jnp.float32), 'b1': s * jax.random.normal(ks[5], (E, H), jnp.float32), 'W2': s * jax.random.normal(ks[6], (E, H, DOUT), jnp.float32), 'b2': s * jax.random.normal(ks[7], (E, DOUT), jnp.float32)}
    _L1_ffn_all = _L1_ffn_setup()
    _L1_ffn_in = {k: v for k, v in _L1_ffn_all.items() if k in ('gamma', 'beta', 'Wr', 'br', 'W1', 'b1', 'W2', 'b2')}
    del _L1_ffn_all
    return {'x': x, 'L0_tok_emb': _L0_tok_in['emb'], 'L0_tok_W_upd': _L0_tok_in['W_upd'], 'L0_tok_b_upd': _L0_tok_in['b_upd'], 'L0_tok_W_f': _L0_tok_in['W_f'], 'L0_tok_b_f': _L0_tok_in['b_f'], 'L0_tok_decay_param': _L0_tok_in['decay_param'], 'L0_tok_norm_g': _L0_tok_in['norm_g'], 'L0_tok_norm_b': _L0_tok_in['norm_b'], 'L0_tok_cms_ln_g': _L0_tok_in['cms_ln_g'], 'L0_tok_cms_ln_b': _L0_tok_in['cms_ln_b'], 'L0_tok_cms_W1': _L0_tok_in['cms_W1'], 'L0_tok_cms_b1': _L0_tok_in['cms_b1'], 'L0_tok_cms_W2': _L0_tok_in['cms_W2'], 'L0_tok_cms_b2': _L0_tok_in['cms_b2'], 'L0_tok_head_W': _L0_tok_in['head_W'], 'L0_tok_head_b': _L0_tok_in['head_b'], 'L0_attn_slow_W': _L0_attn_in['slow_W'], 'L0_attn_out_W': _L0_attn_in['out_W'], 'L0_attn_ln_g': _L0_attn_in['ln_g'], 'L0_attn_ln_b': _L0_attn_in['ln_b'], 'L0_ffn_Wr': _L0_ffn_in['Wr'], 'L0_ffn_br': _L0_ffn_in['br'], 'L0_ffn_W1': _L0_ffn_in['W1'], 'L0_ffn_b1': _L0_ffn_in['b1'], 'L0_ffn_W2': _L0_ffn_in['W2'], 'L0_ffn_b2': _L0_ffn_in['b2'], 'L0_ffn_gamma': _L0_ffn_in['gamma'], 'L0_ffn_beta': _L0_ffn_in['beta'], 'L1_attn_Wqk': _L1_attn_in['Wqk'], 'L1_attn_Wv': _L1_attn_in['Wv'], 'L1_attn_Wpos': _L1_attn_in['Wpos'], 'L1_attn_bpos': _L1_attn_in['bpos'], 'L1_attn_Wproj': _L1_attn_in['Wproj'], 'L1_attn_bproj': _L1_attn_in['bproj'], 'L1_attn_gating': _L1_attn_in['gating'], 'L1_ffn_gamma': _L1_ffn_in['gamma'], 'L1_ffn_beta': _L1_ffn_in['beta'], 'L1_ffn_Wr': _L1_ffn_in['Wr'], 'L1_ffn_br': _L1_ffn_in['br'], 'L1_ffn_W1': _L1_ffn_in['W1'], 'L1_ffn_b1': _L1_ffn_in['b1'], 'L1_ffn_W2': _L1_ffn_in['W2'], 'L1_ffn_b2': _L1_ffn_in['b2']}

def reference(x, L0_tok_emb, L0_tok_W_upd, L0_tok_b_upd, L0_tok_W_f, L0_tok_b_f, L0_tok_decay_param, L0_tok_norm_g, L0_tok_norm_b, L0_tok_cms_ln_g, L0_tok_cms_ln_b, L0_tok_cms_W1, L0_tok_cms_b1, L0_tok_cms_W2, L0_tok_cms_b2, L0_tok_head_W, L0_tok_head_b, L0_attn_slow_W, L0_attn_out_W, L0_attn_ln_g, L0_attn_ln_b, L0_ffn_Wr, L0_ffn_br, L0_ffn_W1, L0_ffn_b1, L0_ffn_W2, L0_ffn_b2, L0_ffn_gamma, L0_ffn_beta, L1_attn_Wqk, L1_attn_Wv, L1_attn_Wpos, L1_attn_bpos, L1_attn_Wproj, L1_attn_bproj, L1_attn_gating, L1_ffn_gamma, L1_ffn_beta, L1_ffn_Wr, L1_ffn_br, L1_ffn_W1, L1_ffn_b1, L1_ffn_W2, L1_ffn_b2):
    import jax
    import jax.numpy as jnp

    def _L0_tok_ref(tokens, emb, W_upd, b_upd, W_f, b_f, decay_param, norm_g, norm_b, cms_ln_g, cms_ln_b, cms_W1, cms_b1, cms_W2, cms_b2, head_W, head_b):
        import jax, jax.numpy as jnp
        import numpy as np
        D_MODEL = 128
        N_LAYERS = 4
        VOCAB = 64
        SEQ = 512
        BATCH = 8
        EPS = 1e-05

        def _ln(x, g, b):
            mu = jnp.mean(x, axis=-1, keepdims=True)
            var = jnp.mean(jnp.square(x - mu), axis=-1, keepdims=True)
            return (x - mu) * jax.lax.rsqrt(var + EPS) * g + b

        def _fast_memory(x, mask, W_upd, b_upd, W_f, b_f, decay_param):
            decay = jax.nn.sigmoid(decay_param[0])
            u = jnp.einsum('bsd,de->bse', x, W_upd) + b_upd
            u_t = jnp.swapaxes(u, 0, 1)
            m_t = jnp.swapaxes(mask, 0, 1)[..., None]

            def step(mem, inp):
                u_i, msk = inp
                new = decay * mem + u_i
                mem = msk * new + (1.0 - msk) * mem
                return (mem, mem)
            mem0 = jnp.zeros((x.shape[0], x.shape[2]), x.dtype)
            _, mems = jax.lax.scan(step, mem0, (u_t, m_t))
            mems = jnp.swapaxes(mems, 0, 1)
            return jnp.einsum('bsd,de->bse', mems, W_f) + b_f
        mask = (tokens != 0).astype(emb.dtype)
        x = emb[tokens]
        x = x + _fast_memory(x, mask, W_upd, b_upd, W_f, b_f, decay_param)
        x = _ln(x, norm_g, norm_b)
        for i in range(N_LAYERS):
            h = _ln(x, cms_ln_g[i], cms_ln_b[i])
            h = jax.nn.gelu(jnp.einsum('bsd,df->bsf', h, cms_W1[i]) + cms_b1[i], approximate=False)
            h = jnp.einsum('bsf,fd->bsd', h, cms_W2[i]) + cms_b2[i]
            x = x + h
        return jnp.einsum('bsd,dv->bsv', x, head_W) + head_b

    def _L0_attn_ref(x, slow_W, out_W, ln_g, ln_b):
        import jax, jax.numpy as jnp
        import numpy as np
        S, B, D, H, DH = (128, 32, 64, 8, 32)
        LN_EPS = 1e-05

        def elu_p1(x):
            return jax.nn.elu(x) + 1.0

        def sum_norm(x):
            return x / jnp.sum(x, axis=-1, keepdims=True)

        def layer_norm(x, g, b):
            mu = jnp.mean(x, axis=-1, keepdims=True)
            var = jnp.mean(jnp.square(x - mu), axis=-1, keepdims=True)
            return (x - mu) * jax.lax.rsqrt(var + LN_EPS) * g + b

        def _fast_rnn_forward(x, slow_W, out_W, ln_g, ln_b):
            slen, bsz, _ = x.shape
            o = layer_norm(x, ln_g, ln_b)
            qkv = jnp.einsum('sbd,ed->sbe', o, slow_W)
            qkv = qkv.reshape(slen, bsz, H, 5 * DH + 2)
            q, k, v, rk, rv, beta, rbeta = jnp.split(qkv, [DH, 2 * DH, 3 * DH, 4 * DH, 5 * DH, 5 * DH + 1], axis=-1)
            beta = jax.nn.sigmoid(beta)
            rbeta = jax.nn.sigmoid(rbeta)
            q = sum_norm(elu_p1(q))
            k = sum_norm(elu_p1(k))
            rk = jax.nn.softmax(rk, axis=-1)

            def ff_step(W, inp):
                qt, kt, vt, bt = inp
                v_old = jnp.einsum('bhij,bhj->bhi', W, kt)
                W = W + (bt * (vt - v_old))[..., :, None] * kt[..., None, :]
                z = jnp.einsum('bhij,bhj->bhi', W, qt)
                return (W, z)
            W0 = jnp.zeros((bsz, H, DH, DH), x.dtype)
            _, z = jax.lax.scan(ff_step, W0, (q, k, v, beta))

            def rec_step(carry, inp):
                R, h = carry
                zt, kt, vt, bt = inp
                q_rec = jax.nn.softmax(h, axis=-1)
                v_old = jnp.einsum('bhij,bhj->bhi', R, kt)
                R = R + (bt * (vt - v_old))[..., :, None] * kt[..., None, :]
                h = zt + jnp.einsum('bhij,bhj->bhi', R, q_rec)
                return ((R, h), h)
            R0 = jnp.zeros((bsz, H, DH, DH), x.dtype)
            h0 = jnp.zeros((bsz, H, DH), x.dtype)
            _, hs = jax.lax.scan(rec_step, (R0, h0), (z, rk, rv, rbeta))
            out = hs.reshape(slen, bsz, H * DH)
            out = jnp.einsum('sbe,de->sbd', out, out_W)
            return x + out
        return _fast_rnn_forward(x, slow_W, out_W, ln_g, ln_b)

    def _L0_ffn_ref(x, Wr, br, W1, b1, W2, b2, gamma, beta):
        import math
        import jax, jax.numpy as jnp
        import numpy as np
        CAPACITY_FACTOR = 1.25
        TOP_K = 2
        LN_EPS = 1e-05

        def _layer_norm(x, gamma, beta):
            mu = jnp.mean(x, axis=-1, keepdims=True)
            var = jnp.var(x, axis=-1, keepdims=True)
            return (x - mu) * jax.lax.rsqrt(var + LN_EPS) * gamma + beta
        B, S, D = x.shape
        E = Wr.shape[1]
        N = B * S
        K = TOP_K
        logits = jnp.mean(x, axis=1) @ Wr + br
        routing_weights = jax.nn.softmax(logits, axis=-1)
        capacity = float(math.ceil(N * CAPACITY_FACTOR / E))
        expected_loads = routing_weights.sum(axis=0) * (N / B)
        scale = jnp.where(expected_loads > capacity, capacity / expected_loads, 1.0)
        routing_weights = jax.nn.softmax(routing_weights * scale, axis=-1)
        rw_tok = jnp.broadcast_to(routing_weights[:, None, :], (B, S, E)).reshape(N, E)
        top_w, top_i = jax.lax.top_k(rw_tok, K)
        top_w = jax.nn.softmax(top_w, axis=-1)
        xf = x.reshape(N, D)
        h = jax.nn.gelu(jnp.einsum('nd,edf->enf', xf, W1) + b1[:, None, :], approximate=False)
        y = jnp.einsum('enf,efd->end', h, W2) + b2[:, None, :]
        w_dense = jnp.zeros((N, E), x.dtype).at[jnp.arange(N)[:, None], top_i].add(top_w)
        out = jnp.einsum('ne,end->nd', w_dense, y).reshape(B, S, D)
        out = _layer_norm(out + x, gamma, beta)
        return out

    def _L1_attn_ref(x, Wqk, Wv, Wpos, bpos, Wproj, bproj, gating):
        import jax, jax.numpy as jnp
        import numpy as np
        B, N, C, H = (64, 75, 64, 8)
        STD = 0.02

        def _rel_indices(n):
            d = (jnp.arange(n)[None, :] - jnp.arange(n)[:, None]).astype(jnp.float32)
            return jnp.stack([d, jnp.zeros_like(d), d * d], axis=-1)
        Bb, Nn, Cc = x.shape
        Hh = gating.shape[0]
        hd = Cc // Hh
        scale = hd ** (-0.5)
        qk = (x @ Wqk.T).reshape(Bb, Nn, 2, Hh, hd)
        q = qk[:, :, 0].transpose(0, 2, 1, 3)
        k = qk[:, :, 1].transpose(0, 2, 1, 3)
        patch_score = jax.nn.softmax(jnp.einsum('bhnd,bhmd->bhnm', q, k) * scale, axis=-1)
        rel = _rel_indices(Nn)
        pos_score = (rel @ Wpos.T + bpos).transpose(2, 0, 1)
        pos_score = jax.nn.softmax(pos_score, axis=-1)
        g = jax.nn.sigmoid(gating)[None, :, None, None]
        attn = (1.0 - g) * patch_score + g * pos_score[None]
        attn = attn / attn.sum(axis=-1, keepdims=True)
        v = (x @ Wv.T).reshape(Bb, Nn, Hh, hd).transpose(0, 2, 1, 3)
        out = jnp.einsum('bhnm,bhmd->bhnd', attn, v)
        out = out.transpose(0, 2, 1, 3).reshape(Bb, Nn, Cc)
        return out @ Wproj.T + bproj

    def _L1_ffn_ref(x, gamma, beta, Wr, br, W1, b1, W2, b2):
        import jax, jax.numpy as jnp
        import numpy as np
        E = 8
        K = 2
        D = 64
        H = 128
        DOUT = 64
        EPS = 1e-05
        mu = jnp.mean(x, axis=-1, keepdims=True)
        var = jnp.mean(jnp.square(x - mu), axis=-1, keepdims=True)
        xn = (x - mu) * jax.lax.rsqrt(var + EPS) * gamma + beta
        logits = jnp.einsum('bsd,de->bse', xn, Wr) + br
        top_vals, top_idx = jax.lax.top_k(logits, K)
        w = jax.nn.softmax(top_vals, axis=-1)
        w_full = jnp.einsum('bsk,bske->bse', w, jax.nn.one_hot(top_idx, E, dtype=w.dtype))
        y = jnp.zeros(x.shape[:-1] + (DOUT,), x.dtype)
        for e in range(E):
            h = jax.nn.gelu(jnp.einsum('bsd,dh->bsh', xn, W1[e]) + b1[e], approximate=False)
            y_e = jnp.einsum('bsh,hd->bsd', h, W2[e]) + b2[e]
            y = y + y_e * w_full[..., e, None]
        return y
    h = _L0_tok_ref(x, L0_tok_emb, L0_tok_W_upd, L0_tok_b_upd, L0_tok_W_f, L0_tok_b_f, L0_tok_decay_param, L0_tok_norm_g, L0_tok_norm_b, L0_tok_cms_ln_g, L0_tok_cms_ln_b, L0_tok_cms_W1, L0_tok_cms_b1, L0_tok_cms_W2, L0_tok_cms_b2, L0_tok_head_W, L0_tok_head_b)
    h = h + _L0_attn_ref(_layernorm(h, axis=-1), L0_attn_slow_W, L0_attn_out_W, L0_attn_ln_g, L0_attn_ln_b)
    h = h + _L0_ffn_ref(_layernorm(h, axis=-1), L0_ffn_Wr, L0_ffn_br, L0_ffn_W1, L0_ffn_b1, L0_ffn_W2, L0_ffn_b2, L0_ffn_gamma, L0_ffn_beta)
    h = h + _L1_attn_ref(_layernorm(h, axis=-1), L1_attn_Wqk, L1_attn_Wv, L1_attn_Wpos, L1_attn_bpos, L1_attn_Wproj, L1_attn_bproj, L1_attn_gating)
    h = h + _L1_ffn_ref(_layernorm(h, axis=-1), L1_ffn_gamma, L1_ffn_beta, L1_ffn_Wr, L1_ffn_br, L1_ffn_W1, L1_ffn_b1, L1_ffn_W2, L1_ffn_b2)
    return h

_drawn_inputs = setup_inputs


def setup_inputs(seed=0):
    import zlib

    import numpy as np

    out = dict(_drawn_inputs(seed))
    spreads = {'L0_tok_b_upd': (0.0, 0.1),
     'L0_tok_b_f': (0.0, 0.1),
     'L0_tok_norm_g': (1.0, 0.2),
     'L0_tok_norm_b': (0.0, 0.1),
     'L0_tok_cms_ln_g': (1.0, 0.2),
     'L0_tok_cms_ln_b': (0.0, 0.8),
     'L0_tok_cms_b1': (0.0, 0.1),
     'L0_tok_cms_b2': (0.0, 0.1),
     'L0_tok_head_b': (0.0, 0.1),
     'L0_attn_ln_g': (1.0, 0.6),
     'L0_attn_ln_b': (0.0, 0.8),
     'L0_ffn_br': (0.0, 0.8),
     'L0_ffn_b1': (0.0, 0.38),
     'L0_ffn_b2': (0.0, 0.269),
     'L0_ffn_gamma': (1.0, 0.2),
     'L0_ffn_beta': (0.0, 0.1),
     'L1_attn_bpos': (0.0, 2.0),
     'L1_attn_bproj': (0.0, 0.1),
     'L1_attn_gating': (1.0, 0.6),
     'L1_ffn_br': (0.0, 0.8)}
    factors = {'L0_tok_W_upd': 6.214,
     'L1_attn_Wqk': 64.0,
     'L1_attn_Wv': 4.596,
     'L1_attn_Wpos': 8.0,
     'L1_attn_Wproj': 4.349,
     'L1_ffn_gamma': 8.0,
     'L1_ffn_beta': 8.0,
     'L1_ffn_Wr': 7.862,
     'L1_ffn_W1': 8.0,
     'L1_ffn_b1': 26.267,
     'L1_ffn_W2': 8.0,
     'L1_ffn_b2': 41.652}
    for name, (base, spread) in spreads.items():
        noise = np.random.default_rng([zlib.crc32(name.encode()), seed]).standard_normal(out[name].shape)
        drawn = base * np.exp(spread * noise) if base else spread * noise
        out[name] = jnp.asarray(drawn.astype(out[name].dtype))
    for name, factor in factors.items():
        out[name] = (out[name] * factor).astype(out[name].dtype)
    return out
```

```python
from contextlib import ExitStack

import concourse.bass as bass
from concourse import mybir

ALU = mybir.AluOpType
ACT = mybir.ActivationFunctionType
F32 = mybir.dt.float32
I32 = mybir.dt.int32
AX_X = mybir.AxisListType.X

EPS = 1e-5
P = 128

T = 16
DT = 128
NL = 4
VOC = 64
D = 64
NH, DH = 8, 32
HB = NH * DH
E, FF = 8, 128
HD = D // NH
CH = 4
NC = T // CH
N = T * P

ROWS = [("norm_g", DT), ("norm_b", DT), ("b2", NL * DT), ("b_upd", DT), ("b_f", DT), ("head_b", VOC), ("decay", 1),
        ("br0", E), ("gamma0", D), ("beta0", D), ("bpos", NH), ("wpos", 3 * NH), ("bproj", D),
        ("gating", NH), ("br1", E)]
COLS = [("ln_g", NL), ("ln_b", NL), ("b1", NL * 4), ("eb10", E), ("eb11", E),
        ("aln_g", 1), ("aln_b", 1), ("gamma1", 1), ("beta1", 1)]


def offsets(parts):
    at, out = 0, {}
    for name, n in parts:
        out[name] = (at, at + n)
        at += n
    return out, at


class Chain:

    def __init__(self, eng, sem):
        self.eng, self.sem, self.n = eng, sem, 0

    def __call__(self, ins):
        ins.then_inc(self.sem, 1)
        self.n += 1

    def settle(self):
        self.eng.wait_ge(self.sem, self.n)


def pieces(n, step=4):
    return [(r, min(r + step, n)) for r in range(0, n, step)]


def piece_base(n, extra=0):
    return sum(len(pieces(t + extra)) for t in range(n))


def upd_count(t):
    return piece_base(t) + piece_base(t, 1)


def build(nc, a):
    ROW, NROW = offsets(ROWS)
    COL, NCOL = offsets(COLS)
    with ExitStack() as ctx:
        def sb(name, shape, dt=F32):
            return ctx.enter_context(nc.sbuf_tensor(name, shape, dt))

        def sem(name):
            return ctx.enter_context(nc.semaphore(name))

        bank = [ctx.enter_context(nc.psum_tensor(f"bank{i}", [P, 512], F32)) for i in range(8)]

        rows = sb("rows", [P, NROW])
        cols = sb("cols", [P, NCOL])
        ident = sb("ident", [P, P])
        ones = sb("ones", [P, P])
        neghalf = sb("neghalf", [P, T])
        iota_i = sb("iota_i", [P, 1], I32)
        iota_f = sb("iota_f", [P, 1])
        emb = sb("emb", [VOC, DT])
        embT = sb("embT", [DT, VOC])
        wupd = sb("wupd", [DT, DT])
        wf = sb("wf", [DT, DT])
        w1 = sb("w1", [DT, NL, 4 * DT])
        w2 = sb("w2", [P, NL, 4, DT])
        headw = sb("headw", [DT, VOC])
        sloww = sb("sloww", [D, 5 * HB + 2 * NH])
        outw = sb("outw", [P, 2, D])
        ew1 = [sb(f"ew1_{k}", [D, E, FF]) for k in range(2)]
        ew2 = [sb(f"ew2_{k}", [FF, E, D]) for k in range(2)]
        wr = [sb(f"wr_{k}", [D, E]) for k in range(2)]
        wq = sb("wq", [D, D])
        wk = sb("wk", [D, D])
        eb2 = [sb(f"eb2_{k}", [P, D]) for k in range(2)]
        wv = sb("wv", [D, D])
        wproj = sb("wproj", [D, D])

        def row(name, n=None, parts=P):
            lo, hi = ROW[name]
            return rows[0:parts, lo:hi]

        def col(name, k=0, parts=P):
            lo = COL[name][0]
            return cols[0:parts, lo + k:lo + k + 1]

        H = sb("H", [P, T, D])
        XN = sb("XN", [P, T, D])
        X = sb("X", [P, T, DT])
        stats = sb("stats", [P, 4, T, 6])
        mv = sb("mv", [P, 4, T, 2])
        rstd = sb("rstd", [P, 4, T])
        xT = sb("xT", [P, 2, 512])
        G = sb("G", [P, 8, 512])
        decay = sb("decay", [P, 4])
        utab = sb("utab", [VOC, DT])
        embf = sb("embf", [VOC, DT])

        KK = sb("KK", [P, T, 2, HB])
        UV = sb("UV", [P, T, 2, HB])
        QQ = sb("QQ", [P, T, HB])
        HS = QQ
        PA = G[:].rearrange("p (k r) n -> p k r n", k=2)
        PB = sb("PB", [P, 2, 4, 2 * HB])
        PC = sb("PC", [P, 2, 4, HB])
        PD = sb("PD", [P, 4, HB])
        CA = sb("CA", [P, T, 2, NH])
        CZ = sb("CZ", [P, T, 2, NH])
        beta = sb("beta", [P, T, 2, NH])
        er = sb("er", [P, 2, HB])
        dd = sb("dd", [P, 2, HB])
        e1 = PB[:, 0, 0:2, :]
        r1 = PB[:, 0, 2:4, :]
        smallv = sb("smallv", [P, 8, 32])
        smallp = sb("smallp", [P, 2, 32])
        mx = sb("mx", [P, 2, 8])

        def flat(t, sizes):
            names = {2: "a b", 3: "a b c"}[len(sizes)]
            return t.rearrange(f"p {names} -> p ({names})")
        KKf = KK[:].rearrange("p t n h -> p (t n h)")
        tok = KKf[:, 0:N].bitcast(I32)
        onehot = KKf[0:VOC, N:2 * N]
        keep = KKf[:, 2 * N:3 * N]
        memT = KKf[:, 3 * N:4 * N]
        QQf = QQ[:].rearrange("p t h -> p (t h)")
        iszero = QQf[:, 0:N]
        UVf = UV[:].rearrange("p t n h -> p (t n h)")
        xn_tok = UVf[:, 0:1024].rearrange("p (k t d) -> p k t d", k=2, t=CH)
        xb_tok = UVf[:, 1024:3072].rearrange("p (k t d) -> p k t d", k=NC, t=CH)
        xtmp = UVf[:, 3072:5120].rearrange("p (t d) -> p t d", t=T)

        G2 = [G[:], KKf[:, 0:4096].rearrange("p (e n) -> p e n", e=E)]
        w2w = KKf[:, 4096:5120].rearrange("p (k e d) -> p k e d", k=2, e=E)
        ytmp = KKf[:, 5120:6144].rearrange("p (k e d) -> p k e d", k=2, e=E)
        b2x = KKf[:, 6144:8192].rearrange("p (k t d) -> p k t d", k=2, t=T)
        qd = UVf[0:D + NH, 0:4096].rearrange("p (h n) -> p h n", h=NH)
        kaug = UVf[0:D + NH, 4096:4608]
        pexp = UVf[:, 4608:6656].rearrange("p (k h n) -> p k h n", k=2, h=NH)
        vaug = UVf[:, 6656:6944].rearrange("p (t h d) -> p t h d", t=CH, h=NH)
        posT = UVf[:, 6944:7968].rearrange("p (h n) -> p h n", h=NH)
        QQf2 = QQ[:].rearrange("p t h -> p (t h)")
        plog = QQf2[:, 0:1024].rearrange("p (h m) -> p h m", h=NH)
        rel = QQf2[:, 1024:1152]
        rel2 = QQf2[:, 1152:1280]
        rel_i = QQf2[:, 1280:1408].bitcast(I32)
        nmax = QQf2[:, 1408:1408 + 2 * (D + NH)].rearrange("p (k n) -> p k n", k=2)
        att = QQf2[:, 1600:1600 + 256].rearrange("p (t d) -> p t d", t=CH)
        att2 = QQf2[:, 1856:1856 + 256].rearrange("p (t d) -> p t d", t=CH)
        cmp1 = QQf2[:, 2112:3136]
        cmp2 = PD[:].rearrange("p r n -> p (r n)")
        YB = [X[:].rearrange("p t d -> p (t d)")[:, 1024 * k:1024 * k + 1024].rearrange("p (t d) -> p t d", t=T)
              for k in range(2)]
        wts = sb("wts", [P, T, E])
        wtsT = sb("wtsT", [P, P])
        rout = sb("rout", [P, T, E])
        rsel = sb("rsel", [P, T, E])
        rsm = sb("rsm", [P, 4, T])
        meanT = sb("meanT", [D, T])
        m16 = sb("m16", [P, T])
        lower = sb("lower", [P, E, E])
        gate = sb("gate", [P, 4, NH])
        comb = sb("comb", [P, 6, CH * NH])

        s = {n: sem(n) for n in """
            load_tok load_rows load_emb load_mlp load_attn load_experts stored
            consts dve_chain act_chain pool_chain
            ln_var ln_rstd decay_exp utab_mm tables_ready u_mm mem_ready x_mm norm_scaled norm_done
            xb_ready tok_norm tok_T tok_hT tok_up tok_gelu tok_down tok_add
            head_T head_xT head_mm head_add
            a_norm a_T a_oT a_qkv a_acts a_acts2 a_sub a_rexp a_elu a_keys a_rsum a_read a_rc
            gram_p gram_used zc_p zc_used upd_p upd_mm upd_used acc_done h_exp e_sub hs_saved
            o_T o_evict o_mm o_add
            masks b2x_ready x_norm mean_mm mean_ready logit_mm r_sub r_exp r_prob load_mm r_spread
            spread_mm w_ready wT_mm wT_ready bias_mm base_ready w2w_ready x_T x_xT x_up x_gelu x_down y_read
            y_ready f1_norm f_affine
            p_rel p_sub p_exp p_done p_T p_evict gate_exp
            d_norm d_T d_xT d_q d_qd d_k d_kcopy d_v d_vcopy s_mm s_max nm_T aug_ready st_mm p_ready av_mm pos_mm
            comb_done at_T at_xT proj_mm d_add hb_ready
            e_norm e_xT rl_mm rl_read rl_exp out_done
            """.split()}

        block = ctx.enter_context(nc.Block())

        LN = [("norm", c) for c in range(NC)] + [("tok", u) for u in range(NL * NC)]
        for c in range(NC):
            LN += [("a1", c), ("a2", c)]
        for k in ("f0", "f1", "d"):
            LN += [(k, c) for c in range(NC)]
        for c in range(NC):
            LN += [("e1", c), ("e2", c)]
        LNI = {k: i for i, k in enumerate(LN)}

        def qd_rows(j):
            return qd[D:D + NH, :, P * j:P * j + P]

        def xin(k, c):
            return xT[0:D, c % 2, :] if k == 0 else UVf[0:D, 512 * c:512 * c + 512]

        def rstd_pool(pool, ch, key, n):
            i = LNI[key]
            k = i % 4
            pool.wait_ge(s["ln_var"], i + 1)
            ch(pool.tensor_scalar(rstd[:, k, 0:n], mv[:, k, 0:n, 1], EPS, None, ALU.add))
            ch.settle()
            pool.tensor_tensor(rstd[:, k, 0:n], rstd[:, k, 0:n], neghalf[:, 0:n], ALU.pow).then_inc(s["ln_rstd"], 1)

        def norm_stats(dve, ch, key, tiles):
            i = LNI[key]
            k = i % 4
            for j, x in enumerate(tiles):
                ch(dve.bn_stats(stats[:, k, j, :], x))
            ch.settle()
            for j in range(len(tiles)):
                last = dve.bn_aggr(mv[:, k, j, :], stats[:, k, j, :])
                if j < len(tiles) - 1:
                    ch(last)
            last.then_inc(s["ln_var"], 1)

        def norm_apply(dve, key, tiles, outs):
            i = LNI[key]
            k = i % 4
            dve.wait_ge(s["ln_var"], i + 1)
            dve.wait_ge(s["ln_rstd"], i + 1)
            for j, (x, o) in enumerate(zip(tiles, outs)):
                last = dve.tensor_scalar(o, x, mv[:, k, j, 0:1], rstd[:, k, j:j + 1], ALU.subtract, ALU.mult)
            return last

        @block.sync
        def _(sp):
            sp.dma_start(tok, a["tok"].partition_broadcast(P)).then_inc(s["load_tok"], 16)
            sp.dma_start(rows[:], a["rows"].partition_broadcast(P)).then_inc(s["load_rows"], 16)
            sp.dma_start(cols[:], a["cols"]).then_inc(s["load_rows"], 16)
            for t, n in ((emb, "emb"), (embT, "embT"), (wupd, "wupd"), (wf, "wf")):
                sp.dma_start(t[:], a[n]).then_inc(s["load_emb"], 16)
            for t, n in ((w1, "w1"), (w2, "w2"), (headw, "headw")):
                sp.dma_start(t[:], a[n]).then_inc(s["load_mlp"], 16)
            for t, n in ((sloww, "sloww"), (outw, "outw")):
                sp.dma_start(t[:], a[n]).then_inc(s["load_attn"], 16)
            for k in range(2):
                for t, n in ((ew1, "ew1"), (ew2, "ew2"), (wr, "wr"), (eb2, "eb2")):
                    sp.dma_start(t[k][:], a[f"{n}_{k}"]).then_inc(s["load_experts"], 16)
            for t, n in ((wq, "wq"), (wk, "wk"), (wv, "wv"), (wproj, "wproj")):
                sp.dma_start(t[:], a[n]).then_inc(s["load_experts"], 16)
            for c in range(NC):
                sp.wait_ge(s["out_done"], c + 1)
                sp.dma_start(a["out"][:, CH * c:CH * c + CH, :], H[:, CH * c:CH * c + CH, :]).then_inc(s["stored"], 16)
            sp.wait_ge(s["stored"], 16 * NC)

        @block.gpsimd
        def _(pool):
            ch = Chain(pool, s["pool_chain"])
            ch(pool.memset(ident[:], 0.0))
            ch(pool.memset(ones[:], 1.0))
            ch(pool.memset(neghalf[:], -0.5))
            ch(pool.iota(iota_i[:], pattern=[[0, 1]], base=0, channel_multiplier=1))
            ch.settle()
            ch(pool.affine_select(out=ident[:], in_=ident[:], compare_op=ALU.not_equal, fill=1.0, base=0,
                                  pattern=[[-1, P]], channel_multiplier=1))
            ch.settle()
            pool.tensor_copy(iota_f[:], iota_i[:]).then_inc(s["consts"], 1)
            ch(pool.memset(m16[:], 1.0))
            ch(pool.memset(lower[:], 1.0))
            ch.settle()
            ch(pool.affine_select(out=m16[:], in_=m16[:], compare_op=ALU.is_ge, fill=0.0, base=0,
                                  pattern=[[-E, T]], channel_multiplier=1))
            ch.settle()
            pool.affine_select(out=m16[:], in_=m16[:], compare_op=ALU.is_ge, fill=0.0, base=E - 1,
                               pattern=[[E, T]], channel_multiplier=-1).then_inc(s["masks"], 1)
            pool.affine_select(out=lower[:], in_=lower[:], compare_op=ALU.is_ge, fill=0.0, base=-1,
                               pattern=[[1, E], [-1, E]], channel_multiplier=0).then_inc(s["masks"], 1)
            pool.wait_ge(s["load_rows"], 32)
            for c in range(NC):
                rstd_pool(pool, ch, ("norm", c), CH)
            for c in range(NC):
                xc = X[:, CH * c:CH * c + CH, :]
                pool.wait_ge(s["norm_scaled"], c + 1)
                g = row("norm_g").unsqueeze(1).broadcast_to([P, CH, DT])
                b = row("norm_b").unsqueeze(1).broadcast_to([P, CH, DT])
                ch(pool.tensor_tensor(xc, xtmp[:, CH * c:CH * c + CH, :], g, ALU.mult))
                ch.settle()
                pool.tensor_tensor(xc, xc, b, ALU.add).then_inc(s["norm_done"], 1)
            b2 = row("b2").rearrange("p (l d) -> p l d", l=NL)

            def plus_b2(u):
                i, c = divmod(u, NC)
                if u < NC:
                    pool.wait_ge(s["norm_done"], c + 1)
                else:
                    pool.wait_ge(s["tok_add"], u - NC + 1)
                pool.tensor_tensor(xb_tok[:, c], X[:, CH * c:CH * c + CH, :],
                                   b2[:, i, :].unsqueeze(1).broadcast_to([P, CH, DT]), ALU.add).then_inc(s["xb_ready"], 1)

            for u in range(NL * NC):
                rstd_pool(pool, ch, ("tok", u), CH)
                plus_b2(u)

            for t in range(T):
                if t % CH == 0:
                    rstd_pool(pool, ch, ("a1", t // CH), CH)
                    rstd_pool(pool, ch, ("a2", t // CH), CH)
                k = t % 2
                pool.wait_ge(s["a_elu"], t + 1)
                ch(pool.tensor_tensor(QQ[:, t, :].rearrange("p (h j) -> p h j", h=NH),
                                      e1[:, k, 0:HB].rearrange("p (h j) -> p h j", h=NH),
                                      smallv[:, k, 0:NH].unsqueeze(2).broadcast_to([P, NH, DH]), ALU.mult))
                ch(pool.tensor_tensor(KK[:, t, 0, :].rearrange("p (h j) -> p h j", h=NH),
                                      e1[:, k, HB:].rearrange("p (h j) -> p h j", h=NH),
                                      smallv[:, k, NH:2 * NH].unsqueeze(2).broadcast_to([P, NH, DH]), ALU.mult))
                pool.tensor_tensor(KK[:, t, 1, :].rearrange("p (h j) -> p h j", h=NH),
                                   er[:, k, :].rearrange("p (h j) -> p h j", h=NH),
                                   smallv[:, k, 16:24].unsqueeze(2).broadcast_to([P, NH, DH]),
                                   ALU.mult).then_inc(s["a_keys"], 1)
            ch.settle()
            pool.wait_ge(s["a_keys"], T)

            for t in range(T):
                for j, (r0, r1_) in enumerate(pieces(t)):
                    i = piece_base(t) + j
                    R = r1_ - r0
                    if i >= 2:
                        pool.wait_ge(s["gram_used"], i - 1)
                    pool.tensor_tensor(PA[:, i % 2, 0:R, :], KK[:, r0:r1_].rearrange("p r n h -> p r (n h)"),
                                       KK[:, t].rearrange("p n h -> p (n h)").unsqueeze(1).broadcast_to([P, R, 2 * HB]),
                                       ALU.mult).then_inc(s["gram_p"], 1)
                for j, (r0, r1_) in enumerate(pieces(t + 1)):
                    i = piece_base(t, 1) + j
                    R = r1_ - r0
                    if i >= 2:
                        pool.wait_ge(s["zc_used"], i - 1)
                    pool.tensor_tensor(PC[:, i % 2, 0:R, :], KK[:, r0:r1_, 0, :],
                                       QQ[:, t].unsqueeze(1).broadcast_to([P, R, HB]),
                                       ALU.mult).then_inc(s["zc_p"], 1)

            pool.wait_ge(s["load_experts"], 16 * 12)
            pool.wait_ge(s["masks"], 2)
            for c in range(NC):
                rstd_pool(pool, ch, ("f0", c), CH)
            pool.wait_ge(s["x_norm"], 1)
            for k in range(2):
                pool.tensor_tensor(b2x[:, k], eb2[k][:].unsqueeze(1).broadcast_to([P, T, D]),
                                   m16[:].unsqueeze(2).broadcast_to([P, T, D]), ALU.mult).then_inc(s["b2x_ready"], 1)
            ch(pool.iota(rel_i, pattern=[[1, P]], base=0, channel_multiplier=-1))
            ch.settle()
            ch(pool.tensor_copy(rel, rel_i))
            ch.settle()
            pool.tensor_tensor(rel2, rel, rel, ALU.mult).then_inc(s["p_rel"], 1)
            pool.wait_ge(s["w_ready"], 1)
            for c in range(NC):
                for t in range(CH * c, CH * c + CH):
                    if t >= 2:
                        pool.wait_ge(s["x_down"], t - 1)
                    pool.tensor_tensor(w2w[:, t % 2], ew2[0][:], wts[:, t].unsqueeze(2).broadcast_to([P, E, D]),
                                       ALU.mult).then_inc(s["w2w_ready"], 1)
                rstd_pool(pool, ch, ("f1", c), CH)
                r = slice(CH * c, CH * c + CH)
                pool.wait_ge(s["f1_norm"], c + 1)
                yb = YB[1][:, r, :]
                ch(pool.tensor_tensor(yb, yb, row("gamma0").unsqueeze(1).broadcast_to([P, CH, D]), ALU.mult))
                ch.settle()
                ch(pool.tensor_tensor(yb, yb, row("beta0").unsqueeze(1).broadcast_to([P, CH, D]), ALU.add))
                ch.settle()
                pool.tensor_tensor(H[:, r, :], H[:, r, :], yb, ALU.add).then_inc(s["f_affine"], 1)
            for c in range(NC):
                rstd_pool(pool, ch, ("d", c), CH)
                r = slice(CH * c, CH * c + CH)
                pool.wait_ge(s["f_affine"], NC)
                pool.wait_ge(s["d_norm"], c + 1)
                pool.tensor_tensor(H[:, r, :], H[:, r, :], row("bproj").unsqueeze(1).broadcast_to([P, CH, D]),
                                   ALU.add).then_inc(s["hb_ready"], 1)
            for c in range(NC):
                rstd_pool(pool, ch, ("e1", c), CH)
                rstd_pool(pool, ch, ("e2", c), CH)

        @block.scalar
        def _(act):
            ch = Chain(act, s["act_chain"])
            act.wait_ge(s["load_rows"], 32)
            act.activation(decay[:, 0:1], row("decay"), ACT.Exp, scale=-1.0).then_inc(s["decay_exp"], 1)

            def evict_T(u):
                i, c = divmod(u, NC)
                act.wait_ge(s["tok_T"], u + 1)
                if u >= 2:
                    act.wait_ge(s["tok_up"], 4 * (u - 1))
                act.activation(xT[:, u % 2, :], bank[u % 2][:], ACT.Identity, bias=col("ln_b", i),
                               scale=col("ln_g", i)).then_inc(s["tok_hT"], 1)

            def gelus(u):
                i, c = divmod(u, NC)
                for f in range(4):
                    act.wait_ge(s["tok_up"], 4 * u + f + 1)
                    if u >= 2 and f == 0:
                        act.wait_ge(s["tok_down"], u - 1)
                    act.activation(G[:, 4 * (u % 2) + f, :], bank[2 + f % 2][:], ACT.Gelu,
                                   bias=col("b1", 4 * i + f)).then_inc(s["tok_gelu"], 1)

            U = NL * NC
            evict_T(0)
            gelus(0)
            evict_T(1)
            gelus(1)
            for u in range(U):
                if u + 2 < U:
                    evict_T(u + 2)
                    gelus(u + 2)
            for c in range(NC):
                act.wait_ge(s["head_T"], c + 1)
                if c >= 2:
                    act.wait_ge(s["head_mm"], c - 1)
                act.activation(xT[:, c % 2, :], bank[c % 2][:], ACT.Copy).then_inc(s["head_xT"], 1)

            def first(t):
                k = t % 2
                act.wait_ge(s["a_qkv"], t + 1)
                if t >= 2:
                    act.wait_ge(s["a_keys"], t - 1)
                act.activation(e1[:, k, :], bank[2][:], ACT.Exp)
                act.activation(r1[:, k, :], bank[2][:], ACT.Relu)
                act.activation(UV[:, t].rearrange("p n h -> p (n h)"), bank[3][:], ACT.Copy).then_inc(s["a_acts"], 1)

            def second(t):
                k = t % 2
                act.wait_ge(s["a_sub"], t + 1)
                act.activation(er[:, k, :], dd[:, k, :], ACT.Exp)
                bt = beta[:, t].rearrange("p n h -> p (n h)")
                act.activation(bt, bt, ACT.Exp, scale=-1.0).then_inc(s["a_rexp"], 1)

            for t in range(T):
                if t % CH == 0:
                    c = t // CH
                    act.wait_ge(s["a_T"], c + 1)
                    if c >= 2:
                        act.wait_ge(s["a_qkv"], CH * (c - 1))
                    act.activation(xT[0:D, c % 2, :], bank[c % 2][0:D, :], ACT.Identity, bias=col("aln_b", parts=D),
                                   scale=col("aln_g", parts=D)).then_inc(s["a_oT"], 1)
                first(t)
                second(t)

            for t in range(1, T):
                act.wait_ge(s["upd_mm"], upd_count(t))
                act.wait_ge(s["e_sub"], t)
                act.activation(er[:, t % 2, :], dd[:, t % 2, :], ACT.Exp).then_inc(s["h_exp"], 1)
                act.activation(HS[:, t - 1, :], bank[6][:, 0:HB], ACT.Copy).then_inc(s["hs_saved"], 1)
            act.wait_ge(s["upd_mm"], upd_count(T))
            act.activation(HS[:, T - 1, :], bank[6][:, 0:HB], ACT.Copy).then_inc(s["hs_saved"], 1)

            for t in range(T):
                act.wait_ge(s["o_T"], t + 1)
                if t >= 2:
                    act.wait_ge(s["o_mm"], t - 1)
                act.activation(xT[:, t % 2, 0:2 * P], bank[t % 2][:, 0:2 * P], ACT.Copy).then_inc(s["o_evict"], 1)

            def experts(k, c):
                x = NC * k + c
                act.wait_ge(s["x_T"], x + 1)
                if k == 0 and c >= 2:
                    act.wait_ge(s["x_up"], E * (c - 1))
                dst, src = xin(k, c), bank[x % 2][0:D, :]
                if k == 0:
                    act.activation(dst, src, ACT.Copy).then_inc(s["x_xT"], 1)
                else:
                    act.activation(dst, src, ACT.Identity, bias=col("beta1", parts=D),
                                   scale=col("gamma1", parts=D)).then_inc(s["x_xT"], 1)

            def expert_gelus(k, c):
                x = NC * k + c
                for e in range(E):
                    act.wait_ge(s["x_up"], E * x + e + 1)
                    if e == 0 and x >= 2:
                        act.wait_ge(s["x_down"], CH * (x - 1))
                    act.activation(G2[x % 2][:, e, :], bank[2 + e % 2][:], ACT.Gelu,
                                   bias=col(f"eb1{k}", e)).then_inc(s["x_gelu"], 1)

            act.wait_ge(s["mean_mm"], 1)
            act.activation(meanT[:], bank[7][0:D, 0:T], ACT.Copy, scale=1.0 / P).then_inc(s["mean_ready"], 1)
            for j in range(3):
                act.wait_ge(s["r_sub"], j + 1)
                act.activation(rsel[0:T, j, :], rsel[0:T, j, :], ACT.Exp).then_inc(s["r_exp"], 1)
            act.wait_ge(s["p_sub"], 1)
            act.activation(plog, plog, ACT.Exp).then_inc(s["p_exp"], 1)
            act.activation(gate[:, 0, :], row("gating"), ACT.Exp, scale=-1.0).then_inc(s["gate_exp"], 1)
            act.wait_ge(s["wT_mm"], 1)
            act.activation(wtsT[:], bank[7][:, 256:384], ACT.Copy).then_inc(s["wT_ready"], 1)
            for g in range(2):
                act.wait_ge(s["p_T"], g + 1)
                act.activation(posT[:, 4 * g:4 * g + 4, :].rearrange("p h n -> p (h n)"), bank[g][:],
                               ACT.Copy).then_inc(s["p_evict"], 1)
            for c in range(NC):
                experts(0, c)
                expert_gelus(0, c)

            for c in range(NC):
                act.wait_ge(s["d_T"], c + 1)
                act.activation(xT[0:D, 0, :], bank[0][0:D, :], ACT.Copy).then_inc(s["d_xT"], 1)
                act.wait_ge(s["d_q"], c + 1)
                if c:
                    act.wait_ge(s["st_mm"], 2 * CH * c)
                for h in range(NH):
                    act.activation(qd[0:D, h, :], bank[1][0:D, :], ACT.Copy,
                                   scale=m16[0:D, h:h + 1]).then_inc(s["d_qd"], 1)
                act.wait_ge(s["d_k"], c + 1)
                act.activation(kaug[0:D, :], bank[2][0:D, :], ACT.Copy).then_inc(s["d_kcopy"], 1)
                act.wait_ge(s["d_v"], c + 1)
                if c:
                    act.wait_ge(s["av_mm"], CH * c)
                    act.wait_ge(s["pos_mm"], c)
                act.activation(vaug[:, :, :, 0:HD], bank[3][:, 0:CH * D].rearrange("p (t h d) -> p t h d", t=CH, h=NH),
                               ACT.Copy).then_inc(s["d_vcopy"], 1)
                for j in range(CH):
                    t = CH * c + j
                    for g in range(2):
                        act.wait_ge(s["st_mm"], 2 * t + g + 1)
                        if t >= 2:
                            act.wait_ge(s["av_mm"], t - 1)
                        act.activation(pexp[:, t % 2, 4 * g:4 * g + 4, :].rearrange("p h n -> p (h n)"), bank[4 + g][:],
                                       ACT.Exp, scale=float(HD) ** -0.5).then_inc(s["p_ready"], 1)
                act.wait_ge(s["at_T"], c + 1)
                act.activation(xT[0:D, 1, :], bank[0][0:D, :], ACT.Copy).then_inc(s["at_xT"], 1)

            for c in range(NC):
                experts(1, c)
            act.wait_ge(s["rl_read"], 1)
            act.activation(rsel[:], rsel[:], ACT.Exp).then_inc(s["rl_exp"], 1)
            act.wait_ge(s["wT_mm"], 2)
            act.activation(wtsT[:], bank[7][:, 256:384], ACT.Copy).then_inc(s["wT_ready"], 1)
            for c in range(NC):
                expert_gelus(1, c)

        @block.tensor
        def _(pe):
            mm = nc.tensor.matmul
            pe.wait_ge(s["load_emb"], 64)
            mm(bank[0][0:VOC, 0:DT], embT[:], wupd[:], start=True, stop=True).then_inc(s["utab_mm"], 1)
            pe.wait_ge(s["tables_ready"], 1)
            for c in range(NC):
                if c >= 2:
                    pe.wait_ge(s["mem_ready"], c - 1)
                mm(bank[2 + c % 2][:], utab[:], onehot[:, 512 * c:512 * c + 512],
                   start=True, stop=True).then_inc(s["u_mm"], 1)
            for c in range(NC):
                pe.wait_ge(s["mem_ready"], c + 1)
                if c == 0:
                    pe.wait_ge(s["tables_ready"], 2)
                for j in range(CH):
                    t = CH * c + j
                    o = bank[4 + c][:, DT * j:DT * j + DT]
                    mm(o, onehot[:, P * t:P * t + P], embf[:], start=True, stop=False)
                    last = mm(o, memT[:, P * t:P * t + P], wf[:], start=False, stop=True)
                last.then_inc(s["x_mm"], 1)

            def turn(u):
                pe.wait_ge(s["tok_norm"], u + 1)
                if u >= 2:
                    pe.wait_ge(s["tok_hT"], u - 1)
                for j in range(CH):
                    last = nc.tensor.transpose(bank[u % 2][:, P * j:P * j + P], xn_tok[:, u % 2, j, :], ident[:])
                last.then_inc(s["tok_T"], 1)

            def up(u):
                i, c = divmod(u, NC)
                pe.wait_ge(s["tok_hT"], u + 1)
                for f in range(4):
                    if 4 * u + f >= 2:
                        pe.wait_ge(s["tok_gelu"], 4 * u + f - 1)
                    mm(bank[2 + f % 2][:], w1[:, i, P * f:P * f + P], xT[:, u % 2, :],
                       start=True, stop=True).then_inc(s["tok_up"], 1)

            def down(u):
                i, c = divmod(u, NC)
                pe.wait_ge(s["tok_gelu"], 4 * u + 4)
                if u >= 2:
                    pe.wait_ge(s["tok_add"], u - 1)
                for j in range(CH):
                    for f in range(4):
                        last = mm(bank[4 + u % 2][:, DT * j:DT * j + DT], G[:, 4 * (u % 2) + f, P * j:P * j + P],
                                  w2[:, i, f, :], start=(f == 0), stop=(f == 3))
                last.then_inc(s["tok_down"], 1)

            U = NL * NC
            pe.wait_ge(s["load_mlp"], 48)
            turn(0)
            pe.wait_ge(s["mem_ready"], NC)
            up(0)
            turn(1)
            up(1)
            for u in range(U):
                if u + 2 < U:
                    turn(u + 2)
                down(u)
                if u + 2 < U:
                    up(u + 2)
            for c in range(NC):
                pe.wait_ge(s["tok_add"], U - NC + c + 1)
                if c == 0:
                    pe.wait_ge(s["tok_hT"], U)
                if c >= 2:
                    pe.wait_ge(s["head_xT"], c - 1)
                for j in range(CH):
                    last = nc.tensor.transpose(bank[c % 2][:, P * j:P * j + P], X[:, CH * c + j, :], ident[:])
                last.then_inc(s["head_T"], 1)
                pe.wait_ge(s["head_xT"], c + 1)
                if c >= 2:
                    pe.wait_ge(s["head_add"], c - 1)
                if c == 0:
                    pe.wait_ge(s["tok_add"], U)
                for j in range(CH):
                    last = mm(bank[4 + c % 2][:, VOC * j:VOC * j + VOC], xT[:, c % 2, P * j:P * j + P], headw[:],
                              start=True, stop=True)
                last.then_inc(s["head_mm"], 1)

            pe.wait_ge(s["load_attn"], 32)
            for t in range(T):
                c = t // CH
                if t % CH == 0:
                    pe.wait_ge(s["a_norm"], c + 1)
                    if c == 0:
                        pe.wait_ge(s["head_add"], NC)
                        pe.wait_ge(s["head_xT"], NC)
                    if c >= 2:
                        pe.wait_ge(s["a_oT"], c - 1)
                    for j in range(CH):
                        last = nc.tensor.transpose(bank[c % 2][0:D, P * j:P * j + P], X[:, t + j, 0:D], ident[:])
                    last.then_inc(s["a_T"], 1)
                    pe.wait_ge(s["a_oT"], c + 1)
                if t:
                    pe.wait_ge(s["a_acts"], t)
                    pe.wait_ge(s["a_sub"], t)
                o = xT[0:D, c % 2, P * (t % CH):P * (t % CH) + P]
                mm(bank[2][:], o, sloww[:, 0:512], start=True, stop=True)
                mm(bank[3][:], o, sloww[:, 512:1024], start=True, stop=True)
                mm(bank[4][:, 0:HB + 16], o, sloww[:, 1024:], start=True, stop=True).then_inc(s["a_qkv"], 1)

            n_p = 0
            for t in range(T):
                ps = pieces(t)
                for j, (r0, r1_) in enumerate(ps):
                    n_p += 1
                    pe.wait_ge(s["upd_p"], n_p)
                    if j == 0 and t > 1:
                        pe.wait_ge(s["acc_done"], t - 1)
                    for r in range(r0, r1_):
                        last = mm(bank[5][:], ident[:], PB[:, (n_p - 1) % 2, r - r0, :], start=(r == 0), stop=(r == t - 1))
                    last.then_inc(s["upd_mm"], 1)
                ps = pieces(t + 1)
                for j, (r0, r1_) in enumerate(ps):
                    n_p += 1
                    pe.wait_ge(s["upd_p"], n_p)
                    if j == 0 and t > 0:
                        pe.wait_ge(s["hs_saved"], t)
                        pe.wait_ge(s["e_sub"], t)
                    for r in range(r0, r1_):
                        for n in range(2):
                            last = mm(bank[6][:, 0:HB], ident[:], PB[:, (n_p - 1) % 2, r - r0, HB * n:HB * n + HB],
                                      start=(r == 0 and n == 0), stop=(r == t and n == 1))
                    last.then_inc(s["upd_mm"], 1)

            for t in range(T):
                pe.wait_ge(s["hs_saved"], T)
                if t >= 2:
                    pe.wait_ge(s["o_evict"], t - 1)
                for n in range(2):
                    last = nc.tensor.transpose(bank[t % 2][:, P * n:P * n + P], HS[:, t, P * n:P * n + P], ident[:])
                last.then_inc(s["o_T"], 1)
                pe.wait_ge(s["o_evict"], t + 1)
                if t >= 8 and t % CH == 0:
                    pe.wait_ge(s["o_add"], t // CH - 1)
                for n in range(2):
                    last = mm(bank[2 + (t // CH) % 2][:, D * (t % CH):D * (t % CH) + D], xT[:, t % 2, P * n:P * n + P], outw[:, n, :],
                              start=(n == 0), stop=(n == 1))
                last.then_inc(s["o_mm"], 1)

            tr = nc.tensor.transpose

            def turn_x(k, c):
                x = NC * k + c
                if x >= 2:
                    pe.wait_ge(s["x_xT"], x - 1)
                src = XN if k == 0 else YB[0]
                for j in range(CH):
                    last = tr(bank[x % 2][0:D, P * j:P * j + P], src[:, CH * c + j, :], ident[:])
                last.then_inc(s["x_T"], 1)

            def expert_up(k, c):
                x = NC * k + c
                pe.wait_ge(s["x_xT"], x + 1)
                for e in range(E):
                    i = E * x + e
                    if i >= 2:
                        pe.wait_ge(s["x_gelu"], i - 1)
                    mm(bank[2 + e % 2][:], ew1[k][:, e, :], xin(k, c),
                       start=True, stop=True).then_inc(s["x_up"], 1)

            def expert_down(k, c):
                x = NC * k + c
                pe.wait_ge(s["x_gelu"], E * x + E)
                for j in range(CH):
                    t = CH * c + j
                    i = T * k + t
                    if i >= 2:
                        pe.wait_ge(s["y_read"], i - 1)
                    if k == 0:
                        pe.wait_ge(s["w2w_ready"], t + 1)
                    for e in range(E):
                        g = G2[x % 2][:, e, P * j:P * j + P]
                        if k == 0:
                            last = mm(bank[4 + t % 2][:, 0:D], g, w2w[:, t % 2, e, :], start=(e == 0), stop=(e == E - 1))
                        else:
                            last = mm(bank[4 + t % 2][:, D * e:D * e + D], g, ew2[1][:, e, :], start=True, stop=True)
                    last.then_inc(s["x_down"], 1)

            def bias(k):
                tr(bank[7][:, 256:384], wts[:].rearrange("p t e -> p (t e)"), ident[:]).then_inc(s["wT_mm"], 1)
                pe.wait_ge(s["wT_ready"], k + 1)
                for g in range(2):
                    mm(bank[4 + g][:], wtsT[:], b2x[:, k, 8 * g:8 * g + 8, :].rearrange("p t d -> p (t d)"),
                       start=True, stop=True).then_inc(s["bias_mm"], 1)

            pe.wait_ge(s["load_experts"], 16 * 12)
            pe.wait_ge(s["x_norm"], NC)
            for t in range(T):
                last = mm(bank[7][0:D, t:t + 1], XN[:, t, :], ones[:, 0:1], start=True, stop=True)
            last.then_inc(s["mean_mm"], 1)
            pe.wait_ge(s["mean_ready"], 1)
            mm(bank[7][0:T, 64:64 + E], meanT[:], wr[0][:], start=True, stop=True).then_inc(s["logit_mm"], 1)
            pe.wait_ge(s["r_prob"], 1)
            mm(bank[7][0:T, 96:96 + E], ones[0:T, 0:T], rout[0:T, 0, :], start=True, stop=True).then_inc(s["load_mm"], 1)
            pe.wait_ge(s["r_spread"], 1)
            mm(bank[7][:, 128:256], ones[0:T, :], rsel[0:T].rearrange("p t e -> p (t e)"),
               start=True, stop=True).then_inc(s["spread_mm"], 1)
            pe.wait_ge(s["w_ready"], 1)
            pe.wait_ge(s["b2x_ready"], 2)
            bias(0)
            pe.wait_ge(s["p_done"], 1)
            for g in range(2):
                for j in range(4):
                    last = tr(bank[g][:, P * j:P * j + P], plog[:, 4 * g + j, :], ident[:])
                last.then_inc(s["p_T"], 1)
            pe.wait_ge(s["base_ready"], 2)
            pe.wait_ge(s["p_evict"], 2)
            turn_x(0, 0)
            expert_up(0, 0)
            for c in range(NC):
                if c + 1 < NC:
                    turn_x(0, c + 1)
                    expert_up(0, c + 1)
                expert_down(0, c)

            def scores(t):
                n = slice(P * (t % CH), P * (t % CH) + P)
                if t:
                    pe.wait_ge(s["s_max"], t)
                for h in range(NH):
                    last = mm(bank[2 + h // 4][:, P * (h % 4):P * (h % 4) + P], qd[0:D, h, n], kaug[0:D, n],
                              start=True, stop=True)
                last.then_inc(s["s_mm"], 1)

            def turn_max(t):
                pe.wait_ge(s["s_max"], t + 1)
                if t:
                    pe.wait_ge(s["aug_ready"], t)
                tr(bank[7][0:D + NH, 0:P], nmax[:, t % 2, :], ident[:]).then_inc(s["nm_T"], 1)

            def scores_T(t):
                n = slice(P * (t % CH), P * (t % CH) + P)
                pe.wait_ge(s["aug_ready"], t + 1)
                for g in range(2):
                    if t:
                        pe.wait_ge(s["p_ready"], 2 * t - 1 + g)
                    mm(bank[4 + g][:], kaug[:, n], qd[:, 4 * g:4 * g + 4, n], start=True, stop=True).then_inc(s["st_mm"], 1)

            def values(t):
                pe.wait_ge(s["p_ready"], 2 * t + 2)
                j = t % CH
                if j == 0 and t:
                    pe.wait_ge(s["comb_done"], t // CH)
                for h in range(NH):
                    o = 9 * (NH * j + h)
                    last = mm(bank[6][:, o:o + 9], pexp[:, t % 2, h, :], vaug[:, j, h, :], start=True, stop=True)
                last.then_inc(s["av_mm"], 1)

            for c in range(NC):
                pe.wait_ge(s["d_norm"], c + 1)
                if c == 0:
                    pe.wait_ge(s["y_read"], T)
                if c:
                    pe.wait_ge(s["at_xT"], c)
                for j in range(CH):
                    last = tr(bank[0][0:D, P * j:P * j + P], XN[:, CH * c + j, :], ident[:])
                last.then_inc(s["d_T"], 1)
                pe.wait_ge(s["d_xT"], c + 1)
                if c:
                    pe.wait_ge(s["d_add"], c)
                    pe.wait_ge(s["s_max"], CH * c)
                mm(bank[1][0:D, :], wq[:], xT[0:D, 0, :], start=True, stop=True).then_inc(s["d_q"], 1)
                mm(bank[2][0:D, :], wk[:], xT[0:D, 0, :], start=True, stop=True).then_inc(s["d_k"], 1)
                for j in range(CH):
                    last = mm(bank[3][:, D * j:D * j + D], xT[0:D, 0, P * j:P * j + P], wv[:], start=True, stop=True)
                last.then_inc(s["d_v"], 1)
                pe.wait_ge(s["d_qd"], NH * (c + 1))
                pe.wait_ge(s["d_kcopy"], c + 1)
                pe.wait_ge(s["d_vcopy"], c + 1)
                scores(CH * c)
                for j in range(CH):
                    t = CH * c + j
                    turn_max(t)
                    if j + 1 < CH:
                        scores(t + 1)
                    scores_T(t)
                    if j:
                        values(t - 1)
                values(CH * c + CH - 1)
                for h in range(NH):
                    last = mm(bank[1][:, 36 * h:36 * h + 36], posT[:, h, :], vaug[:, :, h, :], start=True, stop=True)
                last.then_inc(s["pos_mm"], 1)
                pe.wait_ge(s["comb_done"], c + 1)
                for j in range(CH):
                    last = tr(bank[0][0:D, P * j:P * j + P], att[:, j, :], ident[:])
                last.then_inc(s["at_T"], 1)
                pe.wait_ge(s["at_xT"], c + 1)
                for j in range(CH):
                    last = mm(bank[1][:, D * j:D * j + D], xT[0:D, 1, P * j:P * j + P], wproj[:], start=True, stop=True)
                last.then_inc(s["proj_mm"], 1)

            for c in range(NC):
                pe.wait_ge(s["e_norm"], c + 1)
                if c == 0:
                    pe.wait_ge(s["d_add"], NC)
                turn_x(1, c)
                pe.wait_ge(s["x_xT"], NC + c + 1)
                for j in range(CH):
                    t = CH * c + j
                    last = mm(bank[7][:, E * t:E * t + E], xin(1, c)[:, P * j:P * j + P], wr[1][:],
                              start=True, stop=True)
                last.then_inc(s["rl_mm"], 1)
            pe.wait_ge(s["w_ready"], 2)
            bias(1)
            pe.wait_ge(s["base_ready"], 4)
            for c in range(NC):
                expert_up(1, c)
                expert_down(1, c)

        @block.vector
        def _(dve):
            ch = Chain(dve, s["dve_chain"])
            dve.wait_ge(s["consts"], 1)
            dve.wait_ge(s["load_tok"], 16)
            ch(dve.tensor_scalar(onehot, tok[0:VOC, :], iota_f[0:VOC, 0:1], None, ALU.is_equal))
            dve.wait_ge(s["decay_exp"], 1)
            ch(dve.tensor_scalar(decay[:, 1:2], decay[:, 0:1], 1.0, None, ALU.add))
            ch.settle()
            ch(dve.reciprocal(decay[:, 2:3], decay[:, 1:2]))
            ch.settle()
            ch(dve.tensor_scalar(keep, tok, 0.0, decay[:, 2:3], ALU.not_equal, ALU.mult))
            ch(dve.tensor_scalar(iszero, tok, 0.0, None, ALU.is_equal))
            ch.settle()
            ch(dve.tensor_tensor(keep, keep, iszero, ALU.add))
            ch.settle()
            ch(dve.memset(keep.rearrange("p (t q) -> p t q", t=T)[:, :, 0], 0.0))
            dve.wait_ge(s["utab_mm"], 1)
            dve.wait_ge(s["load_rows"], 32)
            dve.wait_ge(s["load_emb"], 64)
            ch(dve.tensor_tensor(utab[:], bank[0][0:VOC, 0:DT], row("b_upd", parts=VOC), ALU.add))
            ch.settle()
            ch(dve.memset(utab[0:1, :], 0.0))
            ch.settle()
            dve.tensor_copy(decay[:, 3:4], decay[:, 2:3]).then_inc(s["tables_ready"], 1)
            dve.tensor_tensor(embf[:], emb[:], row("b_f", parts=VOC), ALU.add).then_inc(s["tables_ready"], 1)
            for c in range(NC):
                dve.wait_ge(s["u_mm"], c + 1)
                dve.tensor_tensor_scan(memT[:, 512 * c:512 * c + 512], keep[:, 512 * c:512 * c + 512],
                                       bank[2 + c % 2][:], 0.0, ALU.mult, ALU.add).then_inc(s["mem_ready"], 1)
            for c in range(NC):
                dve.wait_ge(s["x_mm"], NC)
                tiles = [bank[4 + c][:, DT * j:DT * j + DT] for j in range(CH)]
                norm_stats(dve, ch, ("norm", c), tiles)
            for c in range(NC):
                tiles = [bank[4 + c][:, DT * j:DT * j + DT] for j in range(CH)]
                norm_apply(dve, ("norm", c), tiles, [xtmp[:, CH * c + j, :] for j in range(CH)])\
                    .then_inc(s["norm_scaled"], 1)

            def norm(u):
                i, c = divmod(u, NC)
                if u < NC:
                    dve.wait_ge(s["norm_done"], c + 1)
                else:
                    dve.wait_ge(s["tok_add"], u - NC + 1)
                tiles = [X[:, CH * c + j, :] for j in range(CH)]
                norm_stats(dve, ch, ("tok", u), tiles)
                if u >= 2:
                    dve.wait_ge(s["tok_T"], u - 1)
                norm_apply(dve, ("tok", u), tiles, [xn_tok[:, u % 2, j, :] for j in range(CH)]).then_inc(s["tok_norm"], 1)

            def add(u):
                i, c = divmod(u, NC)
                dve.wait_ge(s["tok_down"], u + 1)
                dve.wait_ge(s["xb_ready"], u + 1)
                dve.tensor_tensor(X[:, CH * c:CH * c + CH, :], bank[4 + u % 2][:].rearrange("p (t d) -> p t d", t=CH),
                                  xb_tok[:, c], ALU.add).then_inc(s["tok_add"], 1)

            U = NL * NC
            norm(0)
            norm(1)
            for u in range(U):
                if u + 2 < U:
                    norm(u + 2)
                add(u)
            for c in range(NC):
                dve.wait_ge(s["head_mm"], c + 1)
                dve.tensor_tensor(H[:, CH * c:CH * c + CH, :],
                                  bank[4 + c % 2][:, 0:CH * VOC].rearrange("p (t d) -> p t d", t=CH),
                                  row("head_b").unsqueeze(1).broadcast_to([P, CH, VOC]), ALU.add).then_inc(s["head_add"], 1)

            for c in range(NC):
                r = range(CH * c, CH * c + CH)
                dve.wait_ge(s["head_add"], c + 1)
                norm_stats(dve, ch, ("a1", c), [H[:, t, :] for t in r])
                ch(norm_apply(dve, ("a1", c), [H[:, t, :] for t in r], [XN[:, t, :] for t in r]))
                ch.settle()
                norm_stats(dve, ch, ("a2", c), [XN[:, t, :] for t in r])
                if c == 0:
                    dve.wait_ge(s["head_T"], NC)
                norm_apply(dve, ("a2", c), [XN[:, t, :] for t in r], [X[:, t, 0:D] for t in r]).then_inc(s["a_norm"], 1)
                for t in r:
                    k = t % 2
                    heads = [P, NH, DH]
                    dve.wait_ge(s["a_qkv"], t + 1)
                    rk = bank[4][:, 0:HB].rearrange("p (h j) -> p h j", h=NH)
                    bt = beta[:, t].rearrange("p n h -> p (n h)")
                    ch(dve.tensor_reduce(mx[:, k, :], rk, AX_X, ALU.max))
                    ch(dve.tensor_copy(bt, bank[4][:, HB:HB + 16]))
                    ch.settle()
                    dve.tensor_tensor(dd[:, k, :].rearrange("p (h j) -> p h j", h=NH), rk,
                                      mx[:, k, :].unsqueeze(2).broadcast_to(heads), ALU.subtract).then_inc(s["a_sub"], 1)
                    dve.wait_ge(s["a_acts"], t + 1)
                    ch(dve.scalar_tensor_tensor(out=e1[:, k, :], in0=e1[:, k, :], scalar=1.0, in1=r1[:, k, :],
                                                op0=ALU.min, op1=ALU.add))
                    ch.settle()
                    ch(dve.tensor_reduce(smallv[:, 2 + k, 0:16], e1[:, k, :].rearrange("p (h j) -> p h j", h=2 * NH), AX_X, ALU.add))
                    dve.wait_ge(s["a_rexp"], t + 1)
                    ch(dve.tensor_scalar(bt, bt, 1.0, None, ALU.add))
                    ch(dve.tensor_reduce(smallv[:, 2 + k, 16:24], er[:, k, :].rearrange("p (h j) -> p h j", h=NH), AX_X, ALU.add))
                    ch.settle()
                    ch(dve.reciprocal(bt, bt))
                    dve.reciprocal(smallv[:, k, 0:24], smallv[:, 2 + k, 0:24]).then_inc(s["a_elu"], 1)

            dve.wait_ge(s["a_keys"], T)
            ch(dve.memset(er[:, 0, :], 1.0))
            ch.settle()
            n_p = n_g = n_z = 0

            def combine(coef, r0, r1_):
                nonlocal n_p
                if n_p >= 2:
                    dve.wait_ge(s["upd_mm"], n_p - 1)
                R = r1_ - r0
                dve.tensor_tensor(PB[:, n_p % 2, 0:R, :].rearrange("p r (g j) -> p (r g) j", g=2 * NH),
                                  UV[:, r0:r1_].rearrange("p r n (h j) -> p (r n h) j", h=NH),
                                  coef[:, r0:r1_].rearrange("p r n h -> p (r n h)").unsqueeze(2)
                                  .broadcast_to([P, R * 2 * NH, DH]), ALU.mult).then_inc(s["upd_p"], 1)
                n_p += 1

            for t in range(T):
                k = t % 2
                if t:
                    h = bank[6][:, 0:HB].rearrange("p (h j) -> p h j", h=NH)
                    dve.wait_ge(s["upd_mm"], upd_count(t))
                    ch(dve.tensor_reduce(mx[:, k, :], h, AX_X, ALU.max))
                    ch.settle()
                    dve.tensor_tensor(dd[:, k, :].rearrange("p (h j) -> p h j", h=NH), h,
                                      mx[:, k, :].unsqueeze(2).broadcast_to([P, NH, DH]), ALU.subtract).then_inc(s["e_sub"], 1)
                for r0, r1_ in pieces(t):
                    dve.wait_ge(s["gram_p"], n_g + 1)
                    dve.tensor_reduce(CA[:, r0:r1_].rearrange("p r n h -> p (r n h)"),
                                      PA[:, n_g % 2, 0:r1_ - r0, :].rearrange("p r (g j) -> p (r g) j", g=2 * NH),
                                      AX_X, ALU.add).then_inc(s["gram_used"], 1)
                    n_g += 1
                    dve.wait_ge(s["gram_used"], n_g)
                    combine(CA, r0, r1_)
                for r0, r1_ in pieces(t + 1):
                    dve.wait_ge(s["zc_p"], n_z + 1)
                    dve.tensor_reduce(CZ[:, r0:r1_, 0, :],
                                      PC[:, n_z % 2, 0:r1_ - r0, :].rearrange("p r (g j) -> p r g j", g=NH),
                                      AX_X, ALU.add).then_inc(s["zc_used"], 1)
                    n_z += 1
                if t:
                    dve.wait_ge(s["h_exp"], t)
                ch(dve.tensor_reduce(smallv[:, 4, 0:NH], er[:, k, :].rearrange("p (h j) -> p h j", h=NH), AX_X, ALU.add))
                ch.settle()
                ch(dve.reciprocal(smallv[:, 5, 0:NH], smallv[:, 4, 0:NH]))
                for r0, r1_ in pieces(t + 1):
                    R = r1_ - r0
                    ch(dve.tensor_tensor(PD[:, 0:R, :], KK[:, r0:r1_, 1, :],
                                         er[:, k, :].unsqueeze(1).broadcast_to([P, R, HB]), ALU.mult))
                    ch.settle()
                    ch(dve.tensor_reduce(CZ[:, r0:r1_, 1, :], PD[:, 0:R, :].rearrange("p r (g j) -> p r g j", g=NH),
                                         AX_X, ALU.add))
                    ch.settle()
                ch(dve.tensor_tensor(CZ[:, 0:t + 1, 1, :], CZ[:, 0:t + 1, 1, :],
                                     smallv[:, 5, 0:NH].unsqueeze(1).broadcast_to([P, t + 1, NH]), ALU.mult))
                ut = UV[:, t].rearrange("p n (h j) -> p (n h) j", h=NH)
                if t:
                    dve.wait_ge(s["upd_mm"], n_p)
                    ch(dve.tensor_tensor(UV[:, t].rearrange("p n h -> p (n h)"), UV[:, t].rearrange("p n h -> p (n h)"),
                                         bank[5][:], ALU.subtract))
                    ch.settle()
                dve.tensor_tensor(ut, ut, beta[:, t].rearrange("p n h -> p (n h)").unsqueeze(2)
                                  .broadcast_to([P, 2 * NH, DH]), ALU.mult).then_inc(s["acc_done"], 1)
                dve.wait_ge(s["acc_done"], t + 1)
                ch.settle()
                dve.wait_ge(s["zc_used"], n_z)
                for r0, r1_ in pieces(t + 1):
                    combine(CZ, r0, r1_)

            for c in range(NC):
                dve.wait_ge(s["o_mm"], CH * c + CH)
                hc = H[:, CH * c:CH * c + CH, :]
                ch(dve.tensor_tensor(hc, hc, XN[:, CH * c:CH * c + CH, :], ALU.add))
                ch.settle()
                dve.tensor_tensor(hc, bank[2 + c % 2][:, 0:CH * D].rearrange("p (t d) -> p t d", t=CH), hc,
                                  ALU.add).then_inc(s["o_add"], 1)

            sub, mul, plus = ALU.subtract, ALU.mult, ALU.add
            tt = dve.tensor_tensor
            ch(dve.memset(vaug[:, :, :, HD:HD + 1], 1.0))
            ch(dve.memset(kaug[D:D + NH, :], 1.0))
            ch(dve.memset(nmax, 0.0))
            dve.wait_ge(s["masks"], 2)
            for c in range(NC):
                r = range(CH * c, CH * c + CH)
                dve.wait_ge(s["o_add"], c + 1)
                norm_stats(dve, ch, ("f0", c), [H[:, t, :] for t in r])
                norm_apply(dve, ("f0", c), [H[:, t, :] for t in r], [XN[:, t, :] for t in r]).then_inc(s["x_norm"], 1)

            def rank2(x, sel, n, parts):
                shape = [parts, n, E, E]
                own, other = x.unsqueeze(3).broadcast_to(shape), x.unsqueeze(2).broadcast_to(shape)
                a_, b_ = (c[0:parts, 0:n * E * E].rearrange("p (t e f) -> p t e f", t=n, e=E) for c in (cmp1, cmp2))
                ch(tt(a_, other, own, ALU.is_gt))
                ch(tt(b_, other, own, ALU.is_equal))
                ch.settle()
                ch(tt(b_, b_, lower[0:parts].unsqueeze(1).broadcast_to(shape), mul))
                ch.settle()
                ch(tt(a_, a_, b_, plus))
                ch.settle()
                ch(dve.tensor_reduce(sel, a_, AX_X, plus))
                ch.settle()
                ch(dve.tensor_scalar(sel, sel, 1.5, None, ALU.is_lt))
                ch.settle()

            def small_softmax(x, j, out):
                m, z = rsm[0:T, 0, j:j + 1], rsm[0:T, 1, j:j + 1]
                ch(dve.tensor_reduce(m, x, AX_X, ALU.max))
                ch.settle()
                dve.tensor_scalar(rsel[0:T, j, :], x, m, None, sub).then_inc(s["r_sub"], 1)
                dve.wait_ge(s["r_exp"], j + 1)
                if out is None:
                    return
                ch(dve.tensor_reduce(z, rsel[0:T, j, :], AX_X, plus))
                ch.settle()
                ch(dve.reciprocal(z, z))
                ch.settle()
                return dve.tensor_scalar(out, rsel[0:T, j, :], z, None, mul)

            CAPACITY = float(-(-N * 5 // (4 * E)))
            dve.wait_ge(s["logit_mm"], 1)
            ch(tt(rout[0:T, 3, :], bank[7][0:T, 64:64 + E], row("br0", parts=T), plus))
            ch.settle()
            small_softmax(rout[0:T, 3, :], 0, rout[0:T, 0, :]).then_inc(s["r_prob"], 1)
            dve.wait_ge(s["load_mm"], 1)
            sc = rout[0:T, 4, :]
            ch(dve.tensor_scalar(sc, bank[7][0:T, 96:96 + E], float(P), None, mul))
            ch.settle()
            ch(dve.reciprocal(sc, sc))
            ch.settle()
            ch(dve.tensor_scalar(sc, sc, CAPACITY, 1.0, mul, ALU.min))
            ch.settle()
            dve.wait_ge(s["r_prob"], 1)
            ch(tt(rout[0:T, 1, :], rout[0:T, 0, :], sc, mul))
            ch.settle()
            ch(small_softmax(rout[0:T, 1, :], 1, rout[0:T, 2, :]))
            ch.settle()
            small_softmax(rout[0:T, 2, :], 2, None)
            rank2(rout[0:T, 2:3, :], rout[0:T, 5:6, :], 1, T)
            w = rout[0:T, 5, :]
            ch(tt(w, w, rsel[0:T, 2, :], mul))
            ch.settle()
            ch(dve.tensor_reduce(rsm[0:T, 2, 0:1], w, AX_X, plus))
            ch.settle()
            ch(dve.reciprocal(rsm[0:T, 2, 1:2], rsm[0:T, 2, 0:1]))
            ch.settle()
            ch(dve.tensor_scalar(w, w, rsm[0:T, 2, 1:2], None, mul))
            ch.settle()
            tt(rsel[0:T], w.unsqueeze(1).broadcast_to([T, T, E]), ident[0:T, 0:T].unsqueeze(2).broadcast_to([T, T, E]),
               mul).then_inc(s["r_spread"], 1)
            dve.wait_ge(s["spread_mm"], 1)
            dve.tensor_copy(wts[:].rearrange("p t e -> p (t e)"), bank[7][:, 128:256]).then_inc(s["w_ready"], 1)

            dve.wait_ge(s["p_rel"], 1)
            wp = row("wpos").rearrange("p (k h) -> p k h", k=3)
            ch(dve.scalar_tensor_tensor(out=gate[:, 3, :], in0=wp[:, 1, :], scalar=0.0, in1=row("bpos"), op0=mul, op1=plus))
            ch.settle()
            for h in range(NH):
                ch(dve.tensor_scalar(plog[:, h, :], rel, wp[:, 0, h:h + 1], gate[:, 3, h:h + 1], mul, plus))
            ch.settle()
            for h in range(NH):
                ch(dve.scalar_tensor_tensor(out=plog[:, h, :], in0=rel2, scalar=wp[:, 2, h:h + 1], in1=plog[:, h, :],
                                            op0=mul, op1=plus))
            ch.settle()
            ch(dve.tensor_reduce(comb[:, 0, 0:NH], plog, AX_X, ALU.max))
            ch.settle()
            tt(plog, plog, comb[:, 0, 0:NH].unsqueeze(2).broadcast_to([P, NH, P]), sub).then_inc(s["p_sub"], 1)
            dve.wait_ge(s["p_exp"], 1)
            ch(dve.tensor_reduce(comb[:, 0, 0:NH], plog, AX_X, plus))
            ch.settle()
            ch(dve.reciprocal(comb[:, 0, 8:8 + NH], comb[:, 0, 0:NH]))
            ch.settle()
            tt(plog, plog, comb[:, 0, 8:8 + NH].unsqueeze(2).broadcast_to([P, NH, P]), mul).then_inc(s["p_done"], 1)
            dve.wait_ge(s["gate_exp"], 1)
            ch(dve.tensor_scalar(gate[:, 0, :], gate[:, 0, :], 1.0, None, plus))
            ch.settle()
            ch(dve.reciprocal(gate[:, 1, :], gate[:, 0, :]))
            ch.settle()
            ch(dve.tensor_scalar(gate[:, 2, :], gate[:, 1, :], -1.0, 1.0, mul, plus))

            for g in range(2):
                dve.wait_ge(s["bias_mm"], g + 1)
                r = slice(8 * g, 8 * g + 8)
                tt(YB[0][:, r, :], bank[4 + g][:].rearrange("p (t d) -> p t d", t=8), XN[:, r, :],
                   plus).then_inc(s["base_ready"], 1)
            dve.wait_ge(s["base_ready"], 2)
            for c in range(NC):
                r = range(CH * c, CH * c + CH)
                for t in r:
                    dve.wait_ge(s["x_down"], t + 1)
                    tt(YB[0][:, t, :], bank[4 + t % 2][:, 0:D], YB[0][:, t, :], plus).then_inc(s["y_read"], 1)
                dve.wait_ge(s["y_read"], CH * c + CH)
                norm_stats(dve, ch, ("f1", c), [YB[0][:, t, :] for t in r])
                norm_apply(dve, ("f1", c), [YB[0][:, t, :] for t in r], [YB[1][:, t, :] for t in r]).then_inc(s["f1_norm"], 1)

            for c in range(NC):
                r = range(CH * c, CH * c + CH)
                dve.wait_ge(s["f_affine"], c + 1)
                norm_stats(dve, ch, ("d", c), [H[:, t, :] for t in r])
                norm_apply(dve, ("d", c), [H[:, t, :] for t in r], [XN[:, t, :] for t in r]).then_inc(s["d_norm"], 1)
            th = [P, CH, NH]
            g_ = gate[:, 1, :].unsqueeze(1).broadcast_to(th)
            omg = gate[:, 2, :].unsqueeze(1).broadcast_to(th)
            cb = [comb[:, k, :].rearrange("p (t h) -> p t h", t=CH) for k in range(6)]
            ch.settle()
            for c in range(NC):
                for j in range(CH):
                    t = CH * c + j
                    dve.wait_ge(s["s_mm"], t + 1)
                    for g in range(2):
                        last = dve.tensor_reduce(nmax[:, t % 2, D + 4 * g:D + 4 * g + 4],
                                                 bank[2 + g][:].rearrange("p (h m) -> p h m", h=4), AX_X, ALU.max, negate=True)
                    last.then_inc(s["s_max"], 1)
                    dve.wait_ge(s["nm_T"], t + 1)
                    tt(qd_rows(j), bank[7][D:D + NH, 0:P].unsqueeze(1).broadcast_to([NH, NH, P]),
                       ident[D:D + NH, D:D + NH].unsqueeze(2).broadcast_to([NH, NH, P]), mul).then_inc(s["aug_ready"], 1)
                dve.wait_ge(s["av_mm"], CH * c + CH)
                dve.wait_ge(s["pos_mm"], c + 1)
                o = bank[6][:, 0:CH * NH * 9].rearrange("p (t h d) -> p t h d", t=CH, h=NH)
                po = bank[1][:, 0:CH * NH * 9].rearrange("p (h t d) -> p t h d", t=CH, h=NH)
                ch(dve.reciprocal(cb[0], o[:, :, :, HD]))
                ch(tt(cb[3], po[:, :, :, HD], g_, mul))
                ch.settle()
                ch(tt(cb[1], cb[0], omg, mul))
                ch.settle()
                ch(tt(cb[2], o[:, :, :, HD], cb[1], mul))
                ch.settle()
                ch(tt(cb[2], cb[2], cb[3], plus))
                ch.settle()
                ch(dve.reciprocal(cb[4], cb[2]))
                ch.settle()
                ch(tt(cb[1], cb[1], cb[4], mul))
                ch(tt(cb[5], cb[4], g_, mul))
                ch.settle()
                full = [P, CH, NH, HD]
                ch(tt(att.rearrange("p t (h d) -> p t h d", h=NH), o[:, :, :, 0:HD], cb[1].unsqueeze(3).broadcast_to(full), mul))
                ch(tt(att2.rearrange("p t (h d) -> p t h d", h=NH), po[:, :, :, 0:HD], cb[5].unsqueeze(3).broadcast_to(full), mul))
                ch.settle()
                tt(att, att, att2, plus).then_inc(s["comb_done"], 1)
                dve.wait_ge(s["proj_mm"], c + 1)
                dve.wait_ge(s["hb_ready"], c + 1)
                hc = H[:, CH * c:CH * c + CH, :]
                tt(hc, bank[1][:, 0:CH * D].rearrange("p (t d) -> p t d", t=CH), hc, plus).then_inc(s["d_add"], 1)

            for c in range(NC):
                r = range(CH * c, CH * c + CH)
                dve.wait_ge(s["d_add"], c + 1)
                norm_stats(dve, ch, ("e1", c), [H[:, t, :] for t in r])
                ch(norm_apply(dve, ("e1", c), [H[:, t, :] for t in r], [XN[:, t, :] for t in r]))
                ch.settle()
                norm_stats(dve, ch, ("e2", c), [XN[:, t, :] for t in r])
                norm_apply(dve, ("e2", c), [XN[:, t, :] for t in r], [YB[0][:, t, :] for t in r]).then_inc(s["e_norm"], 1)
            te = [P, T, E]
            dve.wait_ge(s["rl_mm"], NC)
            ch(tt(rout[:], bank[7][:, 0:T * E].rearrange("p (t e) -> p t e", t=T),
                  row("br1").unsqueeze(1).broadcast_to(te), plus))
            ch.settle()
            ch(dve.tensor_reduce(rsm[:, 0, :], rout[:], AX_X, ALU.max))
            ch.settle()
            tt(rsel[:], rout[:], rsm[:, 0, :].unsqueeze(2).broadcast_to(te), sub).then_inc(s["rl_read"], 1)
            rank2(rout[:], wts[:], T, P)
            dve.wait_ge(s["rl_exp"], 1)
            ch(tt(wts[:], wts[:], rsel[:], mul))
            ch.settle()
            ch(dve.tensor_reduce(rsm[:, 1, :], wts[:], AX_X, plus))
            ch.settle()
            ch(dve.reciprocal(rsm[:, 2, :], rsm[:, 1, :]))
            ch.settle()
            tt(wts[:], wts[:], rsm[:, 2, :].unsqueeze(2).broadcast_to(te), mul).then_inc(s["w_ready"], 1)
            dve.wait_ge(s["w_ready"], 2)
            for g in range(2):
                dve.wait_ge(s["bias_mm"], 2 + g + 1)
                r = slice(8 * g, 8 * g + 8)
                tt(H[:, r, :], bank[4 + g][:].rearrange("p (t d) -> p t d", t=8), H[:, r, :], plus).then_inc(s["base_ready"], 1)
            dve.wait_ge(s["base_ready"], 4)
            for c in range(NC):
                for t in range(CH * c, CH * c + CH):
                    dve.wait_ge(s["x_down"], T + t + 1)
                    tt(ytmp[:, t % 2], bank[4 + t % 2][:].rearrange("p (e d) -> p e d", e=E),
                       wts[:, t, :].unsqueeze(2).broadcast_to([P, E, D]), mul).then_inc(s["y_read"], 1)
                    dve.wait_ge(s["y_read"], T + t + 1)
                    ch(dve.tensor_reduce(YB[1][:, t, :], ytmp[:, t % 2].rearrange("p e d -> p d e"), AX_X, plus))
                ch.settle()
                hc = H[:, CH * c:CH * c + CH, :]
                tt(hc, hc, YB[1][:, CH * c:CH * c + CH, :], plus).then_inc(s["out_done"], 1)


def kernel(**inp):
    import numpy as np
    import concourse.bacc as bacc
    from concourse.bass_utils import run_bass_kernel_spmd as run

    i = {k: np.asarray(v) for k, v in inp.items()}
    flat = np.ravel
    rows = {
        "norm_g": i["L0_tok_norm_g"], "norm_b": i["L0_tok_norm_b"], "b2": i["L0_tok_cms_b2"],
        "b_upd": i["L0_tok_b_upd"], "b_f": i["L0_tok_b_f"], "head_b": i["L0_tok_head_b"],
        "decay": i["L0_tok_decay_param"], "br0": i["L0_ffn_br"],
        "gamma0": i["L0_ffn_gamma"], "beta0": i["L0_ffn_beta"], "bpos": i["L1_attn_bpos"],
        "wpos": i["L1_attn_Wpos"].T, "bproj": i["L1_attn_bproj"], "gating": i["L1_attn_gating"],
        "br1": i["L1_ffn_br"],
    }
    cols = {
        "ln_g": i["L0_tok_cms_ln_g"].T, "ln_b": i["L0_tok_cms_ln_b"].T,
        "b1": i["L0_tok_cms_b1"].reshape(NL * 4, P).T, "eb10": i["L0_ffn_b1"].T, "eb11": i["L1_ffn_b1"].T,
        "aln_g": i["L0_attn_ln_g"][:, None], "aln_b": i["L0_attn_ln_b"][:, None],
        "gamma1": i["L1_ffn_gamma"][:, None], "beta1": i["L1_ffn_beta"][:, None],
    }
    place, n = offsets(COLS)
    colv = np.zeros((P, n), np.float32)
    for k, v in cols.items():
        colv[0:v.shape[0], place[k][0]:place[k][1]] = v
    sw = i["L0_attn_slow_W"].reshape(NH, 5 * DH + 2, D)
    q, k_, v_, rk, rv = (sw[:, DH * j:DH * j + DH].reshape(HB, D) for j in range(5))
    slow = np.concatenate([q, k_, v_, rv, rk, sw[:, 5 * DH], sw[:, 5 * DH + 1]]).T
    arrays = {
        "tok": i["x"].reshape(-1),
        "rows": np.concatenate([flat(rows[k]) for k, _ in ROWS]),
        "cols": colv,
        "emb": i["L0_tok_emb"], "embT": i["L0_tok_emb"].T, "wupd": i["L0_tok_W_upd"], "wf": i["L0_tok_W_f"],
        "w1": i["L0_tok_cms_W1"].transpose(1, 0, 2),
        "w2": i["L0_tok_cms_W2"].reshape(NL, 4, P, DT).transpose(2, 0, 1, 3),
        "headw": i["L0_tok_head_W"],
        "sloww": slow, "outw": i["L0_attn_out_W"].T.reshape(2, P, D).transpose(1, 0, 2),
        "ew1_0": i["L0_ffn_W1"].transpose(1, 0, 2), "ew2_0": i["L0_ffn_W2"].transpose(1, 0, 2), "wr_0": i["L0_ffn_Wr"],
        "ew1_1": i["L1_ffn_W1"].transpose(1, 0, 2), "ew2_1": i["L1_ffn_W2"].transpose(1, 0, 2), "wr_1": i["L1_ffn_Wr"],
        "wq": i["L1_attn_Wqk"][0:D].T, "wk": i["L1_attn_Wqk"][D:].T,
        "eb2_0": np.tile(i["L0_ffn_b2"], (T, 1)), "eb2_1": np.tile(i["L1_ffn_b2"], (T, 1)),
        "wv": i["L1_attn_Wv"].T, "wproj": i["L1_attn_Wproj"].T,
    }
    nc = bacc.Bacc("TRN2", target_bir_lowering=False, num_devices=1)
    feed, aps = {}, {}
    for k, v in arrays.items():
        v = np.ascontiguousarray(v)
        feed[f"in_{k}"] = v
        aps[k] = nc.dram_tensor(f"in_{k}", v.shape, mybir.dt.from_np(v.dtype), kind="ExternalInput").ap()
    out = nc.dram_tensor("out_h", (T, P, D), F32, kind="ExternalOutput").ap()
    aps["out"] = out.rearrange("t p d -> p t d")
    build(nc, aps)
    r = run(nc, [feed], core_ids=[0])
    return r.results[0]["out_h"]
```

```python
from contextlib import ExitStack

import concourse.bass as bass
from concourse import mybir

ALU = mybir.AluOpType
ACT = mybir.ActivationFunctionType
F32 = mybir.dt.float32
I32 = mybir.dt.int32
AX_X = mybir.AxisListType.X

EPS = 1e-5
P = 128

T = 16
DT = 128
NL = 4
VOC = 64
D = 64
NH, DH = 8, 32
HB = NH * DH
E, FF = 8, 128
HD = D // NH
CH = 4
NC = T // CH
NP = 2
TP = T // NP
UP = 2 * NL
N = T * P

ROWS = [("norm_g", DT), ("norm_b", DT), ("b2", NL * DT), ("b_upd", DT), ("b_f", DT), ("head_b", VOC), ("decay", 1),
        ("br0", E), ("gamma0", D), ("beta0", D), ("bpos", NH), ("wpos", 3 * NH), ("bproj", D),
        ("gating", NH), ("br1", E)]
COLS = [("ln_g", NL), ("ln_b", NL), ("b1", NL * 4), ("eb10", E), ("eb11", E),
        ("aln_g", 1), ("aln_b", 1), ("gamma1", 1), ("beta1", 1)]


def offsets(parts):
    at, out = 0, {}
    for name, n in parts:
        out[name] = (at, at + n)
        at += n
    return out, at


class Chain:

    def __init__(self, eng, sem):
        self.eng, self.sem, self.n = eng, sem, 0

    def __call__(self, ins):
        ins.then_inc(self.sem, 1)
        self.n += 1

    def settle(self):
        self.eng.wait_ge(self.sem, self.n)


def pieces(n, step=4):
    return [(r, min(r + step, n)) for r in range(0, n, step)]


def gram_base(t):
    return sum(len(pieces(i)) for i in range(t))


def combos():
    out = []
    for p in range(NP):
        first, end = TP * p, TP * p + TP
        if p:
            out += [("held", first, r0, r1) for r0, r1 in pieces(first, 2)]
        for t in range(first, end):
            out += [("fast", t, r0, r1) for r0, r1 in pieces(t + 1)]
            if t + 1 < end:
                out += [("held", t + 1, r0, r1) for r0, r1 in pieces(t + 1, 2)]
            out += [("rec", t, r0, r1) for r0, r1 in pieces(t + 1)]
    return out


COMBOS = combos()


def combos_of(kind, t):
    return [(i, r0, r1) for i, (k, s, r0, r1) in enumerate(COMBOS) if k == kind and s == t]


def summed(kind, t):
    return combos_of(kind, t)[-1][0] + 1


def unit(w):
    p, v = divmod(w, UP)
    return v // 2, 2 * p + v % 2


def build(nc, a):
    ROW, NROW = offsets(ROWS)
    COL, NCOL = offsets(COLS)
    with ExitStack() as ctx:
        def sb(name, shape, dt=F32):
            return ctx.enter_context(nc.sbuf_tensor(name, shape, dt))

        def sem(name):
            return ctx.enter_context(nc.semaphore(name))

        bank = [ctx.enter_context(nc.psum_tensor(f"bank{i}", [P, 512], F32)) for i in range(8)]

        rows = sb("rows", [P, NROW])
        cols = sb("cols", [P, NCOL])
        ident = sb("ident", [P, P])
        ones = sb("ones", [P, P])
        neghalf = sb("neghalf", [P, T])
        iota_i = sb("iota_i", [P, 1], I32)
        iota_f = sb("iota_f", [P, 1])
        w1 = sb("w1", [DT, NL, 4 * DT])
        w2 = sb("w2", [P, NL, 4, DT])
        headw = sb("headw", [DT, VOC])
        w1f = w1[:].rearrange("p l n -> p (l n)")
        w2f = w2[:].rearrange("p l f n -> p (l f n)")
        ew1 = [w1f[:, 1024 * k:1024 * k + 1024].rearrange("p (e f) -> p e f", e=E) for k in range(2)]
        ew2 = [w2f[:, 512 * k:512 * k + 512].rearrange("p (e d) -> p e d", e=E) for k in range(2)]
        wq, wk, wv, wproj = (w2f[:, 1024 + D * k:1024 + D * k + D] for k in range(4))
        eb2 = [w2f[:, 1280 + D * k:1280 + D * k + D] for k in range(2)]
        sloww = sb("sloww", [P, 5 * HB + 2 * NH])
        outw = sb("outw", [P, 2, D])
        wr = [sb(f"wr_{k}", [P, E]) for k in range(2)]

        def row(name, n=None, parts=P):
            lo, hi = ROW[name]
            return rows[0:parts, lo:hi]

        def col(name, k=0, parts=P):
            lo = COL[name][0]
            return cols[0:parts, lo + k:lo + k + 1]

        H = sb("H", [P, T, D])
        XN = sb("XN", [P, T, D])
        X = sb("X", [P, T, DT])
        stats = sb("stats", [P, 4, CH, 6])
        mv = sb("mv", [P, 4, CH, 2])
        rstd = sb("rstd", [P, 4, CH])
        xT = sb("xT", [P, 2, 512])
        xa = sb("xa", [P, 2, 512])
        G = sb("G", [P, 8, 512])
        decay = sb("decay", [P, 4])

        KKf = sb("keys", [P, 2 * T * HB])
        QF = sb("QF", [P, T, HB])
        RK = sb("RK", [P, T, HB])
        UV = sb("UV", [P, T, 2, HB])
        PB = sb("PB", [P, 4, 4 * HB])
        PC = sb("PC", [P, 8, HB])
        PD = sb("PD", [P, 4, HB])
        CG = sb("CG", [P, 2, T, 2, NH])
        CQ = sb("CQ", [P, 2, T, NH])
        CR = sb("CR", [P, T, NH])
        beta = sb("beta", [P, T, 2, NH])
        er = sb("er", [P, 2, HB])
        dd = sb("dd", [P, 2, HB])
        hs = sb("hs", [P, 2, HB])
        hsT = sb("hsT", [P, 2, HB])
        PBf = PB[:].rearrange("p k n -> p (k n)")
        e1, r1 = (PBf[:, 1024 * k:1024 * k + 1024].rearrange("p (k n) -> p k n", k=2) for k in range(2))
        ker, kdd = (PBf[:, 2048 + 512 * k:2560 + 512 * k].rearrange("p (k n) -> p k n", k=2) for k in range(2))
        smallv = sb("smallv", [P, 8, 32])
        mx = sb("mx", [P, 2, 8])

        KF = KKf[:, 0:4096].rearrange("p (t n) -> p t n", t=T)

        def key_products(n, t, j):
            if t < TP:
                b = KKf[:, 4096 + 2048 * n:6144 + 2048 * n]
            else:
                b = KKf[:, 4096:8192] if n == 0 else G[:].rearrange("p g n -> p (g n)")
            return b[:, 1024 * j:1024 * j + 1024].rearrange("p (r n) -> p r n", r=4)

        tok = KKf[:, 0:N].bitcast(I32)
        onehot = KKf[0:VOC, N:2 * N]
        keep = KKf[:, 2 * N:3 * N]
        memT = KKf[:, 3 * N:4 * N]
        QQf = QF[:].rearrange("p t n -> p (t n)")
        iszero = QQf[:, 0:N]
        RKf = RK[:].rearrange("p t h -> p (t h)")
        emb, utab, embf = (RKf[0:VOC, DT * k:DT * k + DT] for k in range(3))
        embT = RKf[:, 3 * DT:3 * DT + VOC]
        wupd, wf = (RKf[:, DT * k:DT * k + DT] for k in (4, 5))
        UVf = UV[:].rearrange("p t n h -> p (t n h)")
        xn_tok = UVf[:, 4096:5120].rearrange("p (k t d) -> p k t d", k=2, t=CH)
        xb_tok = UVf[:, 5120:7168].rearrange("p (k t d) -> p k t d", k=NC, t=CH)
        xtmp = UVf[:, 0:2048].rearrange("p (t d) -> p t d", t=T)

        G2 = [G[:], KKf[:, 0:4096].rearrange("p (e n) -> p e n", e=E)]
        w2w = KKf[:, 4096:5120].rearrange("p (k e d) -> p k e d", k=2, e=E)
        ytmp = KKf[:, 5120:6144].rearrange("p (k e d) -> p k e d", k=2, e=E)
        b2x = KKf[:, 6144:8192].rearrange("p (k t d) -> p k t d", k=2, t=T)
        qd = UVf[:, 0:4096].rearrange("p (h n) -> p h n", h=NH)
        kaug = UVf[:, 4096:4608]
        kz = QQf[:, 0:512]
        pexp = UVf[:, 4608:6656].rearrange("p (k h n) -> p k h n", k=2, h=NH)
        vaug = UVf[:, 6656:6944].rearrange("p (t h d) -> p t h d", t=CH, h=NH)
        posT = UVf[:, 6944:7968].rearrange("p (h n) -> p h n", h=NH)
        plog = RKf[:, 0:1024].rearrange("p (h m) -> p h m", h=NH)
        rel = RKf[:, 1024:1152]
        rel2 = RKf[:, 1152:1280]
        rel_i = RKf[:, 1280:1408].bitcast(I32)
        nmax = RKf[:, 1408:1408 + 2 * (D + NH)].rearrange("p (k n) -> p k n", k=2)
        att = RKf[:, 1600:1600 + 256].rearrange("p (t d) -> p t d", t=CH)
        att2 = RKf[:, 1856:1856 + 256].rearrange("p (t d) -> p t d", t=CH)
        cmp1 = RKf[:, 2112:3136]
        cmp2 = PD[:].rearrange("p r n -> p (r n)")
        wts, rout, rsel = (RKf[:, 3136 + P * k:3136 + P * k + P].rearrange("p (t e) -> p t e", t=T) for k in range(3))
        wtsT = RKf[:, 3520:3648]
        rsm = RKf[:, 3648:3712].rearrange("p (k t) -> p k t", k=4)
        meanT = RKf[0:D, 3712:3728]
        YB = [X[:].rearrange("p t d -> p (t d)")[:, 1024 * k:1024 * k + 1024].rearrange("p (t d) -> p t d", t=T)
              for k in range(2)]
        m16 = sb("m16", [P, T])
        lower = sb("lower", [P, E, E])
        gate = sb("gate", [P, 4, NH])
        comb = sb("comb", [P, 6, CH * NH])

        s = {n: sem(n) for n in """
            load_tok load_rows load_emb load_mlp load_attn load_experts stored
            consts dve_chain act_chain pool_chain
            ln_var ln_rstd decay_exp utab_mm tables_ready u_mm mem_ready x_mm norm_scaled norm_done
            xb_ready tok_norm tok_T tok_hT tok_up tok_gelu tok_down tok_add
            head_T head_xT head_mm head_add
            a_norm a_hx a_T a_oT a_qkv a_acts a_sub a_rexp a_elu a_keys pad
            gram_p gram_read query_done upd_p upd_mm acc_done h_exp e_sub hs_saved
            o_T o_evict o_mm o_add
            masks b2x_ready x_norm mean_mm mean_ready logit_mm r_sub r_exp r_prob load_mm r_spread
            spread_mm w_ready wT_mm wT_ready bias_mm base_ready w2w_ready x_T x_xT x_up x_gelu x_down y_read
            y_ready f1_norm f_affine
            p_rel p_sub p_exp p_done p_T p_evict gate_exp
            d_norm d_T d_xT d_q d_qd d_k d_kcopy d_v d_vcopy s_mm s_max nm_T aug_ready st_mm p_ready av_mm pos_mm
            comb_done at_T at_xT proj_mm d_add hb_ready
            e_norm e_xT rl_mm rl_read rl_exp out_done
            """.split()}

        block = ctx.enter_context(nc.Block())

        LN = []
        for p in range(NP):
            if p == 0:
                LN += [("norm", 0), ("norm", 1), ("tok", 0)]
                for v in range(UP):
                    LN += [("tok", v + 1)] if v + 1 < UP else []
                    LN += [("norm", 2)] if v == 1 else [("norm", 3)] if v == 3 else []
                LN += [("tok", UP)]
            for c in (2 * p, 2 * p + 1):
                LN += [("a1", c), ("a2", c)]
            if p == 0:
                LN += [("tok", UP + v + 1) for v in range(UP - 1)]
        for k in ("f0", "f1", "d"):
            LN += [(k, c) for c in range(NC)]
        for c in range(NC):
            LN += [("e1", c), ("e2", c)]
        LNI = {k: i for i, k in enumerate(LN)}

        def up_bank(w, f):
            return bank[(1, 2, 4, 5)[f] if w > UP else 1 + f % 2]

        def qd_rows(j):
            return qd[D:D + NH, :, P * j:P * j + P]

        def xin(k, c):
            return xa[:, c % 2, :] if k == 0 else UVf[:, 512 * c:512 * c + 512]

        def rstd_pool(pool, ch, key, n):
            i = LNI[key]
            k = i % 4
            pool.wait_ge(s["ln_var"], i + 1)
            ch(pool.tensor_scalar(rstd[:, k, 0:n], mv[:, k, 0:n, 1], EPS, None, ALU.add))
            ch.settle()
            pool.tensor_tensor(rstd[:, k, 0:n], rstd[:, k, 0:n], neghalf[:, 0:n], ALU.pow).then_inc(s["ln_rstd"], 1)

        def norm_stats(dve, ch, key, tiles):
            i = LNI[key]
            k = i % 4
            for j, x in enumerate(tiles):
                ch(dve.bn_stats(stats[:, k, j, :], x))
            ch.settle()
            for j in range(len(tiles)):
                last = dve.bn_aggr(mv[:, k, j, :], stats[:, k, j, :])
                if j < len(tiles) - 1:
                    ch(last)
            last.then_inc(s["ln_var"], 1)

        def norm_apply(dve, key, tiles, outs):
            i = LNI[key]
            k = i % 4
            dve.wait_ge(s["ln_var"], i + 1)
            dve.wait_ge(s["ln_rstd"], i + 1)
            for j, (x, o) in enumerate(zip(tiles, outs)):
                last = dve.tensor_scalar(o, x, mv[:, k, j, 0:1], rstd[:, k, j:j + 1], ALU.subtract, ALU.mult)
            return last

        @block.sync
        def _(sp):
            sp.dma_start(tok, a["tok"].partition_broadcast(P)).then_inc(s["load_tok"], 16)
            sp.dma_start(rows[:], a["rows"].partition_broadcast(P)).then_inc(s["load_rows"], 16)
            sp.dma_start(cols[:], a["cols"]).then_inc(s["load_rows"], 16)
            for t, n in ((emb, "emb"), (embT, "embT"), (wupd, "wupd"), (wf, "wf")):
                sp.dma_start(t[:], a[n]).then_inc(s["load_emb"], 16)
            for t, n in ((w1, "w1"), (w2, "w2"), (headw, "headw")):
                sp.dma_start(t[:], a[n]).then_inc(s["load_mlp"], 16)
            sp.dma_start(sloww[0:D], a["sloww"]).then_inc(s["load_attn"], 16)
            sp.dma_start(outw[:], a["outw"]).then_inc(s["load_attn"], 16)
            for k in range(2):
                sp.dma_start(wr[k][0:D], a[f"wr_{k}"]).then_inc(s["load_experts"], 16)
            sp.wait_ge(s["tok_down"], 2 * UP)
            for k in range(2):
                for t, n in ((ew1[k][0:D], "ew1"), (ew2[k][:], "ew2"), (eb2[k][:], "eb2")):
                    sp.dma_start(t, a[f"{n}_{k}"]).then_inc(s["load_experts"], 16)
            for t, n in ((wq, "wq"), (wk, "wk"), (wv, "wv"), (wproj, "wproj")):
                sp.dma_start(t[0:D], a[n]).then_inc(s["load_experts"], 16)
            for c in range(NC):
                sp.wait_ge(s["out_done"], c + 1)
                sp.dma_start(a["out"][:, CH * c:CH * c + CH, :], H[:, CH * c:CH * c + CH, :]).then_inc(s["stored"], 16)
            sp.wait_ge(s["stored"], 16 * NC)

        @block.gpsimd
        def _(pool):
            ch = Chain(pool, s["pool_chain"])
            ch(pool.memset(ident[:], 0.0))
            ch(pool.memset(ones[:], 1.0))
            ch(pool.memset(neghalf[:], -0.5))
            ch(pool.iota(iota_i[:], pattern=[[0, 1]], base=0, channel_multiplier=1))
            ch.settle()
            ch(pool.affine_select(out=ident[:], in_=ident[:], compare_op=ALU.not_equal, fill=1.0, base=0,
                                  pattern=[[-1, P]], channel_multiplier=1))
            ch.settle()
            pool.tensor_copy(iota_f[:], iota_i[:]).then_inc(s["consts"], 1)
            ch(pool.memset(m16[:], 1.0))
            ch(pool.memset(lower[:], 1.0))
            ch.settle()
            ch(pool.affine_select(out=m16[:], in_=m16[:], compare_op=ALU.is_ge, fill=0.0, base=0,
                                  pattern=[[-E, T]], channel_multiplier=1))
            ch.settle()
            pool.affine_select(out=m16[:], in_=m16[:], compare_op=ALU.is_ge, fill=0.0, base=E - 1,
                               pattern=[[E, T]], channel_multiplier=-1).then_inc(s["masks"], 1)
            pool.affine_select(out=lower[:], in_=lower[:], compare_op=ALU.is_ge, fill=0.0, base=-1,
                               pattern=[[1, E], [-1, E]], channel_multiplier=0).then_inc(s["masks"], 1)
            pool.wait_ge(s["masks"], 2)
            for w in (xa, *wr):
                ch(pool.memset(w[D:P], 0.0))
            pool.memset(sloww[D:P], 0.0).then_inc(s["pad"], 1)
            pool.wait_ge(s["pad"], 1)
            ch.settle()
            pool.wait_ge(s["load_rows"], 32)
            b2 = row("b2").rearrange("p (l d) -> p l d", l=NL)

            def affine(c):
                rstd_pool(pool, ch, ("norm", c), CH)
                xc = X[:, CH * c:CH * c + CH, :]
                pool.wait_ge(s["norm_scaled"], c + 1)
                g = row("norm_g").unsqueeze(1).broadcast_to([P, CH, DT])
                b = row("norm_b").unsqueeze(1).broadcast_to([P, CH, DT])
                ch(pool.tensor_tensor(xc, xtmp[:, CH * c:CH * c + CH, :], g, ALU.mult))
                ch.settle()
                pool.tensor_tensor(xc, xc, b, ALU.add).then_inc(s["norm_done"], 1)

            def prepare(w):
                i, c = unit(w)
                rstd_pool(pool, ch, ("tok", w), CH)
                if w % UP < 2:
                    pool.wait_ge(s["norm_done"], c + 1)
                else:
                    pool.wait_ge(s["tok_add"], w - 1)
                pool.tensor_tensor(xb_tok[:, c], X[:, CH * c:CH * c + CH, :],
                                   b2[:, i, :].unsqueeze(1).broadcast_to([P, CH, DT]), ALU.add).then_inc(s["xb_ready"], 1)

            def keys(t):
                k = t % 2
                hd = "p (h j) -> p h j"
                pool.wait_ge(s["a_elu"], t + 1)
                for dst, o in ((QF[:, t, :], 0), (KF[:, t, :], HB)):
                    ch(pool.tensor_tensor(dst.rearrange(hd, j=DH), e1[:, k, o:o + HB].rearrange(hd, j=DH),
                                          smallv[:, k, o // DH:o // DH + NH].unsqueeze(2).broadcast_to([P, NH, DH]), ALU.mult))
                pool.tensor_tensor(RK[:, t, :].rearrange(hd, j=DH), ker[:, k, :].rearrange(hd, j=DH),
                                   smallv[:, k, 16:24].unsqueeze(2).broadcast_to([P, NH, DH]),
                                   ALU.mult).then_inc(s["a_keys"], 1)

            def products(t):
                for j, (r0, r1_) in enumerate(pieces(t)):
                    R = r1_ - r0
                    for n, keys_ in enumerate((KF, RK)):
                        if t == TP:
                            pool.wait_ge(s["gram_read"], 2 * gram_base(TP))
                        elif t >= 2 and j < len(pieces(t - 1)):
                            pool.wait_ge(s["gram_read"], 2 * (gram_base(t - 1) + j) + n + 1)
                        pool.tensor_tensor(key_products(n, t, j)[:, 0:R, :], keys_[:, r0:r1_, :],
                                           keys_[:, t, :].unsqueeze(1).broadcast_to([P, R, HB]),
                                           ALU.mult).then_inc(s["gram_p"], 1)
                if t >= 2:
                    pool.wait_ge(s["upd_p"], summed("fast", t - 2))
                if t:
                    pool.wait_ge(s["query_done"], t)
                for r0, r1_ in pieces(t + 1, 8):
                    R = r1_ - r0
                    ch(pool.tensor_tensor(PC[:, 0:R, :], KF[:, r0:r1_, :],
                                          QF[:, t, :].unsqueeze(1).broadcast_to([P, R, HB]), ALU.mult))
                    ch.settle()
                    pv = PC[:, 0:R, :].rearrange("p r (h j) -> p (r h) j", h=NH)
                    for m in (16, 8, 4, 2):
                        ch(pool.tensor_tensor(pv[:, :, 0:m], pv[:, :, 0:m], pv[:, :, m:2 * m], ALU.add))
                        ch.settle()
                    last = pool.tensor_tensor(CQ[:, t % 2, r0:r1_, :].rearrange("p r h -> p (r h)"), pv[:, :, 0], pv[:, :, 1],
                                              ALU.add)
                    if r1_ < t + 1:
                        ch(last)
                        ch.settle()
                last.then_inc(s["query_done"], 1)

            affine(0)
            affine(1)
            prepare(0)
            for v in range(UP):
                if v + 1 < UP:
                    prepare(v + 1)
                if v in (1, 3):
                    affine(2 + v // 2)
            prepare(UP)
            for p in range(NP):
                for c in (2 * p, 2 * p + 1):
                    rstd_pool(pool, ch, ("a1", c), CH)
                    rstd_pool(pool, ch, ("a2", c), CH)
                    hc = H[:, CH * c:CH * c + CH, :]
                    pool.wait_ge(s["a_norm"], c + 1)
                    pool.tensor_tensor(hc, hc, XN[:, CH * c:CH * c + CH, :], ALU.add).then_inc(s["a_hx"], 1)
                for t in range(TP * p, TP * p + TP):
                    keys(t)
                if p:
                    pool.wait_ge(s["tok_down"], 2 * UP)
                    pool.wait_ge(s["a_keys"], 2 * TP)
                    ch(pool.memset(w2f[D:P, 1024:1280], 0.0))
                    ch.settle()
                    pool.memset(w1f[D:P, 0:2048], 0.0).then_inc(s["pad"], 1)
                    pool.wait_ge(s["pad"], 2)
                    products(TP)
                    products(TP + 1)
                else:
                    pool.wait_ge(s["a_keys"], TP)
                    ch.settle()
                    products(0)
                    products(1)
                for t in range(TP * p, TP * p + TP):
                    if p == 0 and t + 1 < UP:
                        prepare(UP + t + 1)
                    if t + 2 < TP * p + TP:
                        products(t + 2)

            pool.wait_ge(s["load_experts"], 16 * 12)
            pool.wait_ge(s["masks"], 2)
            for c in range(NC):
                rstd_pool(pool, ch, ("f0", c), CH)
            pool.wait_ge(s["x_norm"], 1)
            for k in range(2):
                pool.tensor_tensor(b2x[:, k], eb2[k][:].unsqueeze(1).broadcast_to([P, T, D]),
                                   m16[:].unsqueeze(2).broadcast_to([P, T, D]), ALU.mult).then_inc(s["b2x_ready"], 1)
            pool.wait_ge(s["b2x_ready"], 2)
            ch(pool.memset(qd[D:P], 0.0))
            ch(pool.memset(kz[D:P], 0.0))
            ch(pool.memset(kaug[D:P], 0.0))
            ch.settle()
            pool.memset(kaug[D:D + NH, :], 1.0).then_inc(s["pad"], 1)
            pool.wait_ge(s["pad"], 3)
            ch(pool.iota(rel_i, pattern=[[1, P]], base=0, channel_multiplier=-1))
            ch.settle()
            ch(pool.tensor_copy(rel, rel_i))
            ch.settle()
            pool.tensor_tensor(rel2, rel, rel, ALU.mult).then_inc(s["p_rel"], 1)
            pool.wait_ge(s["w_ready"], 1)
            for c in range(NC):
                for t in range(CH * c, CH * c + CH):
                    if t >= 2:
                        pool.wait_ge(s["x_down"], t - 1)
                    pool.tensor_tensor(w2w[:, t % 2], ew2[0][:], wts[:, t].unsqueeze(2).broadcast_to([P, E, D]),
                                       ALU.mult).then_inc(s["w2w_ready"], 1)
                rstd_pool(pool, ch, ("f1", c), CH)
                r = slice(CH * c, CH * c + CH)
                pool.wait_ge(s["f1_norm"], c + 1)
                yb = YB[1][:, r, :]
                ch(pool.tensor_tensor(yb, yb, row("gamma0").unsqueeze(1).broadcast_to([P, CH, D]), ALU.mult))
                ch.settle()
                ch(pool.tensor_tensor(yb, yb, row("beta0").unsqueeze(1).broadcast_to([P, CH, D]), ALU.add))
                ch.settle()
                pool.tensor_tensor(H[:, r, :], H[:, r, :], yb, ALU.add).then_inc(s["f_affine"], 1)
            for c in range(NC):
                rstd_pool(pool, ch, ("d", c), CH)
                r = slice(CH * c, CH * c + CH)
                pool.wait_ge(s["f_affine"], NC)
                pool.wait_ge(s["d_norm"], c + 1)
                pool.tensor_tensor(H[:, r, :], H[:, r, :], row("bproj").unsqueeze(1).broadcast_to([P, CH, D]),
                                   ALU.add).then_inc(s["hb_ready"], 1)
            for c in range(NC):
                rstd_pool(pool, ch, ("e1", c), CH)
                rstd_pool(pool, ch, ("e2", c), CH)

        @block.scalar
        def _(act):
            ch = Chain(act, s["act_chain"])
            act.wait_ge(s["load_rows"], 32)
            act.activation(decay[:, 0:1], row("decay"), ACT.Exp, scale=-1.0).then_inc(s["decay_exp"], 1)

            def evict_T(w):
                i, c = unit(w)
                act.wait_ge(s["tok_T"], w + 1)
                if w >= 2:
                    act.wait_ge(s["tok_up"], 4 * (w - 1))
                if w == UP + 1:
                    act.wait_ge(s["head_mm"], 2)
                act.activation(xT[:, w % 2, :], bank[0][:], ACT.Identity, bias=col("ln_b", i),
                               scale=col("ln_g", i)).then_inc(s["tok_hT"], 1)

            def gelus(w):
                i, c = unit(w)
                for f in range(4):
                    act.wait_ge(s["tok_up"], 4 * w + f + 1)
                    if w >= 2 and f == 0:
                        act.wait_ge(s["tok_down"], w - 1)
                    act.activation(G[:, 4 * (w % 2) + f, :], up_bank(w, f)[:], ACT.Gelu,
                                   bias=col("b1", 4 * i + f)).then_inc(s["tok_gelu"], 1)

            def head(p):
                for c in (2 * p, 2 * p + 1):
                    act.wait_ge(s["head_T"], c + 1)
                    if c % 2:
                        act.wait_ge(s["head_mm"], c)
                    act.activation(xT[:, 1, :], bank[0][:], ACT.Copy).then_inc(s["head_xT"], 1)

            def qkv_bank(t, j):
                return bank[(4, 5, 6)[j] if t % 2 == 0 else (1, 2, 3)[j]]

            def tile_acts(t):
                k = t % 2
                act.wait_ge(s["a_qkv"], t + 1)
                if t >= 2:
                    act.wait_ge(s["a_keys"], t - 1)
                if t == TP:
                    act.wait_ge(s["upd_mm"], summed("rec", TP - 1))
                act.activation(e1[:, k, :], qkv_bank(t, 0)[:], ACT.Exp)
                act.activation(r1[:, k, :], qkv_bank(t, 0)[:], ACT.Relu)
                act.activation(UV[:, t].rearrange("p n h -> p (n h)"), qkv_bank(t, 1)[:], ACT.Copy).then_inc(s["a_acts"], 1)
                act.wait_ge(s["a_sub"], t + 1)
                act.activation(ker[:, k, :], kdd[:, k, :], ACT.Exp)
                bt = beta[:, t].rearrange("p n h -> p (n h)")
                act.activation(bt, bt, ACT.Exp, scale=-1.0).then_inc(s["a_rexp"], 1)

            def project(p):
                for c in (2 * p, 2 * p + 1):
                    act.wait_ge(s["a_T"], c + 1)
                    act.activation(xa[0:D, c % 2, :], bank[0][0:D, :], ACT.Identity, bias=col("aln_b", parts=D),
                                   scale=col("aln_g", parts=D)).then_inc(s["a_oT"], 1)
                for t in range(TP * p, TP * p + TP):
                    tile_acts(t)

            def state(t):
                act.wait_ge(s["upd_mm"], summed("rec", t))
                if t >= 2:
                    act.wait_ge(s["o_T"], t - 1)
                if t + 1 < T:
                    act.wait_ge(s["e_sub"], t + 1)
                act.activation(hs[:, t % 2, :], bank[7][:, 0:HB], ACT.Copy).then_inc(s["hs_saved"], 1)
                if t + 1 < T:
                    act.activation(er[:, (t + 1) % 2, :], dd[:, (t + 1) % 2, :], ACT.Exp).then_inc(s["h_exp"], 1)

            def state_T(t):
                act.wait_ge(s["o_T"], t + 1)
                if t >= 2:
                    act.wait_ge(s["o_mm"], t - 1)
                act.activation(hsT[:, t % 2, :], bank[0][:, 0:HB], ACT.Copy).then_inc(s["o_evict"], 1)

            evict_T(0)
            gelus(0)
            for v in range(UP - 1):
                evict_T(v + 1)
                gelus(v + 1)
            evict_T(UP)
            gelus(UP)
            for p in range(NP):
                head(p)
                project(p)
                for t in range(TP * p, TP * p + TP):
                    if t % TP:
                        state(t - 1)
                    if p == 0 and t:
                        gelus(UP + t)
                    if p == 0 and t + 1 < UP:
                        evict_T(UP + t + 1)
                    if t:
                        state_T(t - 1)
                state(TP * p + TP - 1)
            state_T(T - 1)

            def experts(k, c):
                x = NC * k + c
                act.wait_ge(s["x_T"], x + 1)
                if k == 0 and c >= 2:
                    act.wait_ge(s["x_up"], E * (c - 1))
                dst, src = xin(k, c)[0:D], bank[x % 2][0:D, :]
                if k == 0:
                    act.activation(dst, src, ACT.Copy).then_inc(s["x_xT"], 1)
                else:
                    act.activation(dst, src, ACT.Identity, bias=col("beta1", parts=D),
                                   scale=col("gamma1", parts=D)).then_inc(s["x_xT"], 1)

            def expert_gelus(k, c):
                x = NC * k + c
                for e in range(E):
                    act.wait_ge(s["x_up"], E * x + e + 1)
                    if e == 0 and x >= 2:
                        act.wait_ge(s["x_down"], CH * (x - 1))
                    act.activation(G2[x % 2][:, e, :], bank[2 + e % 2][:], ACT.Gelu,
                                   bias=col(f"eb1{k}", e)).then_inc(s["x_gelu"], 1)

            act.wait_ge(s["mean_mm"], 1)
            act.activation(meanT[:], bank[7][0:D, 0:T], ACT.Copy, scale=1.0 / P).then_inc(s["mean_ready"], 1)
            for j in range(3):
                act.wait_ge(s["r_sub"], j + 1)
                act.activation(rsel[0:T, j, :], rsel[0:T, j, :], ACT.Exp).then_inc(s["r_exp"], 1)
            act.wait_ge(s["p_sub"], 1)
            act.activation(plog, plog, ACT.Exp).then_inc(s["p_exp"], 1)
            act.activation(gate[:, 0, :], row("gating"), ACT.Exp, scale=-1.0).then_inc(s["gate_exp"], 1)
            act.wait_ge(s["wT_mm"], 1)
            act.activation(wtsT[:], bank[7][:, 256:384], ACT.Copy).then_inc(s["wT_ready"], 1)
            for g in range(2):
                act.wait_ge(s["p_T"], g + 1)
                act.activation(posT[:, 4 * g:4 * g + 4, :].rearrange("p h n -> p (h n)"), bank[g][:],
                               ACT.Copy).then_inc(s["p_evict"], 1)
            for c in range(NC):
                experts(0, c)
                expert_gelus(0, c)

            for c in range(NC):
                act.wait_ge(s["d_T"], c + 1)
                act.activation(xa[0:D, 0, :], bank[0][0:D, :], ACT.Copy).then_inc(s["d_xT"], 1)
                act.wait_ge(s["d_q"], c + 1)
                if c:
                    act.wait_ge(s["st_mm"], 2 * CH * c)
                for h in range(NH):
                    act.activation(qd[0:D, h, :], bank[1][0:D, :], ACT.Copy,
                                   scale=m16[0:D, h:h + 1]).then_inc(s["d_qd"], 1)
                act.wait_ge(s["d_k"], c + 1)
                ch(act.activation(kaug[0:D, :], bank[2][0:D, :], ACT.Copy))
                act.activation(kz[0:D, :], bank[2][0:D, :], ACT.Copy).then_inc(s["d_kcopy"], 1)
                act.wait_ge(s["d_v"], c + 1)
                if c:
                    act.wait_ge(s["av_mm"], CH * c)
                    act.wait_ge(s["pos_mm"], c)
                act.activation(vaug[:, :, :, 0:HD], bank[3][:, 0:CH * D].rearrange("p (t h d) -> p t h d", t=CH, h=NH),
                               ACT.Copy).then_inc(s["d_vcopy"], 1)
                for j in range(CH):
                    t = CH * c + j
                    for g in range(2):
                        act.wait_ge(s["st_mm"], 2 * t + g + 1)
                        if t >= 2:
                            act.wait_ge(s["av_mm"], t - 1)
                        act.activation(pexp[:, t % 2, 4 * g:4 * g + 4, :].rearrange("p h n -> p (h n)"), bank[4 + g][:],
                                       ACT.Exp, scale=float(HD) ** -0.5).then_inc(s["p_ready"], 1)
                act.wait_ge(s["at_T"], c + 1)
                act.activation(xa[0:D, 1, :], bank[0][0:D, :], ACT.Copy).then_inc(s["at_xT"], 1)

            for c in range(NC):
                experts(1, c)
            act.wait_ge(s["rl_read"], 1)
            act.activation(rsel[:], rsel[:], ACT.Exp).then_inc(s["rl_exp"], 1)
            act.wait_ge(s["wT_mm"], 2)
            act.activation(wtsT[:], bank[7][:, 256:384], ACT.Copy).then_inc(s["wT_ready"], 1)
            for c in range(NC):
                expert_gelus(1, c)

        @block.tensor
        def _(pe):
            mm = nc.tensor.matmul
            pe.wait_ge(s["load_emb"], 64)
            mm(bank[0][0:VOC, 0:DT], embT[:], wupd[:], start=True, stop=True).then_inc(s["utab_mm"], 1)
            pe.wait_ge(s["tables_ready"], 1)

            def embed(c):
                if c >= 2:
                    pe.wait_ge(s["norm_scaled"], c - 1)
                mm(bank[4 + c % 2][:], utab[:], onehot[:, 512 * c:512 * c + 512],
                   start=True, stop=True).then_inc(s["u_mm"], 1)
                pe.wait_ge(s["mem_ready"], c + 1)
                if c == 0:
                    pe.wait_ge(s["tables_ready"], 2)
                for j in range(CH):
                    t = CH * c + j
                    o = bank[6 + c % 2][:, DT * j:DT * j + DT]
                    mm(o, onehot[:, P * t:P * t + P], embf[:], start=True, stop=False)
                    last = mm(o, memT[:, P * t:P * t + P], wf[:], start=False, stop=True)
                last.then_inc(s["x_mm"], 1)

            def turn(w):
                pe.wait_ge(s["tok_norm"], w + 1)
                if w:
                    pe.wait_ge(s["tok_hT"], w)
                for j in range(CH):
                    last = nc.tensor.transpose(bank[0][:, P * j:P * j + P], xn_tok[:, w % 2, j, :], ident[:])
                last.then_inc(s["tok_T"], 1)

            def up(w):
                i, c = unit(w)
                pe.wait_ge(s["tok_hT"], w + 1)
                for f in range(4):
                    if 4 * w + f >= 2:
                        pe.wait_ge(s["tok_gelu"], 4 * (w - 1) + f + 1 if w > UP else 4 * w + f - 1)
                    mm(up_bank(w, f)[:], w1[:, i, P * f:P * f + P], xT[:, w % 2, :],
                       start=True, stop=True).then_inc(s["tok_up"], 1)

            def down(w):
                i, c = unit(w)
                pe.wait_ge(s["tok_gelu"], 4 * w + 4)
                if w:
                    pe.wait_ge(s["tok_add"], w)
                for j in range(CH):
                    for f in range(4):
                        last = mm(bank[3][:, DT * j:DT * j + DT], G[:, 4 * (w % 2) + f, P * j:P * j + P],
                                  w2[:, i, f, :], start=(f == 0), stop=(f == 3))
                last.then_inc(s["tok_down"], 1)

            def head(p):
                pe.wait_ge(s["tok_add"], UP * (p + 1))
                pe.wait_ge(s["tok_hT"], UP + 1 if p == 0 else 2 * UP)
                if p:
                    pe.wait_ge(s["o_evict"], TP - 1)
                    pe.wait_ge(s["o_add"], TP - 1)
                for c in (2 * p, 2 * p + 1):
                    if c % 2:
                        pe.wait_ge(s["head_xT"], c)
                    for j in range(CH):
                        last = nc.tensor.transpose(bank[0][:, P * j:P * j + P], X[:, CH * c + j, :], ident[:])
                    last.then_inc(s["head_T"], 1)
                    pe.wait_ge(s["head_xT"], c + 1)
                    if c % 2:
                        pe.wait_ge(s["head_add"], c)
                    for j in range(CH):
                        last = mm(bank[3][:, VOC * j:VOC * j + VOC], xT[:, 1, P * j:P * j + P], headw[:],
                                  start=True, stop=True)
                    last.then_inc(s["head_mm"], 1)

            def project(p):
                if p == 0:
                    pe.wait_ge(s["load_attn"], 32)
                    pe.wait_ge(s["pad"], 1)
                pe.wait_ge(s["head_xT"], 2 * p + 2)
                pe.wait_ge(s["head_add"], 2 * p + 2)
                pe.wait_ge(s["tok_gelu"], 4 * (UP + 1) if p == 0 else 8 * UP)
                pe.wait_ge(s["x_mm"], NC)
                pe.wait_ge(s["norm_scaled"], NC)
                if p:
                    pe.wait_ge(s["acc_done"], TP)
                for c in (2 * p, 2 * p + 1):
                    pe.wait_ge(s["a_norm"], c + 1)
                    if c:
                        pe.wait_ge(s["a_oT"], c)
                    for j in range(CH):
                        last = nc.tensor.transpose(bank[0][0:D, P * j:P * j + P], X[:, CH * c + j, 0:D], ident[:])
                    last.then_inc(s["a_T"], 1)
                for t in range(TP * p, TP * p + TP):
                    if t % CH == 0:
                        pe.wait_ge(s["a_oT"], t // CH + 1)
                    if t % TP >= 2:
                        pe.wait_ge(s["a_acts"], t - 1)
                        pe.wait_ge(s["a_sub"], t - 1)
                    o = xa[:, t // CH % 2, P * (t % CH):P * (t % CH) + P]
                    mm(qkv_bank(t, 0)[:], o, sloww[:, 0:512], start=True, stop=True)
                    mm(qkv_bank(t, 1)[:], o, sloww[:, 512:1024], start=True, stop=True)
                    mm(qkv_bank(t, 2)[:, 0:HB + 16], o, sloww[:, 1024:], start=True, stop=True).then_inc(s["a_qkv"], 1)

            def qkv_bank(t, j):
                return bank[(4, 5, 6)[j] if t % 2 == 0 else (1, 2, 3)[j]]

            def held(t):
                for i, r0, r1_ in combos_of("held", t):
                    pe.wait_ge(s["upd_p"], i + 1)
                    if r0 == 0 and t > 1:
                        pe.wait_ge(s["acc_done"], t)
                    for r in range(r0, r1_):
                        last = mm(bank[6][:], ident[:], PB[:, i % 4, 512 * (r - r0):512 * (r - r0) + 512],
                                  start=(r == 0), stop=(r == t - 1))
                    last.then_inc(s["upd_mm"], 1)

            def read_out(kind, t):
                for i, r0, r1_ in combos_of(kind, t):
                    pe.wait_ge(s["upd_p"], i + 1)
                    if kind == "fast" and r0 == 0 and t > 0:
                        pe.wait_ge(s["hs_saved"], t)
                        pe.wait_ge(s["e_sub"], t)
                    for r in range(r0, r1_):
                        last = mm(bank[7][:, 0:HB], ident[:], PB[:, i % 4, HB * (r - r0):HB * (r - r0) + HB],
                                  start=(kind == "fast" and r == 0), stop=(kind == "rec" and r == t))
                    last.then_inc(s["upd_mm"], 1)

            def state_T(t):
                pe.wait_ge(s["hs_saved"], t + 1)
                pe.wait_ge(s["tok_hT"], min(UP + t + 3, 2 * UP))
                if t:
                    pe.wait_ge(s["o_evict"], t)
                for n in range(2):
                    last = nc.tensor.transpose(bank[0][:, P * n:P * n + P], hs[:, t % 2, P * n:P * n + P], ident[:])
                last.then_inc(s["o_T"], 1)

            def out_projection(t):
                pe.wait_ge(s["o_evict"], t + 1)
                pe.wait_ge(s["tok_add"], min(UP + t + 2, 2 * UP))
                if t:
                    pe.wait_ge(s["o_add"], t)
                for n in range(2):
                    last = mm(bank[3][:, 0:D], hsT[:, t % 2, P * n:P * n + P], outw[:, n, :], start=(n == 0), stop=(n == 1))
                last.then_inc(s["o_mm"], 1)

            pe.wait_ge(s["consts"], 1)
            embed(0)
            embed(1)
            pe.wait_ge(s["load_mlp"], 48)
            turn(0)
            up(0)
            for v in range(UP):
                if v + 1 < UP:
                    turn(v + 1)
                if v in (1, 3):
                    embed(2 + v // 2)
                down(v)
                if v + 1 < UP:
                    up(v + 1)
            turn(UP)
            up(UP)
            for p in range(NP):
                head(p)
                project(p)
                pe.wait_ge(s["a_acts"], TP * (p + 1))
                pe.wait_ge(s["a_sub"], TP * (p + 1))
                if p:
                    held(TP)
                for t in range(TP * p, TP * p + TP):
                    w = UP + t
                    read_out("fast", t)
                    if p == 0 and w + 1 < 2 * UP:
                        if t >= 2:
                            pe.wait_ge(s["o_evict"], t - 1)
                        turn(w + 1)
                    if (t + 1) % TP:
                        held(t + 1)
                    if p == 0:
                        if t >= 2:
                            pe.wait_ge(s["o_add"], t - 1)
                        down(w)
                    if t:
                        state_T(t - 1)
                    read_out("rec", t)
                    if p == 0 and w + 1 < 2 * UP:
                        up(w + 1)
                    if t:
                        out_projection(t - 1)
            state_T(T - 1)
            out_projection(T - 1)

            tr = nc.tensor.transpose

            def turn_x(k, c):
                x = NC * k + c
                if x >= 2:
                    pe.wait_ge(s["x_xT"], x - 1)
                src = XN if k == 0 else YB[0]
                for j in range(CH):
                    last = tr(bank[x % 2][0:D, P * j:P * j + P], src[:, CH * c + j, :], ident[:])
                last.then_inc(s["x_T"], 1)

            def expert_up(k, c):
                x = NC * k + c
                pe.wait_ge(s["x_xT"], x + 1)
                for e in range(E):
                    i = E * x + e
                    if i >= 2:
                        pe.wait_ge(s["x_gelu"], i - 1)
                    mm(bank[2 + e % 2][:], ew1[k][:, e, :], xin(k, c),
                       start=True, stop=True).then_inc(s["x_up"], 1)

            def expert_down(k, c):
                x = NC * k + c
                pe.wait_ge(s["x_gelu"], E * x + E)
                for j in range(CH):
                    t = CH * c + j
                    i = T * k + t
                    if i >= 2:
                        pe.wait_ge(s["y_read"], i - 1)
                    if k == 0:
                        pe.wait_ge(s["w2w_ready"], t + 1)
                    for e in range(E):
                        g = G2[x % 2][:, e, P * j:P * j + P]
                        if k == 0:
                            last = mm(bank[4 + t % 2][:, 0:D], g, w2w[:, t % 2, e, :], start=(e == 0), stop=(e == E - 1))
                        else:
                            last = mm(bank[4 + t % 2][:, D * e:D * e + D], g, ew2[1][:, e, :], start=True, stop=True)
                    last.then_inc(s["x_down"], 1)

            def bias(k):
                tr(bank[7][:, 256:384], wts[:].rearrange("p t e -> p (t e)"), ident[:]).then_inc(s["wT_mm"], 1)
                pe.wait_ge(s["wT_ready"], k + 1)
                for g in range(2):
                    mm(bank[4 + g][:], wtsT[:], b2x[:, k, 8 * g:8 * g + 8, :].rearrange("p t d -> p (t d)"),
                       start=True, stop=True).then_inc(s["bias_mm"], 1)

            pe.wait_ge(s["load_experts"], 16 * 12)
            pe.wait_ge(s["pad"], 2)
            pe.wait_ge(s["x_norm"], NC)
            for t in range(T):
                last = mm(bank[7][0:D, t:t + 1], XN[:, t, :], ones[:, 0:1], start=True, stop=True)
            last.then_inc(s["mean_mm"], 1)
            pe.wait_ge(s["mean_ready"], 1)
            mm(bank[7][0:T, 64:64 + E], meanT[:], wr[0][0:D], start=True, stop=True).then_inc(s["logit_mm"], 1)
            pe.wait_ge(s["r_prob"], 1)
            mm(bank[7][0:T, 96:96 + E], ones[0:T, 0:T], rout[0:T, 0, :], start=True, stop=True).then_inc(s["load_mm"], 1)
            pe.wait_ge(s["r_spread"], 1)
            mm(bank[7][:, 128:256], ones[0:T, :], rsel[0:T].rearrange("p t e -> p (t e)"),
               start=True, stop=True).then_inc(s["spread_mm"], 1)
            pe.wait_ge(s["w_ready"], 1)
            pe.wait_ge(s["b2x_ready"], 2)
            bias(0)
            pe.wait_ge(s["p_done"], 1)
            for g in range(2):
                for j in range(4):
                    last = tr(bank[g][:, P * j:P * j + P], plog[:, 4 * g + j, :], ident[:])
                last.then_inc(s["p_T"], 1)
            pe.wait_ge(s["base_ready"], 2)
            pe.wait_ge(s["p_evict"], 2)
            turn_x(0, 0)
            expert_up(0, 0)
            for c in range(NC):
                if c + 1 < NC:
                    turn_x(0, c + 1)
                    expert_up(0, c + 1)
                expert_down(0, c)

            def scores(t):
                n = slice(P * (t % CH), P * (t % CH) + P)
                if t:
                    pe.wait_ge(s["s_max"], t)
                for h in range(NH):
                    last = mm(bank[2 + h // 4][:, P * (h % 4):P * (h % 4) + P], qd[:, h, n], kz[:, n],
                              start=True, stop=True)
                last.then_inc(s["s_mm"], 1)

            def turn_max(t):
                pe.wait_ge(s["s_max"], t + 1)
                if t:
                    pe.wait_ge(s["aug_ready"], t)
                tr(bank[7][0:D + NH, 0:P], nmax[:, t % 2, :], ident[:]).then_inc(s["nm_T"], 1)

            def scores_T(t):
                n = slice(P * (t % CH), P * (t % CH) + P)
                pe.wait_ge(s["aug_ready"], t + 1)
                for g in range(2):
                    if t:
                        pe.wait_ge(s["p_ready"], 2 * t - 1 + g)
                    mm(bank[4 + g][:], kaug[:, n], qd[:, 4 * g:4 * g + 4, n], start=True, stop=True).then_inc(s["st_mm"], 1)

            def values(t):
                pe.wait_ge(s["p_ready"], 2 * t + 2)
                j = t % CH
                if j == 0 and t:
                    pe.wait_ge(s["comb_done"], t // CH)
                for h in range(NH):
                    o = 9 * (NH * j + h)
                    last = mm(bank[6][:, o:o + 9], pexp[:, t % 2, h, :], vaug[:, j, h, :], start=True, stop=True)
                last.then_inc(s["av_mm"], 1)

            for c in range(NC):
                pe.wait_ge(s["d_norm"], c + 1)
                if c == 0:
                    pe.wait_ge(s["y_read"], T)
                    pe.wait_ge(s["pad"], 3)
                if c:
                    pe.wait_ge(s["at_xT"], c)
                for j in range(CH):
                    last = tr(bank[0][0:D, P * j:P * j + P], XN[:, CH * c + j, :], ident[:])
                last.then_inc(s["d_T"], 1)
                pe.wait_ge(s["d_xT"], c + 1)
                if c:
                    pe.wait_ge(s["d_add"], c)
                    pe.wait_ge(s["s_max"], CH * c)
                mm(bank[1][0:D, :], wq[:], xa[:, 0, :], start=True, stop=True).then_inc(s["d_q"], 1)
                mm(bank[2][0:D, :], wk[:], xa[:, 0, :], start=True, stop=True).then_inc(s["d_k"], 1)
                for j in range(CH):
                    last = mm(bank[3][:, D * j:D * j + D], xa[:, 0, P * j:P * j + P], wv[:], start=True, stop=True)
                last.then_inc(s["d_v"], 1)
                pe.wait_ge(s["d_qd"], NH * (c + 1))
                pe.wait_ge(s["d_kcopy"], c + 1)
                pe.wait_ge(s["d_vcopy"], c + 1)
                scores(CH * c)
                for j in range(CH):
                    t = CH * c + j
                    turn_max(t)
                    if j + 1 < CH:
                        scores(t + 1)
                    scores_T(t)
                    if j:
                        values(t - 1)
                values(CH * c + CH - 1)
                for h in range(NH):
                    last = mm(bank[1][:, 36 * h:36 * h + 36], posT[:, h, :], vaug[:, :, h, :], start=True, stop=True)
                last.then_inc(s["pos_mm"], 1)
                pe.wait_ge(s["comb_done"], c + 1)
                for j in range(CH):
                    last = tr(bank[0][0:D, P * j:P * j + P], att[:, j, :], ident[:])
                last.then_inc(s["at_T"], 1)
                pe.wait_ge(s["at_xT"], c + 1)
                for j in range(CH):
                    last = mm(bank[1][:, D * j:D * j + D], xa[:, 1, P * j:P * j + P], wproj[:], start=True, stop=True)
                last.then_inc(s["proj_mm"], 1)

            for c in range(NC):
                pe.wait_ge(s["e_norm"], c + 1)
                if c == 0:
                    pe.wait_ge(s["d_add"], NC)
                turn_x(1, c)
                pe.wait_ge(s["x_xT"], NC + c + 1)
                for j in range(CH):
                    t = CH * c + j
                    last = mm(bank[7][:, E * t:E * t + E], xin(1, c)[:, P * j:P * j + P], wr[1][:],
                              start=True, stop=True)
                last.then_inc(s["rl_mm"], 1)
            pe.wait_ge(s["w_ready"], 2)
            bias(1)
            pe.wait_ge(s["base_ready"], 4)
            for c in range(NC):
                expert_up(1, c)
                expert_down(1, c)

        @block.vector
        def _(dve):
            ch = Chain(dve, s["dve_chain"])
            dve.wait_ge(s["consts"], 1)
            dve.wait_ge(s["load_tok"], 16)
            ch(dve.tensor_scalar(onehot, tok[0:VOC, :], iota_f[0:VOC, 0:1], None, ALU.is_equal))
            dve.wait_ge(s["decay_exp"], 1)
            ch(dve.tensor_scalar(decay[:, 1:2], decay[:, 0:1], 1.0, None, ALU.add))
            ch.settle()
            ch(dve.reciprocal(decay[:, 2:3], decay[:, 1:2]))
            ch.settle()
            ch(dve.tensor_scalar(keep, tok, 0.0, decay[:, 2:3], ALU.not_equal, ALU.mult))
            ch(dve.tensor_scalar(iszero, tok, 0.0, None, ALU.is_equal))
            ch.settle()
            ch(dve.tensor_tensor(keep, keep, iszero, ALU.add))
            ch.settle()
            ch(dve.memset(keep.rearrange("p (t q) -> p t q", t=T)[:, :, 0], 0.0))
            dve.wait_ge(s["utab_mm"], 1)
            dve.wait_ge(s["load_rows"], 32)
            dve.wait_ge(s["load_emb"], 64)
            ch(dve.tensor_tensor(utab[:], bank[0][0:VOC, 0:DT], row("b_upd", parts=VOC), ALU.add))
            ch.settle()
            ch(dve.memset(utab[0:1, :], 0.0))
            ch.settle()
            dve.tensor_copy(decay[:, 3:4], decay[:, 2:3]).then_inc(s["tables_ready"], 1)
            dve.tensor_tensor(embf[:], emb[:], row("b_f", parts=VOC), ALU.add).then_inc(s["tables_ready"], 1)

            def embed(c):
                dve.wait_ge(s["u_mm"], c + 1)
                dve.tensor_tensor_scan(memT[:, 512 * c:512 * c + 512], keep[:, 512 * c:512 * c + 512],
                                       bank[4 + c % 2][:], 0.0, ALU.mult, ALU.add).then_inc(s["mem_ready"], 1)
                dve.wait_ge(s["x_mm"], c + 1)
                tiles = [bank[6 + c % 2][:, DT * j:DT * j + DT] for j in range(CH)]
                norm_stats(dve, ch, ("norm", c), tiles)
                norm_apply(dve, ("norm", c), tiles, [xtmp[:, CH * c + j, :] for j in range(CH)])\
                    .then_inc(s["norm_scaled"], 1)

            def unit_tiles(w):
                i, c = unit(w)
                return [X[:, CH * c + j, :] for j in range(CH)]

            def unit_stats(w):
                i, c = unit(w)
                if w % UP < 2:
                    dve.wait_ge(s["norm_done"], c + 1)
                else:
                    dve.wait_ge(s["tok_add"], w - 1)
                norm_stats(dve, ch, ("tok", w), unit_tiles(w))

            def unit_norm(w):
                if w >= 2:
                    dve.wait_ge(s["tok_T"], w - 1)
                norm_apply(dve, ("tok", w), unit_tiles(w), [xn_tok[:, w % 2, j, :] for j in range(CH)])\
                    .then_inc(s["tok_norm"], 1)

            def add(w):
                i, c = unit(w)
                dve.wait_ge(s["tok_down"], w + 1)
                dve.wait_ge(s["xb_ready"], w + 1)
                dve.tensor_tensor(X[:, CH * c:CH * c + CH, :], bank[3][:].rearrange("p (t d) -> p t d", t=CH),
                                  xb_tok[:, c], ALU.add).then_inc(s["tok_add"], 1)

            def head(p):
                for c in (2 * p, 2 * p + 1):
                    dve.wait_ge(s["head_mm"], c + 1)
                    dve.tensor_tensor(H[:, CH * c:CH * c + CH, :],
                                      bank[3][:, 0:CH * VOC].rearrange("p (t d) -> p t d", t=CH),
                                      row("head_b").unsqueeze(1).broadcast_to([P, CH, VOC]), ALU.add).then_inc(s["head_add"], 1)

            hd = "p (h j) -> p h j"

            def rk_max(t):
                k = t % 2
                b6 = bank[6 if t % 2 == 0 else 3]
                dve.wait_ge(s["a_qkv"], t + 1)
                if t >= 2:
                    dve.wait_ge(s["a_rexp"], t - 1)
                if t == TP:
                    dve.wait_ge(s["upd_mm"], summed("rec", TP - 1))
                rk = b6[:, 0:HB].rearrange(hd, h=NH)
                ch(dve.tensor_reduce(mx[:, k, :], rk, AX_X, ALU.max))
                ch(dve.tensor_copy(beta[:, t].rearrange("p n h -> p (n h)"), b6[:, HB:HB + 16]))
                ch.settle()
                dve.tensor_tensor(kdd[:, k, :].rearrange(hd, h=NH), rk,
                                  mx[:, k, :].unsqueeze(2).broadcast_to([P, NH, DH]), ALU.subtract).then_inc(s["a_sub"], 1)

            def tile_sums(t):
                k = t % 2
                bt = beta[:, t].rearrange("p n h -> p (n h)")
                dve.wait_ge(s["a_acts"], t + 1)
                ch(dve.scalar_tensor_tensor(out=e1[:, k, :], in0=e1[:, k, :], scalar=1.0, in1=r1[:, k, :],
                                            op0=ALU.min, op1=ALU.add))
                dve.wait_ge(s["a_rexp"], t + 1)
                ch(dve.tensor_scalar(bt, bt, 1.0, None, ALU.add))
                ch(dve.tensor_reduce(smallv[:, 2 + k, 16:24], ker[:, k, :].rearrange(hd, h=NH), AX_X, ALU.add))
                ch.settle()
                ch(dve.tensor_reduce(smallv[:, 2 + k, 0:16], e1[:, k, :].rearrange(hd, h=2 * NH), AX_X, ALU.add))
                ch(dve.reciprocal(bt, bt))
                if t >= 2:
                    dve.wait_ge(s["a_keys"], t - 1)
                ch.settle()
                dve.reciprocal(smallv[:, k, 0:24], smallv[:, 2 + k, 0:24]).then_inc(s["a_elu"], 1)

            def project(p):
                for c in (2 * p, 2 * p + 1):
                    r = range(CH * c, CH * c + CH)
                    dve.wait_ge(s["head_add"], c + 1)
                    norm_stats(dve, ch, ("a1", c), [H[:, t, :] for t in r])
                    ch(norm_apply(dve, ("a1", c), [H[:, t, :] for t in r], [XN[:, t, :] for t in r]))
                    ch.settle()
                    norm_stats(dve, ch, ("a2", c), [XN[:, t, :] for t in r])
                    norm_apply(dve, ("a2", c), [XN[:, t, :] for t in r], [X[:, t, 0:D] for t in r]).then_inc(s["a_norm"], 1)
                for t in range(TP * p, TP * p + TP):
                    rk_max(t)
                    if t % TP:
                        tile_sums(t - 1)
                tile_sums(TP * p + TP - 1)

            def combine(kind, t, between=None):
                for i, r0, r1_ in combos_of(kind, t):
                    if i >= 4:
                        dve.wait_ge(s["upd_mm"], i - 3)
                    R = r1_ - r0
                    if kind == "held":
                        out = PB[:, i % 4, 0:R * 2 * HB].rearrange("p (g j) -> p g j", j=DH)
                        u = UV[:, r0:r1_].rearrange("p r n (h j) -> p (r n h) j", h=NH)
                        co = CG[:, t % 2, r0:r1_].rearrange("p r n h -> p (r n h)").unsqueeze(2).broadcast_to([P, R * 2 * NH, DH])
                    else:
                        out = PB[:, i % 4, 0:R * HB].rearrange("p (r h j) -> p r h j", r=R, h=NH)
                        u = UV[:, r0:r1_, 0 if kind == "fast" else 1].rearrange("p r (h j) -> p r h j", h=NH)
                        co = CQ[:, t % 2, r0:r1_] if kind == "fast" else CR[:, r0:r1_]
                        co = co.unsqueeze(3).broadcast_to([P, R, NH, DH])
                    dve.tensor_tensor(out, u, co, ALU.mult).then_inc(s["upd_p"], 1)
                    if between:
                        between(r0)

            def take_coefficients(t):
                for j, (r0, r1_) in enumerate(pieces(t)):
                    for n in range(2):
                        dve.wait_ge(s["gram_p"], 2 * (gram_base(t) + j) + n + 1)
                        dve.tensor_reduce(CG[:, t % 2, r0:r1_, n, :],
                                          key_products(n, t, j)[:, 0:r1_ - r0, :].rearrange("p r (g j) -> p r g j", g=NH),
                                          AX_X, ALU.add).then_inc(s["gram_read"], 1)
                if t:
                    dve.wait_ge(s["gram_read"], 2 * gram_base(t + 1))

            def updates(t):
                uv = UV[:, t].rearrange("p n h -> p (n h)")
                if t:
                    dve.wait_ge(s["upd_mm"], summed("held", t))
                    ch(dve.tensor_tensor(uv, uv, bank[6][:], ALU.subtract))
                    ch.settle()
                ut = uv.rearrange("p (g j) -> p g j", j=DH)
                dve.tensor_tensor(ut, ut, beta[:, t].rearrange("p n h -> p (n h)").unsqueeze(2)
                                  .broadcast_to([P, 2 * NH, DH]), ALU.mult).then_inc(s["acc_done"], 1)
                dve.wait_ge(s["acc_done"], t + 1)

            def query_sub(t):
                h = bank[7][:, 0:HB].rearrange(hd, h=NH)
                dve.wait_ge(s["upd_mm"], summed("rec", t - 1))
                ch(dve.tensor_reduce(mx[:, t % 2, :], h, AX_X, ALU.max))
                ch.settle()
                dve.tensor_tensor(dd[:, t % 2, :].rearrange(hd, h=NH), h,
                                  mx[:, t % 2, :].unsqueeze(2).broadcast_to([P, NH, DH]), ALU.subtract).then_inc(s["e_sub"], 1)

            def query_sum(t):
                if t:
                    dve.wait_ge(s["h_exp"], t)
                ch(dve.tensor_reduce(smallv[:, 4, 0:NH], er[:, t % 2, :].rearrange(hd, h=NH), AX_X, ALU.add))
                ch.settle()
                ch(dve.reciprocal(smallv[:, 5, 0:NH], smallv[:, 4, 0:NH]))

            def step(t, p):
                w = UP + t
                k = t % 2
                if t % TP:
                    query_sub(t)
                dve.wait_ge(s["query_done"], t + 1)
                combine("fast", t)
                if p == 0 and t + 1 < UP:
                    unit_stats(w + 1)
                if (t + 1) % TP:
                    if p == 0 and t + 1 < UP:
                        unit_norm(w + 1)
                query_sum(t)

                def query_piece(r0):
                    if r0 % 4:
                        return
                    r1_ = min(r0 + 4, t + 1)
                    R = r1_ - r0
                    ch(dve.tensor_tensor(PD[:, 0:R, :], RK[:, r0:r1_, :],
                                         er[:, k, :].unsqueeze(1).broadcast_to([P, R, HB]), ALU.mult))
                    ch.settle()
                    ch(dve.tensor_reduce(CR[:, r0:r1_, :], PD[:, 0:R, :].rearrange("p r (g j) -> p r g j", g=NH),
                                         AX_X, ALU.add))
                    ch.settle()

                if (t + 1) % TP:
                    combine("held", t + 1, query_piece)
                else:
                    for r0, _ in pieces(t + 1):
                        query_piece(r0)
                ch(dve.tensor_tensor(CR[:, 0:t + 1, :], CR[:, 0:t + 1, :],
                                     smallv[:, 5, 0:NH].unsqueeze(1).broadcast_to([P, t + 1, NH]), ALU.mult))
                ch.settle()
                combine("rec", t)
                if p == 0:
                    add(w)
                if (t + 1) % TP:
                    updates(t + 1)
                if t + 2 < TP * p + TP:
                    take_coefficients(t + 2)
                if t:
                    out_add(t - 1)

            def out_add(t):
                if t % CH == 0:
                    dve.wait_ge(s["a_hx"], t // CH + 1)
                dve.wait_ge(s["o_mm"], t + 1)
                dve.tensor_tensor(H[:, t, :], bank[3][:, 0:D], H[:, t, :], ALU.add).then_inc(s["o_add"], 1)

            embed(0)
            embed(1)
            unit_stats(0)
            unit_norm(0)
            for v in range(UP):
                if v + 1 < UP:
                    unit_stats(v + 1)
                    unit_norm(v + 1)
                if v in (1, 3):
                    embed(2 + v // 2)
                add(v)
            unit_stats(UP)
            unit_norm(UP)
            for p in range(NP):
                head(p)
                project(p)
                dve.wait_ge(s["a_keys"], TP * (p + 1))
                if p == 0:
                    ch(dve.memset(er[:, 0, :], 1.0))
                    ch.settle()
                take_coefficients(TP * p)
                if p:
                    combine("held", TP)
                updates(TP * p)
                take_coefficients(TP * p + 1)
                for t in range(TP * p, TP * p + TP):
                    step(t, p)
                if p == 0:
                    query_sub(TP)
            out_add(T - 1)

            sub, mul, plus = ALU.subtract, ALU.mult, ALU.add
            tt = dve.tensor_tensor
            ch(dve.memset(vaug[:, :, :, HD:HD + 1], 1.0))
            ch(dve.memset(nmax, 0.0))
            dve.wait_ge(s["masks"], 2)
            dve.wait_ge(s["pad"], 1)
            for c in range(NC):
                r = range(CH * c, CH * c + CH)
                dve.wait_ge(s["o_add"], CH * c + CH)
                norm_stats(dve, ch, ("f0", c), [H[:, t, :] for t in r])
                norm_apply(dve, ("f0", c), [H[:, t, :] for t in r], [XN[:, t, :] for t in r]).then_inc(s["x_norm"], 1)

            def rank2(x, sel, n, parts):
                shape = [parts, n, E, E]
                own, other = x.unsqueeze(3).broadcast_to(shape), x.unsqueeze(2).broadcast_to(shape)
                a_, b_ = (c[0:parts, 0:n * E * E].rearrange("p (t e f) -> p t e f", t=n, e=E) for c in (cmp1, cmp2))
                ch(tt(a_, other, own, ALU.is_gt))
                ch(tt(b_, other, own, ALU.is_equal))
                ch.settle()
                ch(tt(b_, b_, lower[0:parts].unsqueeze(1).broadcast_to(shape), mul))
                ch.settle()
                ch(tt(a_, a_, b_, plus))
                ch.settle()
                ch(dve.tensor_reduce(sel, a_, AX_X, plus))
                ch.settle()
                ch(dve.tensor_scalar(sel, sel, 1.5, None, ALU.is_lt))
                ch.settle()

            def small_softmax(x, j, out):
                m, z = rsm[0:T, 0, j:j + 1], rsm[0:T, 1, j:j + 1]
                ch(dve.tensor_reduce(m, x, AX_X, ALU.max))
                ch.settle()
                dve.tensor_scalar(rsel[0:T, j, :], x, m, None, sub).then_inc(s["r_sub"], 1)
                dve.wait_ge(s["r_exp"], j + 1)
                if out is None:
                    return
                ch(dve.tensor_reduce(z, rsel[0:T, j, :], AX_X, plus))
                ch.settle()
                ch(dve.reciprocal(z, z))
                ch.settle()
                return dve.tensor_scalar(out, rsel[0:T, j, :], z, None, mul)

            CAPACITY = float(-(-N * 5 // (4 * E)))
            dve.wait_ge(s["logit_mm"], 1)
            ch(tt(rout[0:T, 3, :], bank[7][0:T, 64:64 + E], row("br0", parts=T), plus))
            ch.settle()
            small_softmax(rout[0:T, 3, :], 0, rout[0:T, 0, :]).then_inc(s["r_prob"], 1)
            dve.wait_ge(s["load_mm"], 1)
            sc = rout[0:T, 4, :]
            ch(dve.tensor_scalar(sc, bank[7][0:T, 96:96 + E], float(P), None, mul))
            ch.settle()
            ch(dve.reciprocal(sc, sc))
            ch.settle()
            ch(dve.tensor_scalar(sc, sc, CAPACITY, 1.0, mul, ALU.min))
            ch.settle()
            dve.wait_ge(s["r_prob"], 1)
            ch(tt(rout[0:T, 1, :], rout[0:T, 0, :], sc, mul))
            ch.settle()
            ch(small_softmax(rout[0:T, 1, :], 1, rout[0:T, 2, :]))
            ch.settle()
            small_softmax(rout[0:T, 2, :], 2, None)
            rank2(rout[0:T, 2:3, :], rout[0:T, 5:6, :], 1, T)
            w = rout[0:T, 5, :]
            ch(tt(w, w, rsel[0:T, 2, :], mul))
            ch.settle()
            ch(dve.tensor_reduce(rsm[0:T, 2, 0:1], w, AX_X, plus))
            ch.settle()
            ch(dve.reciprocal(rsm[0:T, 2, 1:2], rsm[0:T, 2, 0:1]))
            ch.settle()
            ch(dve.tensor_scalar(w, w, rsm[0:T, 2, 1:2], None, mul))
            ch.settle()
            tt(rsel[0:T], w.unsqueeze(1).broadcast_to([T, T, E]), ident[0:T, 0:T].unsqueeze(2).broadcast_to([T, T, E]),
               mul).then_inc(s["r_spread"], 1)
            dve.wait_ge(s["spread_mm"], 1)
            dve.tensor_copy(wts[:].rearrange("p t e -> p (t e)"), bank[7][:, 128:256]).then_inc(s["w_ready"], 1)

            dve.wait_ge(s["p_rel"], 1)
            wp = row("wpos").rearrange("p (k h) -> p k h", k=3)
            ch(dve.scalar_tensor_tensor(out=gate[:, 3, :], in0=wp[:, 1, :], scalar=0.0, in1=row("bpos"), op0=mul, op1=plus))
            ch.settle()
            for h in range(NH):
                ch(dve.tensor_scalar(plog[:, h, :], rel, wp[:, 0, h:h + 1], gate[:, 3, h:h + 1], mul, plus))
            ch.settle()
            for h in range(NH):
                ch(dve.scalar_tensor_tensor(out=plog[:, h, :], in0=rel2, scalar=wp[:, 2, h:h + 1], in1=plog[:, h, :],
                                            op0=mul, op1=plus))
            ch.settle()
            ch(dve.tensor_reduce(comb[:, 0, 0:NH], plog, AX_X, ALU.max))
            ch.settle()
            tt(plog, plog, comb[:, 0, 0:NH].unsqueeze(2).broadcast_to([P, NH, P]), sub).then_inc(s["p_sub"], 1)
            dve.wait_ge(s["p_exp"], 1)
            ch(dve.tensor_reduce(comb[:, 0, 0:NH], plog, AX_X, plus))
            ch.settle()
            ch(dve.reciprocal(comb[:, 0, 8:8 + NH], comb[:, 0, 0:NH]))
            ch.settle()
            tt(plog, plog, comb[:, 0, 8:8 + NH].unsqueeze(2).broadcast_to([P, NH, P]), mul).then_inc(s["p_done"], 1)
            dve.wait_ge(s["gate_exp"], 1)
            ch(dve.tensor_scalar(gate[:, 0, :], gate[:, 0, :], 1.0, None, plus))
            ch.settle()
            ch(dve.reciprocal(gate[:, 1, :], gate[:, 0, :]))
            ch.settle()
            ch(dve.tensor_scalar(gate[:, 2, :], gate[:, 1, :], -1.0, 1.0, mul, plus))

            for g in range(2):
                dve.wait_ge(s["bias_mm"], g + 1)
                r = slice(8 * g, 8 * g + 8)
                tt(YB[0][:, r, :], bank[4 + g][:].rearrange("p (t d) -> p t d", t=8), XN[:, r, :],
                   plus).then_inc(s["base_ready"], 1)
            dve.wait_ge(s["base_ready"], 2)
            for c in range(NC):
                r = range(CH * c, CH * c + CH)
                for t in r:
                    dve.wait_ge(s["x_down"], t + 1)
                    tt(YB[0][:, t, :], bank[4 + t % 2][:, 0:D], YB[0][:, t, :], plus).then_inc(s["y_read"], 1)
                dve.wait_ge(s["y_read"], CH * c + CH)
                norm_stats(dve, ch, ("f1", c), [YB[0][:, t, :] for t in r])
                norm_apply(dve, ("f1", c), [YB[0][:, t, :] for t in r], [YB[1][:, t, :] for t in r]).then_inc(s["f1_norm"], 1)

            for c in range(NC):
                r = range(CH * c, CH * c + CH)
                dve.wait_ge(s["f_affine"], c + 1)
                norm_stats(dve, ch, ("d", c), [H[:, t, :] for t in r])
                norm_apply(dve, ("d", c), [H[:, t, :] for t in r], [XN[:, t, :] for t in r]).then_inc(s["d_norm"], 1)
            th = [P, CH, NH]
            g_ = gate[:, 1, :].unsqueeze(1).broadcast_to(th)
            omg = gate[:, 2, :].unsqueeze(1).broadcast_to(th)
            cb = [comb[:, k, :].rearrange("p (t h) -> p t h", t=CH) for k in range(6)]
            ch.settle()
            dve.wait_ge(s["pad"], 3)
            for c in range(NC):
                for j in range(CH):
                    t = CH * c + j
                    dve.wait_ge(s["s_mm"], t + 1)
                    for g in range(2):
                        last = dve.tensor_reduce(nmax[:, t % 2, D + 4 * g:D + 4 * g + 4],
                                                 bank[2 + g][:].rearrange("p (h m) -> p h m", h=4), AX_X, ALU.max, negate=True)
                    last.then_inc(s["s_max"], 1)
                    dve.wait_ge(s["nm_T"], t + 1)
                    tt(qd_rows(j), bank[7][D:D + NH, 0:P].unsqueeze(1).broadcast_to([NH, NH, P]),
                       ident[D:D + NH, D:D + NH].unsqueeze(2).broadcast_to([NH, NH, P]), mul).then_inc(s["aug_ready"], 1)
                dve.wait_ge(s["av_mm"], CH * c + CH)
                dve.wait_ge(s["pos_mm"], c + 1)
                o = bank[6][:, 0:CH * NH * 9].rearrange("p (t h d) -> p t h d", t=CH, h=NH)
                po = bank[1][:, 0:CH * NH * 9].rearrange("p (h t d) -> p t h d", t=CH, h=NH)
                ch(dve.reciprocal(cb[0], o[:, :, :, HD]))
                ch(tt(cb[3], po[:, :, :, HD], g_, mul))
                ch.settle()
                ch(tt(cb[1], cb[0], omg, mul))
                ch.settle()
                ch(tt(cb[2], o[:, :, :, HD], cb[1], mul))
                ch.settle()
                ch(tt(cb[2], cb[2], cb[3], plus))
                ch.settle()
                ch(dve.reciprocal(cb[4], cb[2]))
                ch.settle()
                ch(tt(cb[1], cb[1], cb[4], mul))
                ch(tt(cb[5], cb[4], g_, mul))
                ch.settle()
                full = [P, CH, NH, HD]
                ch(tt(att.rearrange("p t (h d) -> p t h d", h=NH), o[:, :, :, 0:HD], cb[1].unsqueeze(3).broadcast_to(full), mul))
                ch(tt(att2.rearrange("p t (h d) -> p t h d", h=NH), po[:, :, :, 0:HD], cb[5].unsqueeze(3).broadcast_to(full), mul))
                ch.settle()
                tt(att, att, att2, plus).then_inc(s["comb_done"], 1)
                dve.wait_ge(s["proj_mm"], c + 1)
                dve.wait_ge(s["hb_ready"], c + 1)
                hc = H[:, CH * c:CH * c + CH, :]
                tt(hc, bank[1][:, 0:CH * D].rearrange("p (t d) -> p t d", t=CH), hc, plus).then_inc(s["d_add"], 1)

            for c in range(NC):
                r = range(CH * c, CH * c + CH)
                dve.wait_ge(s["d_add"], c + 1)
                norm_stats(dve, ch, ("e1", c), [H[:, t, :] for t in r])
                ch(norm_apply(dve, ("e1", c), [H[:, t, :] for t in r], [XN[:, t, :] for t in r]))
                ch.settle()
                norm_stats(dve, ch, ("e2", c), [XN[:, t, :] for t in r])
                norm_apply(dve, ("e2", c), [XN[:, t, :] for t in r], [YB[0][:, t, :] for t in r]).then_inc(s["e_norm"], 1)
            te = [P, T, E]
            dve.wait_ge(s["rl_mm"], NC)
            ch(tt(rout[:], bank[7][:, 0:T * E].rearrange("p (t e) -> p t e", t=T),
                  row("br1").unsqueeze(1).broadcast_to(te), plus))
            ch.settle()
            ch(dve.tensor_reduce(rsm[:, 0, :], rout[:], AX_X, ALU.max))
            ch.settle()
            tt(rsel[:], rout[:], rsm[:, 0, :].unsqueeze(2).broadcast_to(te), sub).then_inc(s["rl_read"], 1)
            rank2(rout[:], wts[:], T, P)
            dve.wait_ge(s["rl_exp"], 1)
            ch(tt(wts[:], wts[:], rsel[:], mul))
            ch.settle()
            ch(dve.tensor_reduce(rsm[:, 1, :], wts[:], AX_X, plus))
            ch.settle()
            ch(dve.reciprocal(rsm[:, 2, :], rsm[:, 1, :]))
            ch.settle()
            tt(wts[:], wts[:], rsm[:, 2, :].unsqueeze(2).broadcast_to(te), mul).then_inc(s["w_ready"], 1)
            dve.wait_ge(s["w_ready"], 2)
            for g in range(2):
                dve.wait_ge(s["bias_mm"], 2 + g + 1)
                r = slice(8 * g, 8 * g + 8)
                tt(H[:, r, :], bank[4 + g][:].rearrange("p (t d) -> p t d", t=8), H[:, r, :], plus).then_inc(s["base_ready"], 1)
            dve.wait_ge(s["base_ready"], 4)
            for c in range(NC):
                for t in range(CH * c, CH * c + CH):
                    dve.wait_ge(s["x_down"], T + t + 1)
                    tt(ytmp[:, t % 2], bank[4 + t % 2][:].rearrange("p (e d) -> p e d", e=E),
                       wts[:, t, :].unsqueeze(2).broadcast_to([P, E, D]), mul).then_inc(s["y_read"], 1)
                    dve.wait_ge(s["y_read"], T + t + 1)
                    ch(dve.tensor_reduce(YB[1][:, t, :], ytmp[:, t % 2].rearrange("p e d -> p d e"), AX_X, plus))
                ch.settle()
                hc = H[:, CH * c:CH * c + CH, :]
                tt(hc, hc, YB[1][:, CH * c:CH * c + CH, :], plus).then_inc(s["out_done"], 1)


def kernel(**inp):
    import numpy as np
    import concourse.bacc as bacc
    from concourse.bass_utils import run_bass_kernel_spmd as run

    i = {k: np.asarray(v) for k, v in inp.items()}
    flat = np.ravel
    rows = {
        "norm_g": i["L0_tok_norm_g"], "norm_b": i["L0_tok_norm_b"], "b2": i["L0_tok_cms_b2"],
        "b_upd": i["L0_tok_b_upd"], "b_f": i["L0_tok_b_f"], "head_b": i["L0_tok_head_b"],
        "decay": i["L0_tok_decay_param"], "br0": i["L0_ffn_br"],
        "gamma0": i["L0_ffn_gamma"], "beta0": i["L0_ffn_beta"], "bpos": i["L1_attn_bpos"],
        "wpos": i["L1_attn_Wpos"].T, "bproj": i["L1_attn_bproj"], "gating": i["L1_attn_gating"],
        "br1": i["L1_ffn_br"],
    }
    cols = {
        "ln_g": i["L0_tok_cms_ln_g"].T, "ln_b": i["L0_tok_cms_ln_b"].T,
        "b1": i["L0_tok_cms_b1"].reshape(NL * 4, P).T, "eb10": i["L0_ffn_b1"].T, "eb11": i["L1_ffn_b1"].T,
        "aln_g": i["L0_attn_ln_g"][:, None], "aln_b": i["L0_attn_ln_b"][:, None],
        "gamma1": i["L1_ffn_gamma"][:, None], "beta1": i["L1_ffn_beta"][:, None],
    }
    place, n = offsets(COLS)
    colv = np.zeros((P, n), np.float32)
    for k, v in cols.items():
        colv[0:v.shape[0], place[k][0]:place[k][1]] = v
    sw = i["L0_attn_slow_W"].reshape(NH, 5 * DH + 2, D)
    q, k_, v_, rk, rv = (sw[:, DH * j:DH * j + DH].reshape(HB, D) for j in range(5))
    slow = np.concatenate([q, k_, v_, rv, rk, sw[:, 5 * DH], sw[:, 5 * DH + 1]]).T
    arrays = {
        "tok": i["x"].reshape(-1),
        "rows": np.concatenate([flat(rows[k]) for k, _ in ROWS]),
        "cols": colv,
        "emb": i["L0_tok_emb"], "embT": i["L0_tok_emb"].T, "wupd": i["L0_tok_W_upd"], "wf": i["L0_tok_W_f"],
        "w1": i["L0_tok_cms_W1"].transpose(1, 0, 2),
        "w2": i["L0_tok_cms_W2"].reshape(NL, 4, P, DT).transpose(2, 0, 1, 3),
        "headw": i["L0_tok_head_W"],
        "sloww": slow, "outw": i["L0_attn_out_W"].T.reshape(2, P, D).transpose(1, 0, 2),
        "ew1_0": i["L0_ffn_W1"].transpose(1, 0, 2), "ew2_0": i["L0_ffn_W2"].transpose(1, 0, 2), "wr_0": i["L0_ffn_Wr"],
        "ew1_1": i["L1_ffn_W1"].transpose(1, 0, 2), "ew2_1": i["L1_ffn_W2"].transpose(1, 0, 2), "wr_1": i["L1_ffn_Wr"],
        "wq": i["L1_attn_Wqk"][0:D].T, "wk": i["L1_attn_Wqk"][D:].T,
        "eb2_0": np.tile(i["L0_ffn_b2"], (T, 1)), "eb2_1": np.tile(i["L1_ffn_b2"], (T, 1)),
        "wv": i["L1_attn_Wv"].T, "wproj": i["L1_attn_Wproj"].T,
    }
    nc = bacc.Bacc("TRN2", target_bir_lowering=False, num_devices=1)
    feed, aps = {}, {}
    for k, v in arrays.items():
        v = np.ascontiguousarray(v)
        feed[f"in_{k}"] = v
        aps[k] = nc.dram_tensor(f"in_{k}", v.shape, mybir.dt.from_np(v.dtype), kind="ExternalInput").ap()
    out = nc.dram_tensor("out_h", (T, P, D), F32, kind="ExternalOutput").ap()
    aps["out"] = out.rearrange("t p d -> p t d")
    build(nc, aps)
    r = run(nc, [feed], core_ids=[0])
    return r.results[0]["out_h"]
```

```python
from contextlib import ExitStack

import concourse.bass as bass
from concourse import mybir

ALU = mybir.AluOpType
ACT = mybir.ActivationFunctionType
F32 = mybir.dt.float32
I32 = mybir.dt.int32
AX_X = mybir.AxisListType.X

EPS = 1e-5
P = 128

T = 16
DT = 128
NL = 4
VOC = 64
D = 64
NH, DH = 8, 32
HB = NH * DH
E, FF = 8, 128
HD = D // NH
CH = 4
NC = T // CH
NP = 2
TP = T // NP
KS = TP + 2
UP = 2 * NL
N = T * P

ROWS = [("norm_g", DT), ("norm_b", DT), ("b2", NL * DT), ("b_upd", DT), ("b_f", DT), ("head_b", VOC), ("decay", 1),
        ("br0", E), ("gamma0", D), ("beta0", D), ("bpos", NH), ("wpos", 3 * NH), ("bproj", D),
        ("gating", NH), ("br1", E)]
COLS = [("ln_g", NL), ("ln_b", NL), ("b1", NL * 4), ("eb10", E), ("eb11", E),
        ("aln_g", 1), ("aln_b", 1), ("gamma1", 1), ("beta1", 1)]


def offsets(parts):
    at, out = 0, {}
    for name, n in parts:
        out[name] = (at, at + n)
        at += n
    return out, at


class Chain:

    def __init__(self, eng, sem):
        self.eng, self.sem, self.n = eng, sem, 0

    def __call__(self, ins):
        ins.then_inc(self.sem, 1)
        self.n += 1

    def settle(self):
        self.eng.wait_ge(self.sem, self.n)


def pieces(n, step=4):
    return [(r, min(r + step, n)) for r in range(0, n, step)]


def gram_base(t):
    return sum(len(pieces(i)) for i in range(t))


def gram_reads(t, j, n):
    if t < KS:
        return 2 * (gram_base(t) + j) + n + 1
    return gram_base(KS) + gram_base(t) + j + 1


def combos():
    out = []
    for p in range(NP):
        first, end = TP * p, TP * p + TP
        if p:
            out += [("held", first, r0, r1) for r0, r1 in pieces(first, 2)]
        for t in range(first, end):
            out += [("fast", t, r0, r1) for r0, r1 in pieces(t + 1)]
            if t + 1 < end:
                out += [("held", t + 1, r0, r1) for r0, r1 in pieces(t + 1, 2)]
            out += [("rec", t, r0, r1) for r0, r1 in pieces(t + 1)]
    return out


COMBOS = combos()


def combos_of(kind, t):
    return [(i, r0, r1) for i, (k, s, r0, r1) in enumerate(COMBOS) if k == kind and s == t]


def summed(kind, t):
    return combos_of(kind, t)[-1][0] + 1


def unit(w):
    p, v = divmod(w, UP)
    return v // 2, 2 * p + v % 2


def build(nc, a):
    ROW, NROW = offsets(ROWS)
    COL, NCOL = offsets(COLS)
    with ExitStack() as ctx:
        def sb(name, shape, dt=F32):
            return ctx.enter_context(nc.sbuf_tensor(name, shape, dt))

        def sem(name):
            return ctx.enter_context(nc.semaphore(name))

        bank = [ctx.enter_context(nc.psum_tensor(f"bank{i}", [P, 512], F32)) for i in range(8)]

        rows = sb("rows", [P, NROW])
        cols = sb("cols", [P, NCOL])
        ident = sb("ident", [P, P])
        ones = sb("ones", [P, P])
        neghalf = sb("neghalf", [P, T])
        iota_i = sb("iota_i", [P, 1], I32)
        iota_f = sb("iota_f", [P, 1])
        w1 = sb("w1", [DT, NL, 4 * DT])
        w2 = sb("w2", [P, NL, 4, DT])
        headw = sb("headw", [DT, VOC])
        w1f = w1[:].rearrange("p l n -> p (l n)")
        w2f = w2[:].rearrange("p l f n -> p (l f n)")
        ew1 = [w1f[:, 1024 * k:1024 * k + 1024].rearrange("p (e f) -> p e f", e=E) for k in range(2)]
        ew2 = [w2f[:, 512 * k:512 * k + 512].rearrange("p (e d) -> p e d", e=E) for k in range(2)]
        wq, wk, wv, wproj = (w2f[:, 1024 + D * k:1024 + D * k + D] for k in range(4))
        eb2 = [w2f[:, 1280 + D * k:1280 + D * k + D] for k in range(2)]
        sloww = sb("sloww", [P, 5 * HB + 2 * NH])
        outw = sb("outw", [P, 2, D])
        wr = [sb(f"wr_{k}", [P, E]) for k in range(2)]

        def row(name, n=None, parts=P):
            lo, hi = ROW[name]
            return rows[0:parts, lo:hi]

        def col(name, k=0, parts=P):
            lo = COL[name][0]
            return cols[0:parts, lo + k:lo + k + 1]

        H = sb("H", [P, T, D])
        XN = sb("XN", [P, T, D])
        X = sb("X", [P, T, DT])
        stats = sb("stats", [P, 4, CH, 6])
        mv = sb("mv", [P, 4, CH, 2])
        rstd = sb("rstd", [P, 4, CH])
        xT = sb("xT", [P, 2, 512])
        xa = sb("xa", [P, 2, 512])
        G = sb("G", [P, 8, 512])
        decay = sb("decay", [P, 4])

        KKf = sb("keys", [P, 2 * T * HB])
        QF = sb("QF", [P, T, HB])
        RK = sb("RK", [P, T, HB])
        UV = sb("UV", [P, T, 2, HB])
        PB = sb("PB", [P, 4, 4 * HB])
        PC = sb("PC", [P, 8, HB])
        PD = sb("PD", [P, 4, HB])
        CG = sb("CG", [P, 2, T, 2, NH])
        CQ = sb("CQ", [P, 2, T, NH])
        CR = sb("CR", [P, T, NH])
        beta = sb("beta", [P, T, 2, NH])
        er = sb("er", [P, 2, HB])
        dd = sb("dd", [P, 2, HB])
        hs = sb("hs", [P, 2, HB])
        hsT = sb("hsT", [P, 2, HB])
        PBf = PB[:].rearrange("p k n -> p (k n)")
        e1, r1 = (PBf[:, 1024 * k:1024 * k + 1024].rearrange("p (k n) -> p k n", k=2) for k in range(2))
        ker, kdd = (PBf[:, 2048 + 512 * k:2560 + 512 * k].rearrange("p (k n) -> p k n", k=2) for k in range(2))
        smallv = sb("smallv", [P, 8, 32])
        mx = sb("mx", [P, 2, 8])

        KF = KKf[:, 0:4096].rearrange("p (t n) -> p t n", t=T)

        def key_products(n, t, j):
            if t < TP:
                b = KKf[:, 4096 + 2048 * n:6144 + 2048 * n]
            else:
                b = KKf[:, 4096:8192] if n == 0 else G[:].rearrange("p g n -> p (g n)")
            return b[:, 1024 * j:1024 * j + 1024].rearrange("p (r n) -> p r n", r=4)

        halves = X[:].rearrange("p t d -> p (t d)").rearrange("p (g j) -> p g j", j=DH // 2)

        tok = KKf[:, 0:N].bitcast(I32)
        onehot = KKf[0:VOC, N:2 * N]
        keep = KKf[:, 2 * N:3 * N]
        memT = KKf[:, 3 * N:4 * N]
        QQf = QF[:].rearrange("p t n -> p (t n)")
        iszero = QQf[:, 0:N]
        RKf = RK[:].rearrange("p t h -> p (t h)")
        emb, utab, embf = (RKf[0:VOC, DT * k:DT * k + DT] for k in range(3))
        embT = RKf[:, 3 * DT:3 * DT + VOC]
        wupd, wf = (RKf[:, DT * k:DT * k + DT] for k in (4, 5))
        UVf = UV[:].rearrange("p t n h -> p (t n h)")
        xn_tok = UVf[:, 4096:5120].rearrange("p (k t d) -> p k t d", k=2, t=CH)
        xb_tok = UVf[:, 5120:7168].rearrange("p (k t d) -> p k t d", k=NC, t=CH)
        xtmp = UVf[:, 0:2048].rearrange("p (t d) -> p t d", t=T)

        G2 = [G[:], KKf[:, 0:4096].rearrange("p (e n) -> p e n", e=E)]
        w2w = KKf[:, 4096:5120].rearrange("p (k e d) -> p k e d", k=2, e=E)
        ytmp = KKf[:, 5120:6144].rearrange("p (k e d) -> p k e d", k=2, e=E)
        b2x = KKf[:, 6144:8192].rearrange("p (k t d) -> p k t d", k=2, t=T)
        PCf = PC[:].rearrange("p r n -> p (r n)")
        qd = [b.rearrange("p (h n) -> p h n", h=NH) for b in (UVf[:, 0:4096], PBf)]
        kz = [QQf[:, 0:512], PCf[:, 512:1024]]
        sexp = KKf[:, 0:2048].rearrange("p (k h n) -> p k h n", k=2, h=NH)
        pexp = UVf[:, 4608:6656].rearrange("p (k h n) -> p k h n", k=2, h=NH)
        vaug = [b.rearrange("p (t h d) -> p t h d", t=CH, h=NH) for b in (UVf[:, 6656:6944], PCf[:, 1024:1312])]
        posT = UVf[:, 6944:7968].rearrange("p (h n) -> p h n", h=NH)
        plog = RKf[:, 0:1024].rearrange("p (h m) -> p h m", h=NH)
        rel = RKf[:, 1024:1152]
        rel2 = RKf[:, 1152:1280]
        rel_i = RKf[:, 1280:1408].bitcast(I32)
        smax = RKf[:, 1408:1408 + 2 * NH].rearrange("p (k h) -> p k h", k=2)
        att = RKf[:, 1600:1600 + 256].rearrange("p (t d) -> p t d", t=CH)
        att2 = RKf[:, 1856:1856 + 256].rearrange("p (t d) -> p t d", t=CH)
        cmp1 = RKf[:, 2112:3136]
        cmp2 = PD[:].rearrange("p r n -> p (r n)")
        wts, rout, rsel = (RKf[:, 3136 + P * k:3136 + P * k + P].rearrange("p (t e) -> p t e", t=T) for k in range(3))
        wtsT = RKf[:, 3520:3648]
        rsm = RKf[:, 3648:3712].rearrange("p (k t) -> p k t", k=4)
        meanT = RKf[0:D, 3712:3728]
        YB = [X[:].rearrange("p t d -> p (t d)")[:, 1024 * k:1024 * k + 1024].rearrange("p (t d) -> p t d", t=T)
              for k in range(2)]
        m16 = sb("m16", [P, T])
        lower = sb("lower", [P, E, E])
        gate = sb("gate", [P, 4, NH])
        comb = sb("comb", [P, 6, CH * NH])

        s = {n: sem(n) for n in """
            load_tok load_rows load_emb load_mlp load_attn load_experts stored
            consts dve_chain act_chain pool_chain
            ln_var ln_rstd decay_exp utab_mm tables_ready u_mm mem_ready x_mm norm_scaled norm_done
            xb_ready tok_norm tok_T tok_hT tok_up tok_gelu tok_down tok_add
            head_T head_xT head_mm head_add
            a_norm a_hx a_T a_oT a_qkv a_acts a_sub a_rexp a_elu a_keys pad
            gram_p gram_read gram_mm gram_taken query_half query_done upd_p upd_mm acc_done h_exp e_sub hs_saved
            o_T o_evict o_mm o_add
            masks b2x_ready x_norm mean_mm mean_ready logit_mm r_sub r_exp r_prob load_mm r_spread
            spread_mm w_ready wT_mm wT_ready bias_mm base_ready w2w_ready x_T x_xT x_up x_gelu x_down y_read
            f1_norm f_affine
            p_rel p_sub p_exp p_done p_T p_evict gate_exp
            d_norm d_T d_xT d_q d_qd d_k d_kcopy d_v d_vcopy s_mm s_sub s_exp s_T p_ready av_mm pos_mm
            comb_done at_T at_xT proj_mm d_add hb_ready
            e_norm rl_mm rl_read rl_exp out_done
            """.split()}

        block = ctx.enter_context(nc.Block())

        LN = []
        for p in range(NP):
            if p == 0:
                LN += [("norm", 0), ("tok", 0), ("norm", 1)]
                for v in range(UP):
                    LN += [("tok", v + 1)] if v + 1 < UP else []
                    LN += [("norm", 2)] if v == 1 else [("norm", 3)] if v == 3 else []
                LN += [("tok", UP)]
            LN += [(k, c) for k in ("a1", "a2") for c in (2 * p, 2 * p + 1)]
            if p == 0:
                LN += [("tok", UP + v + 1) for v in range(UP - 1)]
        LN += [("f0", c) for c in range(NC)]
        LN += [("f1", c) for c in range(NC)] + [("d", c) for c in range(NC)]
        for c in range(NC - 2):
            LN += [("e1", c), ("e2", c)]
        LN += [(k, c) for k in ("e1", "e2") for c in (NC - 2, NC - 1)]
        LNI = {k: i for i, k in enumerate(LN)}

        def up_bank(w, f):
            return bank[(1, 2, 4, 5)[f] if w > UP else 1 + f % 2]

        def turn_bank(k, c):
            return bank[c % 2 if k == 0 or c >= 2 else 2 + c]

        def xin(k, c):
            return xa[:, c % 2, :] if k == 0 else UVf[:, 512 * c:512 * c + 512]

        def rstd_pool(pool, ch, key, n):
            i = LNI[key]
            k = i % 4
            pool.wait_ge(s["ln_var"], i + 1)
            ch(pool.tensor_scalar(rstd[:, k, 0:n], mv[:, k, 0:n, 1], EPS, None, ALU.add))
            ch.settle()
            pool.tensor_tensor(rstd[:, k, 0:n], rstd[:, k, 0:n], neghalf[:, 0:n], ALU.pow).then_inc(s["ln_rstd"], 1)

        def norm_stats(dve, ch, key, tiles):
            i = LNI[key]
            k = i % 4
            for j, x in enumerate(tiles):
                ch(dve.bn_stats(stats[:, k, j, :], x))
            ch.settle()
            for j in range(len(tiles)):
                last = dve.bn_aggr(mv[:, k, j, :], stats[:, k, j, :])
                if j < len(tiles) - 1:
                    ch(last)
            last.then_inc(s["ln_var"], 1)

        def norm_apply(dve, key, tiles, outs):
            i = LNI[key]
            k = i % 4
            dve.wait_ge(s["ln_var"], i + 1)
            dve.wait_ge(s["ln_rstd"], i + 1)
            for j, (x, o) in enumerate(zip(tiles, outs)):
                last = dve.tensor_scalar(o, x, mv[:, k, j, 0:1], rstd[:, k, j:j + 1], ALU.subtract, ALU.mult)
            return last

        @block.sync
        def _(sp):
            sp.dma_start(tok, a["tok"].partition_broadcast(P)).then_inc(s["load_tok"], 16)
            sp.dma_start(rows[:], a["rows"].partition_broadcast(P)).then_inc(s["load_rows"], 16)
            sp.dma_start(cols[:], a["cols"]).then_inc(s["load_rows"], 16)
            for t, n in ((emb, "emb"), (embT, "embT"), (wupd, "wupd"), (wf, "wf")):
                sp.dma_start(t[:], a[n]).then_inc(s["load_emb"], 16)
            for t, n in ((w1, "w1"), (w2, "w2"), (headw, "headw")):
                sp.dma_start(t[:], a[n]).then_inc(s["load_mlp"], 16)
            sp.dma_start(sloww[0:D], a["sloww"]).then_inc(s["load_attn"], 16)
            sp.dma_start(outw[:], a["outw"]).then_inc(s["load_attn"], 16)
            for k in range(2):
                sp.dma_start(wr[k][0:D], a[f"wr_{k}"]).then_inc(s["load_experts"], 16)
            sp.wait_ge(s["tok_down"], 2 * UP)
            for k in range(2):
                for t, n in ((ew1[k][0:D], "ew1"), (ew2[k][:], "ew2"), (eb2[k][:], "eb2")):
                    sp.dma_start(t, a[f"{n}_{k}"]).then_inc(s["load_experts"], 16)
            for t, n in ((wq, "wq"), (wk, "wk"), (wv, "wv"), (wproj, "wproj")):
                sp.dma_start(t[0:D], a[n]).then_inc(s["load_experts"], 16)
            for c in range(NC):
                sp.wait_ge(s["out_done"], c + 1)
                sp.dma_start(a["out"][:, CH * c:CH * c + CH, :], H[:, CH * c:CH * c + CH, :]).then_inc(s["stored"], 16)
            sp.wait_ge(s["stored"], 16 * NC)

        @block.gpsimd
        def _(pool):
            ch = Chain(pool, s["pool_chain"])
            ch(pool.memset(ident[:], 0.0))
            ch(pool.memset(ones[:], 1.0))
            ch(pool.memset(neghalf[:], -0.5))
            ch(pool.iota(iota_i[:], pattern=[[0, 1]], base=0, channel_multiplier=1))
            ch.settle()
            ch(pool.affine_select(out=ident[:], in_=ident[:], compare_op=ALU.not_equal, fill=1.0, base=0,
                                  pattern=[[-1, P]], channel_multiplier=1))
            ch.settle()
            pool.tensor_copy(iota_f[:], iota_i[:]).then_inc(s["consts"], 1)
            ch(pool.memset(m16[:], 1.0))
            ch(pool.memset(lower[:], 1.0))
            ch.settle()
            ch(pool.affine_select(out=m16[:], in_=m16[:], compare_op=ALU.is_ge, fill=0.0, base=0,
                                  pattern=[[-E, T]], channel_multiplier=1))
            ch.settle()
            pool.affine_select(out=m16[:], in_=m16[:], compare_op=ALU.is_ge, fill=0.0, base=E - 1,
                               pattern=[[E, T]], channel_multiplier=-1).then_inc(s["masks"], 1)
            pool.affine_select(out=lower[:], in_=lower[:], compare_op=ALU.is_ge, fill=0.0, base=-1,
                               pattern=[[1, E], [-1, E]], channel_multiplier=0).then_inc(s["masks"], 1)
            pool.wait_ge(s["masks"], 2)
            for w in (xa, *wr):
                ch(pool.memset(w[D:P], 0.0))
            pool.memset(sloww[D:P], 0.0).then_inc(s["pad"], 1)
            pool.wait_ge(s["pad"], 1)
            ch.settle()
            pool.wait_ge(s["load_rows"], 32)
            b2 = row("b2").rearrange("p (l d) -> p l d", l=NL)

            def affine(c):
                rstd_pool(pool, ch, ("norm", c), CH)
                xc = X[:, CH * c:CH * c + CH, :]
                pool.wait_ge(s["norm_scaled"], c + 1)
                g = row("norm_g").unsqueeze(1).broadcast_to([P, CH, DT])
                b = row("norm_b").unsqueeze(1).broadcast_to([P, CH, DT])
                ch(pool.tensor_tensor(xc, xtmp[:, CH * c:CH * c + CH, :], g, ALU.mult))
                ch.settle()
                pool.tensor_tensor(xc, xc, b, ALU.add).then_inc(s["norm_done"], 1)

            def prepare(w):
                i, c = unit(w)
                rstd_pool(pool, ch, ("tok", w), CH)
                if w % UP < 2:
                    pool.wait_ge(s["norm_done"], c + 1)
                else:
                    pool.wait_ge(s["tok_add"], w - 1)
                pool.tensor_tensor(xb_tok[:, c], X[:, CH * c:CH * c + CH, :],
                                   b2[:, i, :].unsqueeze(1).broadcast_to([P, CH, DT]), ALU.add).then_inc(s["xb_ready"], 1)

            def keys(t):
                k = t % 2
                hd = "p (h j) -> p h j"
                pool.wait_ge(s["a_elu"], t + 1)
                for dst, o in ((QF[:, t, :], 0), (KF[:, t, :], HB)):
                    ch(pool.tensor_tensor(dst.rearrange(hd, j=DH), e1[:, k, o:o + HB].rearrange(hd, j=DH),
                                          smallv[:, k, o // DH:o // DH + NH].unsqueeze(2).broadcast_to([P, NH, DH]), ALU.mult))
                pool.tensor_tensor(RK[:, t, :].rearrange(hd, j=DH), ker[:, k, :].rearrange(hd, j=DH),
                                   smallv[:, k, 16:24].unsqueeze(2).broadcast_to([P, NH, DH]),
                                   ALU.mult).then_inc(s["a_keys"], 1)

            def key_product(t, j, n):
                r0, r1_ = pieces(t)[j]
                keys_ = (KF, RK)[n]
                if t == TP:
                    pool.wait_ge(s["gram_read"], gram_reads(TP - 1, len(pieces(TP - 1)) - 1, 1))
                elif t > KS and n == 0:
                    pool.wait_ge(s["gram_mm"], t - KS)
                elif t >= 2 and j < len(pieces(t - 1)):
                    pool.wait_ge(s["gram_read"], gram_reads(t - 1, j, n))
                pool.tensor_tensor(key_products(n, t, j)[:, 0:r1_ - r0, :], keys_[:, r0:r1_, :],
                                   keys_[:, t, :].unsqueeze(1).broadcast_to([P, r1_ - r0, HB]),
                                   ALU.mult).then_inc(s["gram_p"], 1)

            def key_order(t):
                cut = [(j, n) for j in range(len(pieces(t))) for n in range(2)]
                return cut if t < KS else sorted(cut, key=lambda x: x[1])

            def query_products(t):
                if t >= 2:
                    pool.wait_ge(s["upd_p"], summed("fast", t - 2))
                if t:
                    pool.wait_ge(s["query_done"], t)
                if t > TP:
                    pool.wait_ge(s["query_half"], t - TP)
                for r0, r1_ in pieces(t + 1, 8):
                    R = r1_ - r0
                    ch(pool.tensor_tensor(PC[:, 0:R, :], KF[:, r0:r1_, :],
                                          QF[:, t, :].unsqueeze(1).broadcast_to([P, R, HB]), ALU.mult))
                    ch.settle()
                    pv = PC[:, 0:R, :].rearrange("p r (h j) -> p (r h) j", h=NH)
                    out = pv if t < TP else halves[:, NH * r0:NH * r1_, :]
                    last = pool.tensor_tensor(out[:, :, 0:16], pv[:, :, 0:16], pv[:, :, 16:32], ALU.add)
                    if t >= TP and r1_ == t + 1:
                        last.then_inc(s["query_half"], 1)
                        return
                    ch(last)
                    ch.settle()
                for m in (8, 4, 2):
                    ch(pool.tensor_tensor(pv[:, :, 0:m], pv[:, :, 0:m], pv[:, :, m:2 * m], ALU.add))
                    ch.settle()
                last = pool.tensor_tensor(CQ[:, t % 2, 0:t + 1, :].rearrange("p r h -> p (r h)"), pv[:, :, 0], pv[:, :, 1],
                                          ALU.add)
                last.then_inc(s["query_done"], 1)

            def products(t):
                for j, n in key_order(t):
                    key_product(t, j, n)
                query_products(t)

            affine(0)
            prepare(0)
            affine(1)
            for v in range(UP):
                if v + 1 < UP:
                    prepare(v + 1)
                if v in (1, 3):
                    affine(2 + v // 2)
            prepare(UP)
            for p in range(NP):
                for k in ("a1", "a2"):
                    for c in (2 * p, 2 * p + 1):
                        rstd_pool(pool, ch, (k, c), CH)
                for c in (2 * p, 2 * p + 1):
                    hc = H[:, CH * c:CH * c + CH, :]
                    pool.wait_ge(s["a_norm"], c + 1)
                    pool.tensor_tensor(hc, hc, XN[:, CH * c:CH * c + CH, :], ALU.add).then_inc(s["a_hx"], 1)
                early = key_order(TP) if p else []
                for t in range(TP * p, TP * p + TP):
                    keys(t)
                    if p and t - TP >= TP - len(early):
                        if t - TP == TP - len(early):
                            pool.wait_ge(s["tok_down"], 2 * UP)
                            pool.wait_ge(s["a_keys"], TP + 1)
                        key_product(TP, *early[t - TP - TP + len(early)])
                pool.wait_ge(s["a_keys"], TP * (p + 1))
                ch.settle()
                if p:
                    query_products(TP)
                else:
                    products(0)
                products(TP * p + 1)
                for t in range(TP * p, TP * p + TP):
                    if p == 0 and t + 1 < UP:
                        prepare(UP + t + 1)
                    if t + 2 < TP * p + TP:
                        products(t + 2)

            pool.wait_ge(s["query_half"], TP)
            pool.wait_ge(s["tok_down"], 2 * UP)
            ch(pool.memset(w2f[D:P, 1024:1280], 0.0))
            ch.settle()
            pool.memset(w1f[D:P, 0:2048], 0.0).then_inc(s["pad"], 1)
            pool.wait_ge(s["pad"], 2)

            pool.wait_ge(s["load_experts"], 16 * 12)
            pool.wait_ge(s["masks"], 2)
            for c in range(NC):
                rstd_pool(pool, ch, ("f0", c), CH)
            pool.wait_ge(s["x_norm"], 1)
            for k in range(2):
                pool.tensor_tensor(b2x[:, k], eb2[k][:].unsqueeze(1).broadcast_to([P, T, D]),
                                   m16[:].unsqueeze(2).broadcast_to([P, T, D]), ALU.mult).then_inc(s["b2x_ready"], 1)
            pool.wait_ge(s["b2x_ready"], 2)
            for x in (qd[0], qd[1], kz[0]):
                ch(pool.memset(x[D:P], 0.0))
            ch.settle()
            pool.memset(kz[1][D:P], 0.0).then_inc(s["pad"], 1)
            pool.wait_ge(s["pad"], 3)
            ch(pool.iota(rel_i, pattern=[[1, P]], base=0, channel_multiplier=-1))
            ch.settle()
            ch(pool.tensor_copy(rel, rel_i))
            ch.settle()
            pool.tensor_tensor(rel2, rel, rel, ALU.mult).then_inc(s["p_rel"], 1)
            pool.wait_ge(s["w_ready"], 1)
            for c in range(NC):
                for t in range(CH * c, CH * c + CH):
                    if t >= 2:
                        pool.wait_ge(s["x_down"], t - 1)
                    pool.tensor_tensor(w2w[:, t % 2], ew2[0][:], wts[:, t].unsqueeze(2).broadcast_to([P, E, D]),
                                       ALU.mult).then_inc(s["w2w_ready"], 1)
                rstd_pool(pool, ch, ("f1", c), CH)
                r = slice(CH * c, CH * c + CH)
                pool.wait_ge(s["f1_norm"], c + 1)
                yb = YB[1][:, r, :]
                ch(pool.tensor_tensor(yb, yb, row("gamma0").unsqueeze(1).broadcast_to([P, CH, D]), ALU.mult))
                ch.settle()
                ch(pool.tensor_tensor(yb, yb, row("beta0").unsqueeze(1).broadcast_to([P, CH, D]), ALU.add))
                ch.settle()
                pool.tensor_tensor(H[:, r, :], H[:, r, :], yb, ALU.add).then_inc(s["f_affine"], 1)
            for c in range(NC):
                rstd_pool(pool, ch, ("d", c), CH)
                r = slice(CH * c, CH * c + CH)
                pool.wait_ge(s["f_affine"], NC)
                pool.wait_ge(s["d_norm"], c + 1)
                pool.tensor_tensor(H[:, r, :], H[:, r, :], row("bproj").unsqueeze(1).broadcast_to([P, CH, D]),
                                   ALU.add).then_inc(s["hb_ready"], 1)
            for key in LN[-2 * NC:]:
                rstd_pool(pool, ch, key, CH)

        @block.scalar
        def _(act):
            ch = Chain(act, s["act_chain"])
            act.wait_ge(s["load_rows"], 32)
            act.activation(decay[:, 0:1], row("decay"), ACT.Exp, scale=-1.0).then_inc(s["decay_exp"], 1)

            def evict_T(w):
                i, c = unit(w)
                act.wait_ge(s["tok_T"], w + 1)
                if w >= 2:
                    act.wait_ge(s["tok_up"], 4 * (w - 1))
                if w == UP + 1:
                    act.wait_ge(s["head_mm"], 2)
                act.activation(xT[:, w % 2, :], bank[0][:], ACT.Identity, bias=col("ln_b", i),
                               scale=col("ln_g", i)).then_inc(s["tok_hT"], 1)

            def gelus(w):
                i, c = unit(w)
                for f in range(4):
                    act.wait_ge(s["tok_up"], 4 * w + f + 1)
                    if w >= 2 and f == 0:
                        act.wait_ge(s["tok_down"], w - 1)
                    act.activation(G[:, 4 * (w % 2) + f, :], up_bank(w, f)[:], ACT.Gelu,
                                   bias=col("b1", 4 * i + f)).then_inc(s["tok_gelu"], 1)

            def head(p):
                for c in (2 * p, 2 * p + 1):
                    act.wait_ge(s["head_T"], c + 1)
                    if c % 2:
                        act.wait_ge(s["head_mm"], c)
                    act.activation(xT[:, 1, :], bank[0][:], ACT.Copy).then_inc(s["head_xT"], 1)

            def qkv_bank(t, j):
                return bank[(4, 5, 6)[j] if t % 2 == 0 else (1, 2, 3)[j]]

            def tile_acts(t):
                k = t % 2
                act.wait_ge(s["a_qkv"], t + 1)
                if t >= 2:
                    act.wait_ge(s["a_keys"], t - 1)
                if t == TP:
                    act.wait_ge(s["upd_mm"], summed("rec", TP - 1))
                act.activation(e1[:, k, :], qkv_bank(t, 0)[:], ACT.Exp)
                act.activation(r1[:, k, :], qkv_bank(t, 0)[:], ACT.Relu)
                act.activation(UV[:, t].rearrange("p n h -> p (n h)"), qkv_bank(t, 1)[:], ACT.Copy).then_inc(s["a_acts"], 1)
                act.wait_ge(s["a_sub"], t + 1)
                act.activation(ker[:, k, :], kdd[:, k, :], ACT.Exp)
                bt = beta[:, t].rearrange("p n h -> p (n h)")
                act.activation(bt, bt, ACT.Exp, scale=-1.0).then_inc(s["a_rexp"], 1)

            def project(p):
                for c in (2 * p, 2 * p + 1):
                    act.wait_ge(s["a_T"], c + 1)
                    act.activation(xa[0:D, c % 2, :], bank[0][0:D, :], ACT.Identity, bias=col("aln_b", parts=D),
                                   scale=col("aln_g", parts=D)).then_inc(s["a_oT"], 1)
                for t in range(TP * p, TP * p + TP):
                    tile_acts(t)

            def state(t):
                act.wait_ge(s["upd_mm"], summed("rec", t))
                if t >= 2:
                    act.wait_ge(s["o_T"], t - 1)
                if t + 1 < T:
                    act.wait_ge(s["e_sub"], t + 1)
                act.activation(hs[:, t % 2, :], bank[7][:, 0:HB], ACT.Copy).then_inc(s["hs_saved"], 1)
                if t + 1 < T:
                    act.activation(er[:, (t + 1) % 2, :], dd[:, (t + 1) % 2, :], ACT.Exp).then_inc(s["h_exp"], 1)

            def state_T(t):
                act.wait_ge(s["o_T"], t + 1)
                if t >= 2:
                    act.wait_ge(s["o_mm"], t - 1)
                act.activation(hsT[:, t % 2, :], bank[0][:, 0:HB], ACT.Copy).then_inc(s["o_evict"], 1)

            evict_T(0)
            gelus(0)
            for v in range(UP - 1):
                evict_T(v + 1)
                gelus(v + 1)
            evict_T(UP)
            for p in range(NP):
                head(p)
                if p == 0:
                    gelus(UP)
                project(p)
                for t in range(TP * p, TP * p + TP):
                    if t % TP:
                        state(t - 1)
                    if p == 0 and t:
                        gelus(UP + t)
                    if t:
                        state_T(t - 1)
                    if p == 0 and t + 1 < UP:
                        evict_T(UP + t + 1)
                state(TP * p + TP - 1)
            state_T(T - 1)

            def experts(k, c):
                x = NC * k + c
                act.wait_ge(s["x_T"], x + 1)
                if k == 0 and c >= 2:
                    act.wait_ge(s["x_up"], E * (c - 1))
                dst, src = xin(k, c)[0:D], turn_bank(k, c)[0:D, :]
                if k == 0:
                    act.activation(dst, src, ACT.Copy).then_inc(s["x_xT"], 1)
                else:
                    act.activation(dst, src, ACT.Identity, bias=col("beta1", parts=D),
                                   scale=col("gamma1", parts=D)).then_inc(s["x_xT"], 1)

            def expert_gelus(k, c, e0=0, e1_=E):
                x = NC * k + c
                for e in range(e0, e1_):
                    act.wait_ge(s["x_up"], E * x + e + 1)
                    if e == 0 and x >= 2:
                        act.wait_ge(s["x_down"], CH * (x - 1))
                    act.activation(G2[x % 2][:, e, :], bank[2 + e % 2][:], ACT.Gelu,
                                   bias=col(f"eb1{k}", e)).then_inc(s["x_gelu"], 1)

            act.wait_ge(s["mean_mm"], 1)
            act.activation(meanT[:], bank[7][0:D, 0:T], ACT.Copy, scale=1.0 / P).then_inc(s["mean_ready"], 1)
            experts(0, 0)
            for j in range(3):
                act.wait_ge(s["r_sub"], j + 1)
                act.activation(rsel[0:T, j, :], rsel[0:T, j, :], ACT.Exp).then_inc(s["r_exp"], 1)
                expert_gelus(0, 0, 2 * j, 2 * j + 2)
            expert_gelus(0, 0, 6, E)
            act.wait_ge(s["wT_mm"], 1)
            act.activation(wtsT[:], bank[7][:, 256:384], ACT.Copy).then_inc(s["wT_ready"], 1)
            experts(0, 1)
            for c in range(NC):
                if c:
                    expert_gelus(0, c)
                    if c + 1 < NC:
                        experts(0, c + 1)
                if c == 1:
                    act.wait_ge(s["p_sub"], 1)
                    act.activation(plog, plog, ACT.Exp).then_inc(s["p_exp"], 1)
                    act.activation(gate[:, 0, :], row("gating"), ACT.Exp, scale=-1.0).then_inc(s["gate_exp"], 1)
                if c in (2, 3):
                    act.wait_ge(s["p_T"], c - 1)
                    act.activation(posT[:, 4 * c - 8:4 * c - 4, :].rearrange("p h n -> p (h n)"), bank[6][:],
                                   ACT.Copy).then_inc(s["p_evict"], 1)

            def take_x(c):
                act.wait_ge(s["d_T"], c + 1)
                if c:
                    act.wait_ge(s["d_v"], c)
                act.activation(xa[0:D, 0, :], bank[0][0:D, :], ACT.Copy).then_inc(s["d_xT"], 1)

            def queries(c, h0, h1):
                act.wait_ge(s["d_q"], c + 1)
                for h in range(h0, h1):
                    act.activation(qd[c % 2][0:D, h, :], bank[1][0:D, :], ACT.Copy,
                                   scale=m16[0:D, h:h + 1]).then_inc(s["d_qd"], 1)

            def take_keys(c):
                act.wait_ge(s["d_k"], c + 1)
                act.activation(kz[c % 2][0:D, :], bank[0][0:D, :], ACT.Copy).then_inc(s["d_kcopy"], 1)

            def take_values(c):
                act.wait_ge(s["d_v"], c + 1)
                act.activation(vaug[c % 2][:, :, :, 0:HD], bank[1][:, 0:CH * D].rearrange("p (t h d) -> p t h d", t=CH, h=NH),
                               ACT.Copy).then_inc(s["d_vcopy"], 1)

            def take_attended(c):
                act.wait_ge(s["at_T"], c + 1)
                act.activation(xa[0:D, 1, :], bank[0][0:D, :], ACT.Copy).then_inc(s["at_xT"], 1)

            def take_turned(t):
                for g in range(2):
                    act.wait_ge(s["s_T"], 2 * t + g + 1)
                    if t >= 2:
                        act.wait_ge(s["av_mm"], t - 1)
                    act.activation(pexp[:, t % 2, 4 * g:4 * g + 4, :].rearrange("p h n -> p (h n)"), bank[4 + g][:],
                                   ACT.Copy).then_inc(s["p_ready"], 1)

            take_x(0)
            queries(0, 0, NH)
            take_keys(0)
            take_values(0)
            for t in range(T):
                c, j = divmod(t, CH)
                if t:
                    take_turned(t - 1)
                act.wait_ge(s["s_sub"], 2 * t + 2)
                act.activation(sexp[:, t % 2], sexp[:, t % 2], ACT.Exp, scale=float(HD) ** -0.5).then_inc(s["s_exp"], 1)
                if j == 3 and c:
                    take_attended(c - 1)
                if c + 1 < NC:
                    if j == 0:
                        take_x(c + 1)
                    elif j == 1:
                        queries(c + 1, 0, 4)
                        take_keys(c + 1)
                    elif j == 2:
                        queries(c + 1, 4, NH)
                    else:
                        take_values(c + 1)
            take_turned(T - 1)
            experts(1, 0)
            experts(1, 1)
            take_attended(NC - 1)

            expert_gelus(1, 0)
            experts(1, 2)
            experts(1, 3)
            act.wait_ge(s["rl_read"], 1)
            act.activation(rsel[:], rsel[:], ACT.Exp).then_inc(s["rl_exp"], 1)
            expert_gelus(1, 1)
            act.wait_ge(s["wT_mm"], 2)
            act.activation(wtsT[:], bank[7][:, 256:384], ACT.Copy).then_inc(s["wT_ready"], 1)
            for c in range(2, NC):
                expert_gelus(1, c)

        @block.tensor
        def _(pe):
            mm = nc.tensor.matmul
            pe.wait_ge(s["load_emb"], 64)
            mm(bank[0][0:VOC, 0:DT], embT[:], wupd[:], start=True, stop=True).then_inc(s["utab_mm"], 1)
            pe.wait_ge(s["tables_ready"], 1)

            def embed(c):
                if c >= 2:
                    pe.wait_ge(s["norm_scaled"], c - 1)
                mm(bank[4 + c % 2][:], utab[:], onehot[:, 512 * c:512 * c + 512],
                   start=True, stop=True).then_inc(s["u_mm"], 1)
                pe.wait_ge(s["mem_ready"], c + 1)
                if c == 0:
                    pe.wait_ge(s["tables_ready"], 2)
                for j in range(CH):
                    t = CH * c + j
                    o = bank[6 + c % 2][:, DT * j:DT * j + DT]
                    mm(o, onehot[:, P * t:P * t + P], embf[:], start=True, stop=False)
                    last = mm(o, memT[:, P * t:P * t + P], wf[:], start=False, stop=True)
                last.then_inc(s["x_mm"], 1)

            def turn(w):
                pe.wait_ge(s["tok_norm"], w + 1)
                if w > UP + 1:
                    pe.wait_ge(s["o_evict"], w - UP - 1)
                if w:
                    pe.wait_ge(s["tok_hT"], w)
                for j in range(CH):
                    last = nc.tensor.transpose(bank[0][:, P * j:P * j + P], xn_tok[:, w % 2, j, :], ident[:])
                last.then_inc(s["tok_T"], 1)

            def up(w):
                i, c = unit(w)
                pe.wait_ge(s["tok_hT"], w + 1)
                for f in range(4):
                    if 4 * w + f >= 2:
                        pe.wait_ge(s["tok_gelu"], 4 * (w - 1) + f + 1 if w > UP else 4 * w + f - 1)
                    mm(up_bank(w, f)[:], w1[:, i, P * f:P * f + P], xT[:, w % 2, :],
                       start=True, stop=True).then_inc(s["tok_up"], 1)

            def down(w):
                i, c = unit(w)
                pe.wait_ge(s["tok_gelu"], 4 * w + 4)
                if w:
                    pe.wait_ge(s["tok_add"], w)
                for j in range(CH):
                    for f in range(4):
                        last = mm(bank[3][:, DT * j:DT * j + DT], G[:, 4 * (w % 2) + f, P * j:P * j + P],
                                  w2[:, i, f, :], start=(f == 0), stop=(f == 3))
                last.then_inc(s["tok_down"], 1)

            def head(p):
                pe.wait_ge(s["tok_add"], UP * (p + 1))
                pe.wait_ge(s["tok_hT"], UP + 1 if p == 0 else 2 * UP)
                if p:
                    pe.wait_ge(s["o_evict"], TP - 1)
                    pe.wait_ge(s["o_add"], TP - 1)
                for c in (2 * p, 2 * p + 1):
                    if c % 2:
                        pe.wait_ge(s["head_xT"], c)
                    for j in range(CH):
                        last = nc.tensor.transpose(bank[0][:, P * j:P * j + P], X[:, CH * c + j, :], ident[:])
                    last.then_inc(s["head_T"], 1)
                    pe.wait_ge(s["head_xT"], c + 1)
                    if c % 2:
                        pe.wait_ge(s["head_add"], c)
                    for j in range(CH):
                        last = mm(bank[3][:, VOC * j:VOC * j + VOC], xT[:, 1, P * j:P * j + P], headw[:],
                                  start=True, stop=True)
                    last.then_inc(s["head_mm"], 1)

            def project(p):
                if p == 0:
                    pe.wait_ge(s["load_attn"], 32)
                    pe.wait_ge(s["pad"], 1)
                pe.wait_ge(s["head_xT"], 2 * p + 2)
                pe.wait_ge(s["head_add"], 2 * p + 2)
                pe.wait_ge(s["tok_gelu"], 4 * (UP + 1) if p == 0 else 8 * UP)
                pe.wait_ge(s["x_mm"], NC)
                pe.wait_ge(s["norm_scaled"], NC)
                if p:
                    pe.wait_ge(s["acc_done"], TP)
                for c in (2 * p, 2 * p + 1):
                    pe.wait_ge(s["a_norm"], c + 1)
                    if c:
                        pe.wait_ge(s["a_oT"], c)
                    for j in range(CH):
                        last = nc.tensor.transpose(bank[0][0:D, P * j:P * j + P], X[:, CH * c + j, 0:D], ident[:])
                    last.then_inc(s["a_T"], 1)
                for t in range(TP * p, TP * p + TP):
                    if t % CH == 0:
                        pe.wait_ge(s["a_oT"], t // CH + 1)
                    if t % TP >= 2:
                        pe.wait_ge(s["a_acts"], t - 1)
                        pe.wait_ge(s["a_sub"], t - 1)
                    o = xa[:, t // CH % 2, P * (t % CH):P * (t % CH) + P]
                    mm(qkv_bank(t, 0)[:], o, sloww[:, 0:512], start=True, stop=True)
                    mm(qkv_bank(t, 1)[:], o, sloww[:, 512:1024], start=True, stop=True)
                    mm(qkv_bank(t, 2)[:, 0:HB + 16], o, sloww[:, 1024:], start=True, stop=True).then_inc(s["a_qkv"], 1)

            def qkv_bank(t, j):
                return bank[(4, 5, 6)[j] if t % 2 == 0 else (1, 2, 3)[j]]

            def key_sums(t):
                pe.wait_ge(s["gram_p"], 2 * gram_base(t) + len(pieces(t)))
                if t - KS >= 2:
                    pe.wait_ge(s["gram_taken"], t - KS - 1)
                x = KKf[:, 4096:4096 + HB * t].rearrange("p (g j) -> p g j", j=DH)
                for j in range(DH):
                    last = mm(bank[4 + t % 2][:, 0:NH * t], ident[:], x[:, :, j], start=(j == 0), stop=(j == DH - 1))
                last.then_inc(s["gram_mm"], 1)

            def held(t):
                for i, r0, r1_ in combos_of("held", t):
                    pe.wait_ge(s["upd_p"], i + 1)
                    if r0 == 0 and t > 1:
                        pe.wait_ge(s["acc_done"], t)
                    for r in range(r0, r1_):
                        last = mm(bank[6][:], ident[:], PB[:, i % 4, 512 * (r - r0):512 * (r - r0) + 512],
                                  start=(r == 0), stop=(r == t - 1))
                    last.then_inc(s["upd_mm"], 1)

            def read_out(kind, t):
                for i, r0, r1_ in combos_of(kind, t):
                    pe.wait_ge(s["upd_p"], i + 1)
                    if kind == "fast" and r0 == 0 and t > 0:
                        pe.wait_ge(s["hs_saved"], t)
                        pe.wait_ge(s["e_sub"], t)
                    for r in range(r0, r1_):
                        last = mm(bank[7][:, 0:HB], ident[:], PB[:, i % 4, HB * (r - r0):HB * (r - r0) + HB],
                                  start=(kind == "fast" and r == 0), stop=(kind == "rec" and r == t))
                    last.then_inc(s["upd_mm"], 1)

            def state_T(t):
                pe.wait_ge(s["hs_saved"], t + 1)
                pe.wait_ge(s["tok_hT"], min(UP + t + 2, 2 * UP))
                if t:
                    pe.wait_ge(s["o_evict"], t)
                for n in range(2):
                    last = nc.tensor.transpose(bank[0][:, P * n:P * n + P], hs[:, t % 2, P * n:P * n + P], ident[:])
                last.then_inc(s["o_T"], 1)

            def out_projection(t):
                pe.wait_ge(s["o_evict"], t + 1)
                pe.wait_ge(s["tok_add"], min(UP + t + 1, 2 * UP))
                if t:
                    pe.wait_ge(s["o_add"], t)
                for n in range(2):
                    last = mm(bank[3][:, 0:D], hsT[:, t % 2, P * n:P * n + P], outw[:, n, :], start=(n == 0), stop=(n == 1))
                last.then_inc(s["o_mm"], 1)

            pe.wait_ge(s["consts"], 1)
            embed(0)
            embed(1)
            pe.wait_ge(s["load_mlp"], 48)
            turn(0)
            up(0)
            for v in range(UP):
                if v + 1 < UP:
                    turn(v + 1)
                if v in (1, 3):
                    embed(2 + v // 2)
                down(v)
                if v + 1 < UP:
                    up(v + 1)
            turn(UP)
            for p in range(NP):
                head(p)
                if p == 0:
                    up(UP)
                project(p)
                pe.wait_ge(s["a_acts"], TP * (p + 1))
                pe.wait_ge(s["a_sub"], TP * (p + 1))
                if p:
                    held(TP)
                for t in range(TP * p, TP * p + TP):
                    w = UP + t
                    read_out("fast", t)
                    if (t + 1) % TP:
                        held(t + 1)
                    if t:
                        state_T(t - 1)
                    if p == 0 and w + 1 < 2 * UP:
                        turn(w + 1)
                    if t:
                        out_projection(t - 1)
                    read_out("rec", t)
                    if p == 0:
                        if t:
                            pe.wait_ge(s["o_add"], t)
                        down(w)
                        if w + 1 < 2 * UP:
                            up(w + 1)
                    if p and t + 2 < T:
                        key_sums(t + 2)
            def means(c):
                pe.wait_ge(s["x_norm"], c + 1)
                for t in range(CH * c, CH * c + CH):
                    last = mm(bank[7][0:D, t:t + 1], XN[:, t, :], ones[:, 0:1], start=True, stop=True)
                if c == NC - 1:
                    last.then_inc(s["mean_mm"], 1)

            state_T(T - 1)
            for c in range(NC - 1):
                means(c)
            out_projection(T - 1)
            means(NC - 1)

            tr = nc.tensor.transpose

            def turn_x(k, c):
                x = NC * k + c
                if x >= 2:
                    pe.wait_ge(s["x_xT"], x - 1)
                src = XN if k == 0 else YB[0]
                for j in range(CH):
                    last = tr(turn_bank(k, c)[0:D, P * j:P * j + P], src[:, CH * c + j, :], ident[:])
                last.then_inc(s["x_T"], 1)

            def expert_up(k, c, e0=0, e1_=E):
                x = NC * k + c
                pe.wait_ge(s["x_xT"], x + 1)
                for e in range(e0, e1_):
                    i = E * x + e
                    if i >= 2:
                        pe.wait_ge(s["x_gelu"], i - 1)
                    mm(bank[2 + e % 2][:], ew1[k][:, e, :], xin(k, c),
                       start=True, stop=True).then_inc(s["x_up"], 1)

            def expert_down(k, c):
                x = NC * k + c
                pe.wait_ge(s["x_gelu"], E * x + E)
                for j in range(CH):
                    t = CH * c + j
                    i = T * k + t
                    if i >= 2:
                        pe.wait_ge(s["y_read"], i - 1)
                    if k == 0:
                        pe.wait_ge(s["w2w_ready"], t + 1)
                    for e in range(E):
                        g = G2[x % 2][:, e, P * j:P * j + P]
                        if k == 0:
                            last = mm(bank[4 + t % 2][:, 0:D], g, w2w[:, t % 2, e, :], start=(e == 0), stop=(e == E - 1))
                        else:
                            last = mm(bank[4 + t % 2][:, D * e:D * e + D], g, ew2[1][:, e, :], start=True, stop=True)
                    last.then_inc(s["x_down"], 1)

            def bias(k):
                tr(bank[7][:, 256:384], wts[:].rearrange("p t e -> p (t e)"), ident[:]).then_inc(s["wT_mm"], 1)
                pe.wait_ge(s["wT_ready"], k + 1)
                for g in range(2):
                    mm(bank[4 + g][:], wtsT[:], b2x[:, k, 8 * g:8 * g + 8, :].rearrange("p t d -> p (t d)"),
                       start=True, stop=True).then_inc(s["bias_mm"], 1)

            pe.wait_ge(s["load_experts"], 16 * 12)
            pe.wait_ge(s["pad"], 2)
            turn_x(0, 0)
            pe.wait_ge(s["mean_ready"], 1)
            mm(bank[7][0:T, 64:64 + E], meanT[:], wr[0][0:D], start=True, stop=True).then_inc(s["logit_mm"], 1)
            expert_up(0, 0, 0, 2)
            pe.wait_ge(s["r_prob"], 1)
            mm(bank[7][0:T, 96:96 + E], ones[0:T, 0:T], rout[0:T, 0, :], start=True, stop=True).then_inc(s["load_mm"], 1)
            expert_up(0, 0, 2, 6)
            pe.wait_ge(s["r_spread"], 1)
            mm(bank[7][:, 128:256], ones[0:T, :], rsel[0:T].rearrange("p t e -> p (t e)"),
               start=True, stop=True).then_inc(s["spread_mm"], 1)
            expert_up(0, 0, 6, E)
            pe.wait_ge(s["w_ready"], 1)
            pe.wait_ge(s["b2x_ready"], 2)
            turn_x(0, 1)
            bias(0)
            for c in range(NC):
                if c + 1 < NC:
                    expert_up(0, c + 1)
                if c + 2 < NC:
                    turn_x(0, c + 2)
                if c == 0:
                    pe.wait_ge(s["base_ready"], 2)
                expert_down(0, c)
                if c in (1, 2):
                    pe.wait_ge(s["p_done"], 1)
                    if c == 2:
                        pe.wait_ge(s["p_evict"], 1)
                    for j in range(4):
                        last = tr(bank[6][:, P * j:P * j + P], plog[:, 4 * c - 4 + j, :], ident[:])
                    last.then_inc(s["p_T"], 1)

            def scores(t):
                n = slice(P * (t % CH), P * (t % CH) + P)
                q_, k_ = qd[t // CH % 2], kz[t // CH % 2]
                if t % CH == 0:
                    pe.wait_ge(s["d_qd"], NH * (t // CH + 1))
                    pe.wait_ge(s["d_kcopy"], t // CH + 1)
                for g in range(2):
                    if t:
                        pe.wait_ge(s["s_sub"], 2 * (t - 1) + g + 1)
                    for j in range(4):
                        last = mm(bank[2 + g][:, P * j:P * j + P], q_[:, 4 * g + j, n], k_[:, n], start=True, stop=True)
                    last.then_inc(s["s_mm"], 1)

            def turn_scores(t):
                pe.wait_ge(s["s_exp"], t + 1)
                for g in range(2):
                    if t:
                        pe.wait_ge(s["p_ready"], 2 * (t - 1) + g + 1)
                    for j in range(4):
                        last = tr(bank[4 + g][:, P * j:P * j + P], sexp[:, t % 2, 4 * g + j, :], ident[:])
                    last.then_inc(s["s_T"], 1)

            def values(t):
                pe.wait_ge(s["p_ready"], 2 * t + 2)
                j = t % CH
                if j == 0:
                    pe.wait_ge(s["d_vcopy"], t // CH + 1)
                    if t:
                        pe.wait_ge(s["comb_done"], t // CH)
                for h in range(NH):
                    o = 9 * (NH * j + h)
                    last = mm(bank[6][:, o:o + 9], pexp[:, t % 2, h, :], vaug[t // CH % 2][:, j, h, :], start=True, stop=True)
                last.then_inc(s["av_mm"], 1)

            def turn_input(c):
                pe.wait_ge(s["d_norm"], c + 1)
                if c:
                    pe.wait_ge(s["d_kcopy"], c)
                if c >= 3:
                    pe.wait_ge(s["d_add"], c - 2)
                for j in range(CH):
                    last = tr(bank[0][0:D, P * j:P * j + P], XN[:, CH * c + j, :], ident[:])
                last.then_inc(s["d_T"], 1)

            def project_qk(c):
                pe.wait_ge(s["d_xT"], c + 1)
                if c:
                    pe.wait_ge(s["d_vcopy"], c)
                if c >= 2:
                    pe.wait_ge(s["comb_done"], c - 1)
                mm(bank[1][0:D, :], wq[:], xa[:, 0, :], start=True, stop=True).then_inc(s["d_q"], 1)
                mm(bank[0][0:D, :], wk[:], xa[:, 0, :], start=True, stop=True).then_inc(s["d_k"], 1)

            def project_v(c):
                pe.wait_ge(s["d_qd"], NH * (c + 1))
                for j in range(CH):
                    last = mm(bank[1][:, D * j:D * j + D], xa[:, 0, P * j:P * j + P], wv[:], start=True, stop=True)
                last.then_inc(s["d_v"], 1)

            def positional(c):
                pe.wait_ge(s["d_vcopy"], min(c + 2, NC))
                if c == 0:
                    pe.wait_ge(s["p_evict"], 2)
                for h in range(NH):
                    last = mm(bank[1][:, 36 * h:36 * h + 36], posT[:, h, :], vaug[c % 2][:, :, h, :], start=True, stop=True)
                last.then_inc(s["pos_mm"], 1)

            def turn_attended(c):
                pe.wait_ge(s["comb_done"], c + 1)
                pe.wait_ge(s["d_kcopy"], min(c + 3, NC))
                if c:
                    pe.wait_ge(s["d_add"], c)
                for j in range(CH):
                    last = tr(bank[0][0:D, P * j:P * j + P], att[:, j, :], ident[:])
                last.then_inc(s["at_T"], 1)

            def project_out(c):
                pe.wait_ge(s["at_xT"], c + 1)
                for j in range(CH):
                    last = mm(bank[0][:, D * j:D * j + D], xa[:, 1, P * j:P * j + P], wproj[:], start=True, stop=True)
                last.then_inc(s["proj_mm"], 1)

            pe.wait_ge(s["y_read"], T)
            pe.wait_ge(s["pad"], 3)
            turn_input(0)
            project_qk(0)
            project_v(0)
            scores(0)
            for t in range(T):
                c, j = divmod(t, CH)
                if t + 1 < T:
                    scores(t + 1)
                if t:
                    values(t - 1)
                turn_scores(t)
                if j == 0 and c:
                    positional(c - 1)
                if j == 0 and c + 1 < NC:
                    turn_input(c + 1)
                if j == 1 and c + 1 < NC:
                    project_qk(c + 1)
                if j == 3 and c:
                    turn_attended(c - 1)
                if j == 3 and c + 1 < NC:
                    project_v(c + 1)
                if j == 3 and c:
                    project_out(c - 1)
            def router(c):
                pe.wait_ge(s["x_xT"], NC + c + 1)
                for j in range(CH):
                    t = CH * c + j
                    last = mm(bank[7][:, E * t:E * t + E], xin(1, c)[:, P * j:P * j + P], wr[1][:],
                              start=True, stop=True)
                last.then_inc(s["rl_mm"], 1)

            values(T - 1)
            positional(NC - 1)
            for c in range(2):
                pe.wait_ge(s["e_norm"], c + 1)
                turn_x(1, c)
            turn_attended(NC - 1)
            router(0)
            router(1)
            project_out(NC - 1)

            expert_up(1, 0)
            pe.wait_ge(s["d_add"], NC)
            for c in range(2, NC):
                pe.wait_ge(s["e_norm"], c + 1)
                turn_x(1, c)
            router(2)
            router(3)
            expert_up(1, 1)
            pe.wait_ge(s["w_ready"], 2)
            bias(1)
            pe.wait_ge(s["base_ready"], 4)
            for c in range(NC):
                if c and c + 1 < NC:
                    expert_up(1, c + 1)
                expert_down(1, c)

        @block.vector
        def _(dve):
            ch = Chain(dve, s["dve_chain"])
            dve.wait_ge(s["consts"], 1)
            dve.wait_ge(s["load_tok"], 16)
            ch(dve.tensor_scalar(onehot, tok[0:VOC, :], iota_f[0:VOC, 0:1], None, ALU.is_equal))
            dve.wait_ge(s["decay_exp"], 1)
            ch(dve.tensor_scalar(decay[:, 1:2], decay[:, 0:1], 1.0, None, ALU.add))
            ch.settle()
            ch(dve.reciprocal(decay[:, 2:3], decay[:, 1:2]))
            ch.settle()
            ch(dve.tensor_scalar(keep, tok, 0.0, decay[:, 2:3], ALU.not_equal, ALU.mult))
            ch(dve.tensor_scalar(iszero, tok, 0.0, None, ALU.is_equal))
            ch.settle()
            ch(dve.tensor_tensor(keep, keep, iszero, ALU.add))
            ch.settle()
            ch(dve.memset(keep.rearrange("p (t q) -> p t q", t=T)[:, :, 0], 0.0))
            dve.wait_ge(s["utab_mm"], 1)
            dve.wait_ge(s["load_rows"], 32)
            dve.wait_ge(s["load_emb"], 64)
            ch(dve.tensor_tensor(utab[:], bank[0][0:VOC, 0:DT], row("b_upd", parts=VOC), ALU.add))
            ch.settle()
            ch(dve.memset(utab[0:1, :], 0.0))
            ch.settle()
            dve.tensor_copy(decay[:, 3:4], decay[:, 2:3]).then_inc(s["tables_ready"], 1)
            dve.tensor_tensor(embf[:], emb[:], row("b_f", parts=VOC), ALU.add).then_inc(s["tables_ready"], 1)

            def memory(c):
                dve.wait_ge(s["u_mm"], c + 1)
                dve.tensor_tensor_scan(memT[:, 512 * c:512 * c + 512], keep[:, 512 * c:512 * c + 512],
                                       bank[4 + c % 2][:], 0.0, ALU.mult, ALU.add).then_inc(s["mem_ready"], 1)

            def first_norm(c):
                dve.wait_ge(s["x_mm"], c + 1)
                tiles = [bank[6 + c % 2][:, DT * j:DT * j + DT] for j in range(CH)]
                norm_stats(dve, ch, ("norm", c), tiles)
                norm_apply(dve, ("norm", c), tiles, [xtmp[:, CH * c + j, :] for j in range(CH)])\
                    .then_inc(s["norm_scaled"], 1)

            def unit_tiles(w):
                i, c = unit(w)
                return [X[:, CH * c + j, :] for j in range(CH)]

            def unit_stats(w):
                i, c = unit(w)
                if w % UP < 2:
                    dve.wait_ge(s["norm_done"], c + 1)
                else:
                    dve.wait_ge(s["tok_add"], w - 1)
                norm_stats(dve, ch, ("tok", w), unit_tiles(w))

            def unit_norm(w):
                if w >= 2:
                    dve.wait_ge(s["tok_T"], w - 1)
                norm_apply(dve, ("tok", w), unit_tiles(w), [xn_tok[:, w % 2, j, :] for j in range(CH)])\
                    .then_inc(s["tok_norm"], 1)

            def add(w):
                i, c = unit(w)
                dve.wait_ge(s["tok_down"], w + 1)
                dve.wait_ge(s["xb_ready"], w + 1)
                dve.tensor_tensor(X[:, CH * c:CH * c + CH, :], bank[3][:].rearrange("p (t d) -> p t d", t=CH),
                                  xb_tok[:, c], ALU.add).then_inc(s["tok_add"], 1)

            def head(p):
                for c in (2 * p, 2 * p + 1):
                    dve.wait_ge(s["head_mm"], c + 1)
                    dve.tensor_tensor(H[:, CH * c:CH * c + CH, :],
                                      bank[3][:, 0:CH * VOC].rearrange("p (t d) -> p t d", t=CH),
                                      row("head_b").unsqueeze(1).broadcast_to([P, CH, VOC]), ALU.add).then_inc(s["head_add"], 1)

            hd = "p (h j) -> p h j"

            def rk_max(t):
                k = t % 2
                b6 = bank[6 if t % 2 == 0 else 3]
                dve.wait_ge(s["a_qkv"], t + 1)
                if t >= 2:
                    dve.wait_ge(s["a_rexp"], t - 1)
                if t == TP:
                    dve.wait_ge(s["upd_mm"], summed("rec", TP - 1))
                rk = b6[:, 0:HB].rearrange(hd, h=NH)
                ch(dve.tensor_reduce(mx[:, k, :], rk, AX_X, ALU.max))
                ch(dve.tensor_copy(beta[:, t].rearrange("p n h -> p (n h)"), b6[:, HB:HB + 16]))
                ch.settle()
                dve.tensor_tensor(kdd[:, k, :].rearrange(hd, h=NH), rk,
                                  mx[:, k, :].unsqueeze(2).broadcast_to([P, NH, DH]), ALU.subtract).then_inc(s["a_sub"], 1)

            def tile_sums(t):
                k = t % 2
                bt = beta[:, t].rearrange("p n h -> p (n h)")
                dve.wait_ge(s["a_acts"], t + 1)
                ch(dve.scalar_tensor_tensor(out=e1[:, k, :], in0=e1[:, k, :], scalar=1.0, in1=r1[:, k, :],
                                            op0=ALU.min, op1=ALU.add))
                dve.wait_ge(s["a_rexp"], t + 1)
                ch(dve.tensor_scalar(bt, bt, 1.0, None, ALU.add))
                ch(dve.tensor_reduce(smallv[:, 2 + k, 16:24], ker[:, k, :].rearrange(hd, h=NH), AX_X, ALU.add))
                ch.settle()
                ch(dve.tensor_reduce(smallv[:, 2 + k, 0:16], e1[:, k, :].rearrange(hd, h=2 * NH), AX_X, ALU.add))
                ch(dve.reciprocal(bt, bt))
                if t >= 2:
                    dve.wait_ge(s["a_keys"], t - 1)
                ch.settle()
                dve.reciprocal(smallv[:, k, 0:24], smallv[:, 2 + k, 0:24]).then_inc(s["a_elu"], 1)

            def project(p):
                both = [(c, range(CH * c, CH * c + CH)) for c in (2 * p, 2 * p + 1)]
                dve.wait_ge(s["head_add"], 2 * p + 2)
                for c, r in both:
                    norm_stats(dve, ch, ("a1", c), [H[:, t, :] for t in r])
                for c, r in both:
                    ch(norm_apply(dve, ("a1", c), [H[:, t, :] for t in r], [XN[:, t, :] for t in r]))
                ch.settle()
                for c, r in both:
                    norm_stats(dve, ch, ("a2", c), [XN[:, t, :] for t in r])
                for c, r in both:
                    norm_apply(dve, ("a2", c), [XN[:, t, :] for t in r], [X[:, t, 0:D] for t in r]).then_inc(s["a_norm"], 1)
                for t in range(TP * p, TP * p + TP):
                    rk_max(t)
                    if t % TP:
                        tile_sums(t - 1)
                tile_sums(TP * p + TP - 1)

            def combine(kind, t, between=None):
                for i, r0, r1_ in combos_of(kind, t):
                    if i >= 4:
                        dve.wait_ge(s["upd_mm"], i - 3)
                    R = r1_ - r0
                    if kind == "held":
                        out = PB[:, i % 4, 0:R * 2 * HB].rearrange("p (g j) -> p g j", j=DH)
                        u = UV[:, r0:r1_].rearrange("p r n (h j) -> p (r n h) j", h=NH)
                        co = CG[:, t % 2, r0:r1_].rearrange("p r n h -> p (r n h)").unsqueeze(2).broadcast_to([P, R * 2 * NH, DH])
                    else:
                        out = PB[:, i % 4, 0:R * HB].rearrange("p (r h j) -> p r h j", r=R, h=NH)
                        u = UV[:, r0:r1_, 0 if kind == "fast" else 1].rearrange("p r (h j) -> p r h j", h=NH)
                        co = CQ[:, t % 2, r0:r1_] if kind == "fast" else CR[:, r0:r1_]
                        co = co.unsqueeze(3).broadcast_to([P, R, NH, DH])
                    dve.tensor_tensor(out, u, co, ALU.mult).then_inc(s["upd_p"], 1)
                    if between:
                        between(r0)

            def take_coefficients(t):
                for j, (r0, r1_) in enumerate(pieces(t)):
                    for n in range(2) if t < KS else (1,):
                        if t < KS:
                            dve.wait_ge(s["gram_p"], 2 * (gram_base(t) + j) + n + 1)
                        else:
                            dve.wait_ge(s["gram_p"], 2 * gram_base(t) + len(pieces(t)) + j + 1)
                        dve.tensor_reduce(CG[:, t % 2, r0:r1_, n, :],
                                          key_products(n, t, j)[:, 0:r1_ - r0, :].rearrange("p r (g j) -> p r g j", g=NH),
                                          AX_X, ALU.add).then_inc(s["gram_read"], 1)

            def take_key_sums(t):
                if t >= KS:
                    dve.wait_ge(s["gram_mm"], t - KS + 1)
                    dve.tensor_copy(CG[:, t % 2, 0:t, 0, :],
                                    bank[4 + t % 2][:, 0:NH * t].rearrange("p (r h) -> p r h", h=NH)).then_inc(s["gram_taken"], 1)
                    dve.wait_ge(s["gram_taken"], t - KS + 1)
                dve.wait_ge(s["gram_read"], gram_reads(t, len(pieces(t)) - 1, 1))

            def take_query_sums(t):
                if t >= 2:
                    dve.wait_ge(s["upd_p"], summed("fast", t - 2))
                dve.wait_ge(s["query_half"], t - TP + 1)
                dve.tensor_reduce(CQ[:, t % 2, 0:t + 1, :], halves[:, 0:NH * (t + 1), :].rearrange("p (r h) j -> p r h j", h=NH),
                                  AX_X, ALU.add).then_inc(s["query_done"], 1)

            def updates(t):
                uv = UV[:, t].rearrange("p n h -> p (n h)")
                if t:
                    dve.wait_ge(s["upd_mm"], summed("held", t))
                    ch(dve.tensor_tensor(uv, uv, bank[6][:], ALU.subtract))
                    ch.settle()
                ut = uv.rearrange("p (g j) -> p g j", j=DH)
                dve.tensor_tensor(ut, ut, beta[:, t].rearrange("p n h -> p (n h)").unsqueeze(2)
                                  .broadcast_to([P, 2 * NH, DH]), ALU.mult).then_inc(s["acc_done"], 1)
                dve.wait_ge(s["acc_done"], t + 1)

            def query_sub(t):
                h = bank[7][:, 0:HB].rearrange(hd, h=NH)
                dve.wait_ge(s["upd_mm"], summed("rec", t - 1))
                ch(dve.tensor_reduce(mx[:, t % 2, :], h, AX_X, ALU.max))
                ch.settle()
                dve.tensor_tensor(dd[:, t % 2, :].rearrange(hd, h=NH), h,
                                  mx[:, t % 2, :].unsqueeze(2).broadcast_to([P, NH, DH]), ALU.subtract).then_inc(s["e_sub"], 1)

            def query_sum(t):
                if t:
                    dve.wait_ge(s["h_exp"], t)
                ch(dve.tensor_reduce(smallv[:, 4, 0:NH], er[:, t % 2, :].rearrange(hd, h=NH), AX_X, ALU.add))
                ch.settle()
                ch(dve.reciprocal(smallv[:, 5, 0:NH], smallv[:, 4, 0:NH]))

            def x_apply(c):
                r = range(CH * c, CH * c + CH)
                norm_apply(dve, ("f0", c), [H[:, t, :] for t in r], [XN[:, t, :] for t in r]).then_inc(s["x_norm"], 1)

            def step(t, p):
                w = UP + t
                k = t % 2
                if t % TP:
                    query_sub(t)
                dve.wait_ge(s["query_done"], t + 1)
                combine("fast", t)
                if p == 0 and t:
                    add(w - 1)
                if p == 0 and t + 1 < UP:
                    unit_stats(w + 1)
                if t == TP * p:
                    take_coefficients(t + 1)
                query_sum(t)

                def query_piece(r0):
                    if r0 == 0 and p == 0 and t + 1 < UP:
                        unit_norm(w + 1)
                    if r0 % 4:
                        return
                    r1_ = min(r0 + 4, t + 1)
                    R = r1_ - r0
                    ch(dve.tensor_tensor(PD[:, 0:R, :], RK[:, r0:r1_, :],
                                         er[:, k, :].unsqueeze(1).broadcast_to([P, R, HB]), ALU.mult))
                    ch.settle()
                    ch(dve.tensor_reduce(CR[:, r0:r1_, :], PD[:, 0:R, :].rearrange("p r (g j) -> p r g j", g=NH),
                                         AX_X, ALU.add))
                    ch.settle()

                if (t + 1) % TP:
                    take_key_sums(t + 1)
                    combine("held", t + 1, query_piece)
                else:
                    for r0, _ in pieces(t + 1):
                        query_piece(r0)
                ch(dve.tensor_tensor(CR[:, 0:t + 1, :], CR[:, 0:t + 1, :],
                                     smallv[:, 5, 0:NH].unsqueeze(1).broadcast_to([P, t + 1, NH]), ALU.mult))
                ch.settle()
                combine("rec", t)
                if t == T - 1:
                    for c in range(NC - 1):
                        norm_stats(dve, ch, ("f0", c), [H[:, i, :] for i in range(CH * c, CH * c + CH)])
                    for c in range(NC - 1):
                        x_apply(c)
                if t:
                    out_add(t - 1)
                if (t + 1) % TP:
                    updates(t + 1)
                    if p:
                        take_query_sums(t + 1)
                if t + 2 < TP * p + TP:
                    take_coefficients(t + 2)

            def out_add(t):
                if t % CH == 0:
                    dve.wait_ge(s["a_hx"], t // CH + 1)
                dve.wait_ge(s["o_mm"], t + 1)
                dve.tensor_tensor(H[:, t, :], bank[3][:, 0:D], H[:, t, :], ALU.add).then_inc(s["o_add"], 1)

            memory(0)
            first_norm(0)
            memory(1)
            unit_stats(0)
            unit_norm(0)
            first_norm(1)
            for v in range(UP):
                if v + 1 < UP:
                    unit_stats(v + 1)
                    unit_norm(v + 1)
                if v in (1, 3):
                    memory(2 + v // 2)
                    first_norm(2 + v // 2)
                add(v)
            unit_stats(UP)
            unit_norm(UP)
            for p in range(NP):
                head(p)
                project(p)
                dve.wait_ge(s["a_keys"], TP * (p + 1))
                if p == 0:
                    ch(dve.memset(er[:, 0, :], 1.0))
                    ch.settle()
                take_coefficients(TP * p)
                if p:
                    take_key_sums(TP)
                    combine("held", TP)
                updates(TP * p)
                if p:
                    take_query_sums(TP)
                for t in range(TP * p, TP * p + TP):
                    step(t, p)
                if p == 0:
                    query_sub(TP)
                    add(2 * UP - 1)
            out_add(T - 1)

            sub, mul, plus = ALU.subtract, ALU.mult, ALU.add
            tt = dve.tensor_tensor
            for k in range(2):
                ch(dve.memset(vaug[k][:, :, :, HD:HD + 1], 1.0))
            dve.wait_ge(s["masks"], 2)
            dve.wait_ge(s["pad"], 1)
            dve.wait_ge(s["o_add"], T)
            norm_stats(dve, ch, ("f0", NC - 1), [H[:, t, :] for t in range(T - CH, T)])
            x_apply(NC - 1)

            def rank2(x, sel, n, parts):
                shape = [parts, n, E, E]
                own, other = x.unsqueeze(3).broadcast_to(shape), x.unsqueeze(2).broadcast_to(shape)
                a_, b_ = (c[0:parts, 0:n * E * E].rearrange("p (t e f) -> p t e f", t=n, e=E) for c in (cmp1, cmp2))
                ch(tt(a_, other, own, ALU.is_gt))
                ch(tt(b_, other, own, ALU.is_equal))
                ch.settle()
                ch(tt(b_, b_, lower[0:parts].unsqueeze(1).broadcast_to(shape), mul))
                ch.settle()
                ch(tt(a_, a_, b_, plus))
                ch.settle()
                ch(dve.tensor_reduce(sel, a_, AX_X, plus))
                ch.settle()
                ch(dve.tensor_scalar(sel, sel, 1.5, None, ALU.is_lt))
                ch.settle()

            def small_softmax(x, j, out):
                m, z = rsm[0:T, 0, j:j + 1], rsm[0:T, 1, j:j + 1]
                ch(dve.tensor_reduce(m, x, AX_X, ALU.max))
                ch.settle()
                dve.tensor_scalar(rsel[0:T, j, :], x, m, None, sub).then_inc(s["r_sub"], 1)
                dve.wait_ge(s["r_exp"], j + 1)
                if out is None:
                    return
                ch(dve.tensor_reduce(z, rsel[0:T, j, :], AX_X, plus))
                ch.settle()
                ch(dve.reciprocal(z, z))
                ch.settle()
                return dve.tensor_scalar(out, rsel[0:T, j, :], z, None, mul)

            CAPACITY = float(-(-N * 5 // (4 * E)))
            dve.wait_ge(s["logit_mm"], 1)
            ch(tt(rout[0:T, 3, :], bank[7][0:T, 64:64 + E], row("br0", parts=T), plus))
            ch.settle()
            small_softmax(rout[0:T, 3, :], 0, rout[0:T, 0, :]).then_inc(s["r_prob"], 1)
            dve.wait_ge(s["load_mm"], 1)
            sc = rout[0:T, 4, :]
            ch(dve.tensor_scalar(sc, bank[7][0:T, 96:96 + E], float(P), None, mul))
            ch.settle()
            ch(dve.reciprocal(sc, sc))
            ch.settle()
            ch(dve.tensor_scalar(sc, sc, CAPACITY, 1.0, mul, ALU.min))
            ch.settle()
            dve.wait_ge(s["r_prob"], 1)
            ch(tt(rout[0:T, 1, :], rout[0:T, 0, :], sc, mul))
            ch.settle()
            ch(small_softmax(rout[0:T, 1, :], 1, rout[0:T, 2, :]))
            ch.settle()
            small_softmax(rout[0:T, 2, :], 2, None)
            rank2(rout[0:T, 2:3, :], rout[0:T, 5:6, :], 1, T)
            w = rout[0:T, 5, :]
            ch(tt(w, w, rsel[0:T, 2, :], mul))
            ch.settle()
            ch(dve.tensor_reduce(rsm[0:T, 2, 0:1], w, AX_X, plus))
            ch.settle()
            ch(dve.reciprocal(rsm[0:T, 2, 1:2], rsm[0:T, 2, 0:1]))
            ch.settle()
            ch(dve.tensor_scalar(w, w, rsm[0:T, 2, 1:2], None, mul))
            ch.settle()
            tt(rsel[0:T], w.unsqueeze(1).broadcast_to([T, T, E]), ident[0:T, 0:T].unsqueeze(2).broadcast_to([T, T, E]),
               mul).then_inc(s["r_spread"], 1)
            dve.wait_ge(s["spread_mm"], 1)
            dve.tensor_copy(wts[:].rearrange("p t e -> p (t e)"), bank[7][:, 128:256]).then_inc(s["w_ready"], 1)

            for g in range(2):
                dve.wait_ge(s["bias_mm"], g + 1)
                r = slice(8 * g, 8 * g + 8)
                tt(YB[0][:, r, :], bank[4 + g][:].rearrange("p (t d) -> p t d", t=8), XN[:, r, :],
                   plus).then_inc(s["base_ready"], 1)
            dve.wait_ge(s["base_ready"], 2)

            def positional_softmax():
                dve.wait_ge(s["p_exp"], 1)
                ch(dve.tensor_reduce(comb[:, 0, 0:NH], plog, AX_X, plus))
                ch.settle()
                ch(dve.reciprocal(comb[:, 0, 8:8 + NH], comb[:, 0, 0:NH]))
                ch.settle()
                tt(plog, plog, comb[:, 0, 8:8 + NH].unsqueeze(2).broadcast_to([P, NH, P]), mul).then_inc(s["p_done"], 1)
                dve.wait_ge(s["gate_exp"], 1)
                ch(dve.tensor_scalar(gate[:, 0, :], gate[:, 0, :], 1.0, None, plus))
                ch.settle()
                ch(dve.reciprocal(gate[:, 1, :], gate[:, 0, :]))
                ch.settle()
                ch(dve.tensor_scalar(gate[:, 2, :], gate[:, 1, :], -1.0, 1.0, mul, plus))

            dve.wait_ge(s["p_rel"], 1)
            wp = row("wpos").rearrange("p (k h) -> p k h", k=3)
            ch(dve.scalar_tensor_tensor(out=gate[:, 3, :], in0=wp[:, 1, :], scalar=0.0, in1=row("bpos"), op0=mul, op1=plus))
            ch.settle()
            for h in range(NH):
                ch(dve.tensor_scalar(plog[:, h, :], rel, wp[:, 0, h:h + 1], gate[:, 3, h:h + 1], mul, plus))
            ch.settle()
            for h in range(NH):
                ch(dve.scalar_tensor_tensor(out=plog[:, h, :], in0=rel2, scalar=wp[:, 2, h:h + 1], in1=plog[:, h, :],
                                            op0=mul, op1=plus))
            ch.settle()
            ch(dve.tensor_reduce(comb[:, 0, 0:NH], plog, AX_X, ALU.max))
            ch.settle()
            tt(plog, plog, comb[:, 0, 0:NH].unsqueeze(2).broadcast_to([P, NH, P]), sub).then_inc(s["p_sub"], 1)
            for c in range(NC):
                r = range(CH * c, CH * c + CH)
                for t in r:
                    dve.wait_ge(s["x_down"], t + 1)
                    tt(YB[0][:, t, :], bank[4 + t % 2][:, 0:D], YB[0][:, t, :], plus).then_inc(s["y_read"], 1)
                dve.wait_ge(s["y_read"], CH * c + CH)
                norm_stats(dve, ch, ("f1", c), [YB[0][:, t, :] for t in r])
                norm_apply(dve, ("f1", c), [YB[0][:, t, :] for t in r], [YB[1][:, t, :] for t in r]).then_inc(s["f1_norm"], 1)
                if c == 0:
                    positional_softmax()

            chunk = [range(CH * c, CH * c + CH) for c in range(NC)]
            for c in range(NC):
                dve.wait_ge(s["f_affine"], c + 1)
                norm_stats(dve, ch, ("d", c), [H[:, t, :] for t in chunk[c]])
            for c in range(NC):
                norm_apply(dve, ("d", c), [H[:, t, :] for t in chunk[c]], [XN[:, t, :] for t in chunk[c]]).then_inc(s["d_norm"], 1)
            th = [P, CH, NH]
            g_ = gate[:, 1, :].unsqueeze(1).broadcast_to(th)
            omg = gate[:, 2, :].unsqueeze(1).broadcast_to(th)
            cb = [comb[:, k, :].rearrange("p (t h) -> p t h", t=CH) for k in range(6)]
            ch.settle()
            def normalise(t):
                for g in range(2):
                    x = bank[2 + g][:].rearrange("p (h m) -> p h m", h=4)
                    m = smax[:, t % 2, 4 * g:4 * g + 4]
                    dve.wait_ge(s["s_mm"], 2 * t + g + 1)
                    ch(dve.tensor_reduce(m, x, AX_X, ALU.max))
                    if t >= 2 and g == 0:
                        dve.wait_ge(s["s_T"], 2 * (t - 1))
                    ch.settle()
                    tt(sexp[:, t % 2, 4 * g:4 * g + 4, :], x, m.unsqueeze(2).broadcast_to([P, 4, P]), sub)\
                        .then_inc(s["s_sub"], 1)

            def mix(c):
                dve.wait_ge(s["av_mm"], CH * c + CH)
                dve.wait_ge(s["pos_mm"], c + 1)
                if c:
                    dve.wait_ge(s["at_T"], c)
                o = bank[6][:, 0:CH * NH * 9].rearrange("p (t h d) -> p t h d", t=CH, h=NH)
                po = bank[1][:, 0:CH * NH * 9].rearrange("p (h t d) -> p t h d", t=CH, h=NH)
                ch(dve.reciprocal(cb[0], o[:, :, :, HD]))
                ch(tt(cb[3], po[:, :, :, HD], g_, mul))
                ch.settle()
                ch(tt(cb[1], cb[0], omg, mul))
                ch.settle()
                ch(tt(cb[2], o[:, :, :, HD], cb[1], mul))
                ch.settle()
                ch(tt(cb[2], cb[2], cb[3], plus))
                ch.settle()
                ch(dve.reciprocal(cb[4], cb[2]))
                ch.settle()
                ch(tt(cb[1], cb[1], cb[4], mul))
                ch(tt(cb[5], cb[4], g_, mul))
                ch.settle()
                full = [P, CH, NH, HD]
                ch(tt(att.rearrange("p t (h d) -> p t h d", h=NH), o[:, :, :, 0:HD], cb[1].unsqueeze(3).broadcast_to(full), mul))
                ch(tt(att2.rearrange("p t (h d) -> p t h d", h=NH), po[:, :, :, 0:HD], cb[5].unsqueeze(3).broadcast_to(full), mul))
                ch.settle()
                tt(att, att, att2, plus).then_inc(s["comb_done"], 1)

            def add_attended(c):
                dve.wait_ge(s["proj_mm"], c + 1)
                dve.wait_ge(s["hb_ready"], c + 1)
                hc = H[:, CH * c:CH * c + CH, :]
                tt(hc, bank[0][:, 0:CH * D].rearrange("p (t d) -> p t d", t=CH), hc, plus).then_inc(s["d_add"], 1)

            def e_stats(k, c):
                if k == 1:
                    dve.wait_ge(s["d_add"], c + 1)
                src = H if k == 1 else XN
                norm_stats(dve, ch, (f"e{k}", c), [src[:, t, :] for t in chunk[c]])

            def e_apply(k, c):
                src, dst = (H, XN) if k == 1 else (XN, YB[0])
                last = norm_apply(dve, (f"e{k}", c), [src[:, t, :] for t in chunk[c]], [dst[:, t, :] for t in chunk[c]])
                if k == 1:
                    ch(last)
                    ch.settle()
                else:
                    last.then_inc(s["e_norm"], 1)

            for t in range(T):
                c, j = divmod(t, CH)
                normalise(t)
                if j == 0 and c >= 2:
                    add_attended(c - 2)
                    e_stats(1, c - 2)
                if j == 1 and c:
                    mix(c - 1)
                if j == 1 and c >= 2:
                    e_apply(1, c - 2)
                    e_stats(2, c - 2)
                if j == 2 and c >= 2:
                    e_apply(2, c - 2)
            add_attended(NC - 2)
            e_stats(1, NC - 2)
            mix(NC - 1)
            add_attended(NC - 1)
            e_stats(1, NC - 1)

            e_apply(1, NC - 2)
            e_apply(1, NC - 1)
            e_stats(2, NC - 2)
            e_stats(2, NC - 1)
            e_apply(2, NC - 2)
            e_apply(2, NC - 1)
            te = [P, T, E]
            dve.wait_ge(s["rl_mm"], NC)
            ch(tt(rout[:], bank[7][:, 0:T * E].rearrange("p (t e) -> p t e", t=T),
                  row("br1").unsqueeze(1).broadcast_to(te), plus))
            ch.settle()
            ch(dve.tensor_reduce(rsm[:, 0, :], rout[:], AX_X, ALU.max))
            ch.settle()
            tt(rsel[:], rout[:], rsm[:, 0, :].unsqueeze(2).broadcast_to(te), sub).then_inc(s["rl_read"], 1)
            rank2(rout[:], wts[:], T, P)
            dve.wait_ge(s["rl_exp"], 1)
            ch(tt(wts[:], wts[:], rsel[:], mul))
            ch.settle()
            ch(dve.tensor_reduce(rsm[:, 1, :], wts[:], AX_X, plus))
            ch.settle()
            ch(dve.reciprocal(rsm[:, 2, :], rsm[:, 1, :]))
            ch.settle()
            tt(wts[:], wts[:], rsm[:, 2, :].unsqueeze(2).broadcast_to(te), mul).then_inc(s["w_ready"], 1)
            dve.wait_ge(s["w_ready"], 2)
            for g in range(2):
                dve.wait_ge(s["bias_mm"], 2 + g + 1)
                r = slice(8 * g, 8 * g + 8)
                tt(H[:, r, :], bank[4 + g][:].rearrange("p (t d) -> p t d", t=8), H[:, r, :], plus).then_inc(s["base_ready"], 1)
            dve.wait_ge(s["base_ready"], 4)
            for c in range(NC):
                for t in range(CH * c, CH * c + CH):
                    dve.wait_ge(s["x_down"], T + t + 1)
                    tt(ytmp[:, t % 2], bank[4 + t % 2][:].rearrange("p (e d) -> p e d", e=E),
                       wts[:, t, :].unsqueeze(2).broadcast_to([P, E, D]), mul).then_inc(s["y_read"], 1)
                    dve.wait_ge(s["y_read"], T + t + 1)
                    ch(dve.tensor_reduce(YB[1][:, t, :], ytmp[:, t % 2].rearrange("p e d -> p d e"), AX_X, plus))
                ch.settle()
                hc = H[:, CH * c:CH * c + CH, :]
                tt(hc, hc, YB[1][:, CH * c:CH * c + CH, :], plus).then_inc(s["out_done"], 1)


def kernel(**inp):
    import numpy as np
    import concourse.bacc as bacc
    from concourse.bass_utils import run_bass_kernel_spmd as run

    i = {k: np.asarray(v) for k, v in inp.items()}
    flat = np.ravel
    rows = {
        "norm_g": i["L0_tok_norm_g"], "norm_b": i["L0_tok_norm_b"], "b2": i["L0_tok_cms_b2"],
        "b_upd": i["L0_tok_b_upd"], "b_f": i["L0_tok_b_f"], "head_b": i["L0_tok_head_b"],
        "decay": i["L0_tok_decay_param"], "br0": i["L0_ffn_br"],
        "gamma0": i["L0_ffn_gamma"], "beta0": i["L0_ffn_beta"], "bpos": i["L1_attn_bpos"],
        "wpos": i["L1_attn_Wpos"].T, "bproj": i["L1_attn_bproj"], "gating": i["L1_attn_gating"],
        "br1": i["L1_ffn_br"],
    }
    cols = {
        "ln_g": i["L0_tok_cms_ln_g"].T, "ln_b": i["L0_tok_cms_ln_b"].T,
        "b1": i["L0_tok_cms_b1"].reshape(NL * 4, P).T, "eb10": i["L0_ffn_b1"].T, "eb11": i["L1_ffn_b1"].T,
        "aln_g": i["L0_attn_ln_g"][:, None], "aln_b": i["L0_attn_ln_b"][:, None],
        "gamma1": i["L1_ffn_gamma"][:, None], "beta1": i["L1_ffn_beta"][:, None],
    }
    place, n = offsets(COLS)
    colv = np.zeros((P, n), np.float32)
    for k, v in cols.items():
        colv[0:v.shape[0], place[k][0]:place[k][1]] = v
    sw = i["L0_attn_slow_W"].reshape(NH, 5 * DH + 2, D)
    q, k_, v_, rk, rv = (sw[:, DH * j:DH * j + DH].reshape(HB, D) for j in range(5))
    slow = np.concatenate([q, k_, v_, rv, rk, sw[:, 5 * DH], sw[:, 5 * DH + 1]]).T
    arrays = {
        "tok": i["x"].reshape(-1),
        "rows": np.concatenate([flat(rows[k]) for k, _ in ROWS]),
        "cols": colv,
        "emb": i["L0_tok_emb"], "embT": i["L0_tok_emb"].T, "wupd": i["L0_tok_W_upd"], "wf": i["L0_tok_W_f"],
        "w1": i["L0_tok_cms_W1"].transpose(1, 0, 2),
        "w2": i["L0_tok_cms_W2"].reshape(NL, 4, P, DT).transpose(2, 0, 1, 3),
        "headw": i["L0_tok_head_W"],
        "sloww": slow, "outw": i["L0_attn_out_W"].T.reshape(2, P, D).transpose(1, 0, 2),
        "ew1_0": i["L0_ffn_W1"].transpose(1, 0, 2), "ew2_0": i["L0_ffn_W2"].transpose(1, 0, 2), "wr_0": i["L0_ffn_Wr"],
        "ew1_1": i["L1_ffn_W1"].transpose(1, 0, 2), "ew2_1": i["L1_ffn_W2"].transpose(1, 0, 2), "wr_1": i["L1_ffn_Wr"],
        "wq": i["L1_attn_Wqk"][0:D].T, "wk": i["L1_attn_Wqk"][D:].T,
        "eb2_0": np.tile(i["L0_ffn_b2"], (T, 1)), "eb2_1": np.tile(i["L1_ffn_b2"], (T, 1)),
        "wv": i["L1_attn_Wv"].T, "wproj": i["L1_attn_Wproj"].T,
    }
    nc = bacc.Bacc("TRN2", target_bir_lowering=False, num_devices=1)
    feed, aps = {}, {}
    for k, v in arrays.items():
        v = np.ascontiguousarray(v)
        feed[f"in_{k}"] = v
        aps[k] = nc.dram_tensor(f"in_{k}", v.shape, mybir.dt.from_np(v.dtype), kind="ExternalInput").ap()
    out = nc.dram_tensor("out_h", (T, P, D), F32, kind="ExternalOutput").ap()
    aps["out"] = out.rearrange("t p d -> p t d")
    build(nc, aps)
    r = run(nc, [feed], core_ids=[0])
    return r.results[0]["out_h"]
```
